# Optimizing a Trainium2 kernel written in Bass

```python
import numpy as np
import jax
import jax.numpy as jnp

def _softmax(x, axis=-1):
    return jax.nn.softmax(x, axis=axis)

def _gelu(x):
    return jax.nn.gelu(x, approximate=True)

def _silu(x):
    return jax.nn.silu(x)

def _sigmoid(x):
    return jax.nn.sigmoid(x)

def _layernorm(x, axis=-1, eps=1e-05):
    m = jnp.mean(x, axis=axis, keepdims=True)
    v = jnp.var(x, axis=axis, keepdims=True)
    return (x - m) / jnp.sqrt(v + eps)

def _scatter_add(tgt, idx, src, axis=0):
    return tgt.at[idx].add(src)

def _segment_sum(src, seg, n):
    return jax.ops.segment_sum(src, seg, n)
kernel_name = 'mk_xattn_ffn_d2_seqx_r8_d4d31c'

def setup_inputs(seed: int=0):
    np.random.seed(seed)
    _w = jnp.asarray

    def _rec_inputs():
        import jax
        import jax.numpy as jnp
        _rk = jax.random.key(seed)
        x = 7.22e-05 + 1 * jax.random.normal(jax.random.fold_in(_rk, 1), (16, 128, 128), jnp.float32)
        _lenS = 128 - jax.random.randint(jax.random.fold_in(_rk, 7), (16,), 0, max(1, 128 // 4) + 1, jnp.int32)
        _lenS2 = 128 - jax.random.randint(jax.random.fold_in(_rk, 8), (16,), 0, max(1, 128 // 4) + 1, jnp.int32)
        _ctx_1024P = jax.random.normal(jax.random.fold_in(_rk, 11), (16, 16, 128), jnp.float32)
        _ctx_1024c = jax.random.dirichlet(jax.random.fold_in(_rk, 511), 0.3 * jnp.ones((16,), jnp.float32), (16, 128))
        _ctx_1024t = jnp.einsum('bsk,bkd->bsd', _ctx_1024c, _ctx_1024P)
        _ctx_1024t = _ctx_1024t * jax.lax.rsqrt(jnp.mean(jnp.square(_ctx_1024t)) + 1e-12) * 0.953939
        ctx_1024 = 4.13588e-05 + 0.999923 * (_ctx_1024t + 0.3 * jax.random.normal(jax.random.fold_in(_rk, 611), (16, 128, 128), jnp.float32))
        return (x, ctx_1024)
    x, ctx_1024 = _rec_inputs()

    def _L0_xattn_setup():
        import jax, jax.numpy as jnp
        import numpy as np
        D_MODEL = 128
        HEADS = 16
        D_HEAD = D_MODEL // HEADS
        SEQ = 256
        C = 2
        K_TOP = int(C * np.log(SEQ))
        key = jax.random.key(seed)
        ks = jax.random.split(key, 5)
        s = 0.02
        return {'Q': jax.random.normal(ks[0], (4, SEQ, D_MODEL), jnp.float32), 'K': jax.random.normal(ks[1], (4, SEQ, D_MODEL), jnp.float32), 'V': jax.random.normal(ks[2], (4, SEQ, D_MODEL), jnp.float32), 'Wq': jax.random.normal(ks[3], (D_MODEL, D_HEAD), jnp.float32) * s, 'bq': jnp.zeros((D_HEAD,), jnp.float32), 'Wout': jax.random.normal(ks[4], (HEADS * D_HEAD, D_MODEL), jnp.float32) * s, 'bout': jnp.zeros((D_MODEL,), jnp.float32)}
    _L0_xattn_all = _L0_xattn_setup()
    _L0_xattn_in = {k: v for k, v in _L0_xattn_all.items() if k in ('Wq', 'bq', 'Wout', 'bout')}
    del _L0_xattn_all

    def _L0_ffn_setup():
        import jax, jax.numpy as jnp
        import numpy as np
        TOP_K = 32
        TEMPERATURE = 1.0
        PARAM_SCALE = 0.02

        def _compose_weight(logits, A, B):
            vals, idx = jax.lax.top_k(logits, TOP_K)
            w = jax.nn.softmax(vals / TEMPERATURE)
            A_sel = A[idx]
            B_sel = B[idx]
            return jnp.einsum('k,kir,kro->io', w, A_sel, B_sel)
        key = jax.random.key(seed)
        ks = jax.random.split(key, 7)
        B, S, D, F, P, R = (2, 128, 128, 512, 32, 64)
        x = jax.random.normal(ks[0], (B, S, D), dtype=jnp.float32)
        fc1_A = jax.random.normal(ks[1], (P, D, R), dtype=jnp.float32) * PARAM_SCALE
        fc1_B = jax.random.normal(ks[2], (P, R, F), dtype=jnp.float32) * PARAM_SCALE
        fc2_A = jax.random.normal(ks[3], (P, F, R), dtype=jnp.float32) * PARAM_SCALE
        fc2_B = jax.random.normal(ks[4], (P, R, D), dtype=jnp.float32) * PARAM_SCALE
        fc1_logits = jax.random.normal(ks[5], (P,), dtype=jnp.float32)
        fc2_logits = jax.random.normal(ks[6], (P,), dtype=jnp.float32)
        return {'x': x, 'fc1_A': fc1_A, 'fc1_B': fc1_B, 'fc2_A': fc2_A, 'fc2_B': fc2_B, 'fc1_logits': fc1_logits, 'fc2_logits': fc2_logits}
    _L0_ffn_all = _L0_ffn_setup()
    _L0_ffn_in = {k: v for k, v in _L0_ffn_all.items() if k in ('fc1_A', 'fc1_B', 'fc2_A', 'fc2_B', 'fc1_logits', 'fc2_logits')}
    del _L0_ffn_all

    def _L1_xattn_setup():
        import jax, jax.numpy as jnp
        import numpy as np
        D = 128
        key = jax.random.key(seed)
        ks = jax.random.split(key, 11)
        B, Sq, Skv = (4, 256, 256)
        s = 0.02
        return {'query': jax.random.normal(ks[0], (B, Sq, D), jnp.float32), 'key': jax.random.normal(ks[1], (B, Skv, D), jnp.float32), 'value': jax.random.normal(ks[2], (B, Skv, D), jnp.float32), 'Wq': jax.random.normal(ks[3], (D, D), jnp.float32) * s, 'bq': jnp.zeros((D,), jnp.float32), 'Wk': jax.random.normal(ks[4], (D, D), jnp.float32) * s, 'bk': jnp.zeros((D,), jnp.float32), 'Wv': jax.random.normal(ks[5], (D, D), jnp.float32) * s, 'bv': jnp.zeros((D,), jnp.float32), 'Wo': jax.random.normal(ks[6], (D, D), jnp.float32) * s, 'bo': jnp.zeros((D,), jnp.float32)}
    _L1_xattn_all = _L1_xattn_setup()
    _L1_xattn_in = {k: v for k, v in _L1_xattn_all.items() if k in ('Wq', 'bq', 'Wk', 'bk', 'Wv', 'bv', 'Wo', 'bo')}
    del _L1_xattn_all

    def _L1_ffn_setup():
        import jax, jax.numpy as jnp
        import numpy as np
        D = 128
        E = 8
        K = 2
        NUM_ITER = 2
        DT = 0.1
        H = 64
        CTX = 2 * D

        def _gelu(t):
            return jax.nn.gelu(t, approximate=False)

        def _inl(ctrl, x, v, mu):
            alpha_raw, beta_raw, gate_raw = jnp.split(ctrl, 3, axis=-1)
            alpha = jax.nn.sigmoid(alpha_raw)
            beta = jax.nn.softplus(beta_raw)
            gate = jax.nn.sigmoid(gate_raw)
            error = x - mu
            v_next = alpha * v - beta * error
            x_next = x + DT * gate * v_next
            return (x_next, v_next)
        key = jax.random.key(seed)
        ks = jax.random.split(key, 20)
        s = 0.02
        inp = {'x': jax.random.normal(ks[0], (4, 512, D), jnp.float32), 'w_r1': jax.random.normal(ks[1], (D, D // 4), jnp.float32) * s, 'b_r1': jnp.zeros((D // 4,), jnp.float32), 'w_r2': jax.random.normal(ks[2], (D // 4, E), jnp.float32) * s, 'b_r2': jnp.zeros((E,), jnp.float32), 'w_h1': jax.random.normal(ks[3], (D, D // 4), jnp.float32) * s, 'b_h1': jnp.zeros((D // 4,), jnp.float32), 'w_h2': jax.random.normal(ks[4], (D // 4, 1), jnp.float32) * s, 'b_h2': jnp.zeros((1,), jnp.float32), 'expert_w1': jax.random.normal(ks[5], (E, CTX, H), jnp.float32) * s, 'expert_b1': jnp.zeros((E, H), jnp.float32), 'expert_w2': jax.random.normal(ks[6], (E, H, 3 * D), jnp.float32) * s, 'expert_b2': jnp.zeros((E, 3 * D), jnp.float32), 'w_s1': jax.random.normal(ks[7], (CTX, H), jnp.float32) * s, 'b_s1': jnp.zeros((H,), jnp.float32), 'w_s2': jax.random.normal(ks[8], (H, 3 * D), jnp.float32) * s, 'b_s2': jnp.zeros((3 * D,), jnp.float32), 'shared_weight': jnp.asarray(0.5, jnp.float32), 'w_f1': jax.random.normal(ks[9], (D, 2 * D), jnp.float32) * s, 'b_f1': jnp.zeros((2 * D,), jnp.float32), 'w_f2': jax.random.normal(ks[10], (2 * D, D), jnp.float32) * s, 'b_f2': jnp.zeros((D,), jnp.float32), 'integration_weight': jnp.full((D,), 0.5, jnp.float32), 'mu': jnp.zeros((D,), jnp.float32)}
        return inp
    _L1_ffn_all = _L1_ffn_setup()
    _L1_ffn_in = {k: v for k, v in _L1_ffn_all.items() if k in ('w_r1', 'b_r1', 'w_r2', 'b_r2', 'w_h1', 'b_h1', 'w_h2', 'b_h2', 'expert_w1', 'expert_b1', 'expert_w2', 'expert_b2', 'w_s1', 'b_s1', 'w_s2', 'b_s2', 'shared_weight', 'w_f1', 'b_f1', 'w_f2', 'b_f2', 'integration_weight', 'mu')}
    del _L1_ffn_all
    return {'x': x, 'ctx_1024': ctx_1024, 'L0_xattn_Wq': _L0_xattn_in['Wq'], 'L0_xattn_bq': _L0_xattn_in['bq'], 'L0_xattn_Wout': _L0_xattn_in['Wout'], 'L0_xattn_bout': _L0_xattn_in['bout'], 'L0_ffn_fc1_A': _L0_ffn_in['fc1_A'], 'L0_ffn_fc1_B': _L0_ffn_in['fc1_B'], 'L0_ffn_fc2_A': _L0_ffn_in['fc2_A'], 'L0_ffn_fc2_B': _L0_ffn_in['fc2_B'], 'L0_ffn_fc1_logits': _L0_ffn_in['fc1_logits'], 'L0_ffn_fc2_logits': _L0_ffn_in['fc2_logits'], 'L1_xattn_Wq': _L1_xattn_in['Wq'], 'L1_xattn_bq': _L1_xattn_in['bq'], 'L1_xattn_Wk': _L1_xattn_in['Wk'], 'L1_xattn_bk': _L1_xattn_in['bk'], 'L1_xattn_Wv': _L1_xattn_in['Wv'], 'L1_xattn_bv': _L1_xattn_in['bv'], 'L1_xattn_Wo': _L1_xattn_in['Wo'], 'L1_xattn_bo': _L1_xattn_in['bo'], 'L1_ffn_w_r1': _L1_ffn_in['w_r1'], 'L1_ffn_b_r1': _L1_ffn_in['b_r1'], 'L1_ffn_w_r2': _L1_ffn_in['w_r2'], 'L1_ffn_b_r2': _L1_ffn_in['b_r2'], 'L1_ffn_w_h1': _L1_ffn_in['w_h1'], 'L1_ffn_b_h1': _L1_ffn_in['b_h1'], 'L1_ffn_w_h2': _L1_ffn_in['w_h2'], 'L1_ffn_b_h2': _L1_ffn_in['b_h2'], 'L1_ffn_expert_w1': _L1_ffn_in['expert_w1'], 'L1_ffn_expert_b1': _L1_ffn_in['expert_b1'], 'L1_ffn_expert_w2': _L1_ffn_in['expert_w2'], 'L1_ffn_expert_b2': _L1_ffn_in['expert_b2'], 'L1_ffn_w_s1': _L1_ffn_in['w_s1'], 'L1_ffn_b_s1': _L1_ffn_in['b_s1'], 'L1_ffn_w_s2': _L1_ffn_in['w_s2'], 'L1_ffn_b_s2': _L1_ffn_in['b_s2'], 'L1_ffn_shared_weight': _L1_ffn_in['shared_weight'], 'L1_ffn_w_f1': _L1_ffn_in['w_f1'], 'L1_ffn_b_f1': _L1_ffn_in['b_f1'], 'L1_ffn_w_f2': _L1_ffn_in['w_f2'], 'L1_ffn_b_f2': _L1_ffn_in['b_f2'], 'L1_ffn_integration_weight': _L1_ffn_in['integration_weight'], 'L1_ffn_mu': _L1_ffn_in['mu']}

def reference(x, ctx_1024, L0_xattn_Wq, L0_xattn_bq, L0_xattn_Wout, L0_xattn_bout, L0_ffn_fc1_A, L0_ffn_fc1_B, L0_ffn_fc2_A, L0_ffn_fc2_B, L0_ffn_fc1_logits, L0_ffn_fc2_logits, L1_xattn_Wq, L1_xattn_bq, L1_xattn_Wk, L1_xattn_bk, L1_xattn_Wv, L1_xattn_bv, L1_xattn_Wo, L1_xattn_bo, L1_ffn_w_r1, L1_ffn_b_r1, L1_ffn_w_r2, L1_ffn_b_r2, L1_ffn_w_h1, L1_ffn_b_h1, L1_ffn_w_h2, L1_ffn_b_h2, L1_ffn_expert_w1, L1_ffn_expert_b1, L1_ffn_expert_w2, L1_ffn_expert_b2, L1_ffn_w_s1, L1_ffn_b_s1, L1_ffn_w_s2, L1_ffn_b_s2, L1_ffn_shared_weight, L1_ffn_w_f1, L1_ffn_b_f1, L1_ffn_w_f2, L1_ffn_b_f2, L1_ffn_integration_weight, L1_ffn_mu):
    import jax
    import jax.numpy as jnp

    def _L0_xattn_ref(Q, K, V, Wq, bq, Wout, bout):
        import jax, jax.numpy as jnp
        import numpy as np
        D_MODEL = 128
        HEADS = 16
        D_HEAD = D_MODEL // HEADS
        SEQ = 256
        C = 2
        K_TOP = int(C * np.log(SEQ))
        B, L, _ = Q.shape
        q = (Q @ Wq + bq).transpose(0, 2, 1)
        k_ = (K @ Wq + bq).transpose(0, 2, 1)
        v = (V @ Wq + bq).transpose(0, 2, 1)
        Qf = jnp.fft.fft(q.astype(jnp.complex64))
        Kf = jnp.fft.fft(k_.astype(jnp.complex64))
        corr = jnp.real(jnp.fft.ifft(Qf * jnp.conj(Kf)))
        corr = corr.mean(axis=(0, 1))
        W_topk, I_topk = jax.lax.top_k(corr, K_TOP)
        W_topk = jax.nn.softmax(W_topk)

        def body(R, ws):
            w, shift = ws
            return (R + w * jnp.roll(v, -shift, axis=-1), None)
        R3, _ = jax.lax.scan(body, jnp.zeros_like(v), (W_topk, I_topk))
        R = jnp.broadcast_to(R3[:, None], (B, HEADS, D_HEAD, L)).reshape(B, L, HEADS * D_HEAD)
        return R @ Wout + bout

    def _L0_ffn_ref(x, fc1_A, fc1_B, fc2_A, fc2_B, fc1_logits, fc2_logits):
        import jax, jax.numpy as jnp
        import numpy as np
        TOP_K = 32
        TEMPERATURE = 1.0
        PARAM_SCALE = 0.02

        def _compose_weight(logits, A, B):
            vals, idx = jax.lax.top_k(logits, TOP_K)
            w = jax.nn.softmax(vals / TEMPERATURE)
            A_sel = A[idx]
            B_sel = B[idx]
            return jnp.einsum('k,kir,kro->io', w, A_sel, B_sel)
        W1 = _compose_weight(fc1_logits, fc1_A, fc1_B)
        W2 = _compose_weight(fc2_logits, fc2_A, fc2_B)
        h = jax.nn.gelu(jnp.einsum('bsd,df->bsf', x, W1))
        return jnp.einsum('bsf,fd->bsd', h, W2)

    def _L1_xattn_ref(query, key, value, Wq, bq, Wk, bk, Wv, bv, Wo, bo):
        import jax, jax.numpy as jnp
        import numpy as np
        D = 128
        Q = jnp.einsum('bsd,de->bse', query, Wq) + bq
        K = jnp.einsum('bsd,de->bse', key, Wk) + bk
        V = jnp.einsum('bsd,de->bse', value, Wv) + bv
        scale = 1.0 / jnp.sqrt(jnp.asarray(D, Q.dtype))
        scores = jnp.einsum('bqd,bkd->bqk', Q, K) * scale
        attn = jax.nn.softmax(scores, axis=-1)
        out = jnp.einsum('bqk,bkd->bqd', attn, V)
        return jnp.einsum('bsd,de->bse', out, Wo) + bo

    def _L1_ffn_ref(x, w_r1, b_r1, w_r2, b_r2, w_h1, b_h1, w_h2, b_h2, expert_w1, expert_b1, expert_w2, expert_b2, w_s1, b_s1, w_s2, b_s2, shared_weight, w_f1, b_f1, w_f2, b_f2, integration_weight, mu):
        import jax, jax.numpy as jnp
        import numpy as np
        D = 128
        E = 8
        K = 2
        NUM_ITER = 2
        DT = 0.1
        H = 64
        CTX = 2 * D

        def _gelu(t):
            return jax.nn.gelu(t, approximate=False)

        def _inl(ctrl, x, v, mu):
            alpha_raw, beta_raw, gate_raw = jnp.split(ctrl, 3, axis=-1)
            alpha = jax.nn.sigmoid(alpha_raw)
            beta = jax.nn.softplus(beta_raw)
            gate = jax.nn.sigmoid(gate_raw)
            error = x - mu
            v_next = alpha * v - beta * error
            x_next = x + DT * gate * v_next
            return (x_next, v_next)
        B, N, Dm = x.shape
        xf = x.reshape(B * N, Dm)
        logits = _gelu(xf @ w_r1 + b_r1) @ w_r2 + b_r2
        probs = jax.nn.softmax(logits, axis=-1)
        top_p, top_i = jax.lax.top_k(probs, K)
        top_p = top_p / jnp.sum(top_p, axis=-1, keepdims=True)
        flat_idx = top_i.reshape(-1)
        flat_w = top_p.reshape(-1, 1)
        v = jnp.zeros_like(xf)
        integrated = xf
        for _ in range(NUM_ITER):
            ctx = jnp.concatenate([integrated, v], axis=-1)
            shared_ctrl = _gelu(ctx @ w_s1 + b_s1) @ w_s2 + b_s2
            x_shared, v_shared = _inl(shared_ctrl, integrated, v, mu)
            sw = jax.nn.sigmoid(shared_weight)
            ctx_e = jnp.repeat(ctx, K, axis=0)
            x_e = jnp.repeat(integrated, K, axis=0)
            v_e = jnp.repeat(v, K, axis=0)
            w1 = expert_w1[flat_idx]
            b1 = expert_b1[flat_idx]
            w2 = expert_w2[flat_idx]
            b2 = expert_b2[flat_idx]
            hidden = _gelu(jnp.einsum('tc,tch->th', ctx_e, w1) + b1)
            ctrl = jnp.einsum('th,tho->to', hidden, w2) + b2
            x_r, v_r = _inl(ctrl, x_e, v_e, mu)
            x_r = (x_r * flat_w).reshape(B * N, K, Dm).sum(axis=1)
            v_r = (v_r * flat_w).reshape(B * N, K, Dm).sum(axis=1)
            x_next = sw * x_shared + (1.0 - sw) * x_r
            v_next = sw * v_shared + (1.0 - sw) * v_r
            halt = jax.nn.sigmoid(_gelu(x_next @ w_h1 + b_h1) @ w_h2 + b_h2)
            refined = _gelu(x_next @ w_f1 + b_f1) @ w_f2 + b_f2
            integrated = integrated + halt * refined * integration_weight
            v = v_next
        return integrated.reshape(B, N, Dm)
    x = x + _L0_xattn_ref(_layernorm(x, axis=-1), ctx_1024, ctx_1024, L0_xattn_Wq, L0_xattn_bq, L0_xattn_Wout, L0_xattn_bout)
    x = x + _L0_ffn_ref(_layernorm(x, axis=-1), L0_ffn_fc1_A, L0_ffn_fc1_B, L0_ffn_fc2_A, L0_ffn_fc2_B, L0_ffn_fc1_logits, L0_ffn_fc2_logits)
    x = x + _L1_xattn_ref(_layernorm(x, axis=-1), ctx_1024, ctx_1024, L1_xattn_Wq, L1_xattn_bq, L1_xattn_Wk, L1_xattn_bk, L1_xattn_Wv, L1_xattn_bv, L1_xattn_Wo, L1_xattn_bo)
    x = x + _L1_ffn_ref(_layernorm(x, axis=-1), L1_ffn_w_r1, L1_ffn_b_r1, L1_ffn_w_r2, L1_ffn_b_r2, L1_ffn_w_h1, L1_ffn_b_h1, L1_ffn_w_h2, L1_ffn_b_h2, L1_ffn_expert_w1, L1_ffn_expert_b1, L1_ffn_expert_w2, L1_ffn_expert_b2, L1_ffn_w_s1, L1_ffn_b_s1, L1_ffn_w_s2, L1_ffn_b_s2, L1_ffn_shared_weight, L1_ffn_w_f1, L1_ffn_b_f1, L1_ffn_w_f2, L1_ffn_b_f2, L1_ffn_integration_weight, L1_ffn_mu)
    return x

_drawn_inputs = setup_inputs


def setup_inputs(seed=0):
    import zlib

    import numpy as np

    out = dict(_drawn_inputs(seed))
    spreads = {'L0_xattn_bq': (0.0, 0.1),
     'L0_xattn_bout': (0.0, 0.1),
     'L1_xattn_bq': (0.0, 2.0),
     'L1_xattn_bk': (0.0, 2.0),
     'L1_xattn_bv': (0.0, 2.0),
     'L1_xattn_bo': (0.0, 0.557),
     'L1_ffn_b_r1': (0.0, 2.0),
     'L1_ffn_b_r2': (0.0, 2.0),
     'L1_ffn_b_h1': (0.0, 0.8),
     'L1_ffn_expert_b1': (0.0, 2.0),
     'L1_ffn_expert_b2': (0.0, 2.0),
     'L1_ffn_b_s1': (0.0, 2.0),
     'L1_ffn_b_s2': (0.0, 2.0),
     'L1_ffn_b_f1': (0.0, 0.8),
     'L1_ffn_b_f2': (0.0, 0.308),
     'L1_ffn_integration_weight': (0.5, 0.6),
     'L1_ffn_mu': (0.0, 2.0)}
    factors = {'L0_ffn_fc1_A': 8.0,
     'L0_ffn_fc1_B': 8.0,
     'L0_ffn_fc2_A': 8.0,
     'L0_ffn_fc2_B': 8.0,
     'L0_ffn_fc1_logits': 8.0,
     'L0_ffn_fc2_logits': 8.0,
     'L1_xattn_Wq': 64.0,
     'L1_xattn_Wk': 64.0,
     'L1_ffn_w_r1': 64.0,
     'L1_ffn_w_r2': 49.155,
     'L1_ffn_w_h1': 8.0,
     'L1_ffn_w_h2': 8.0,
     'L1_ffn_expert_w1': 56.262,
     'L1_ffn_expert_w2': 47.873,
     'L1_ffn_w_s1': 25.618,
     'L1_ffn_w_s2': 8.0,
     'L1_ffn_w_f1': 6.152,
     'L1_ffn_w_f2': 5.485,
     'L1_xattn_Wv': 8.0,
     'L1_xattn_Wo': 4.181}
    for name, (base, spread) in spreads.items():
        noise = np.random.default_rng([zlib.crc32(name.encode()), seed]).standard_normal(out[name].shape)
        drawn = base * np.exp(spread * noise) if base else spread * noise
        out[name] = jnp.asarray(drawn.astype(out[name].dtype))
    for name, factor in factors.items():
        out[name] = (out[name] * factor).astype(out[name].dtype)
    return out
```

```python
import numpy as np
import concourse.bass as bass
from concourse import mybir
from contextlib import ExitStack

B, S, D = 16, 128, 128
T = B * S
CH = 512
NCH = T // CH
BPC = CH // S
DH, HEADS = 8, 16
NF = S // 2 + 1
TOPK = int(2 * np.log(256))
PRIM, RANK, FF = 32, 64, 512
KC = PRIM * RANK // 128
FT = FF // 128
E, H, HT = 8, 64, 4
ITER = 2
EPS = 1e-5
NEG = -3.0e38

PACK_A = [("wq8", 128, DH), ("bq8", 128, DH), ("log1", 128, PRIM), ("log2", 128, PRIM),
          ("wout", 128, D), ("cl", 128, NF), ("sl", 128, NF), ("cf", NF, S), ("sf", NF, S),
          ("a1", NF, 1), ("a2", NF, 1), ("bout", 128, 1), ("ident", 128, 128),
          ("bk", 128, 1), ("wk", 128, D), ("wv", 128, D)]
PACK_B = [("wq", 128, D), ("wo", 128, D), ("bq", 128, 1), ("bv", 128, 1), ("bo", 128, 1),
          ("wr1", 128, 32), ("br1", 32, 1), ("wr2", 33, E), ("wh1", 128, 32), ("bh1", 32, 1),
          ("wh2", 32, 1), ("bh2", 128, 1), ("ew1", 128, 2 * E * H), ("eb1", 128, HT),
          ("ew2", 128, HT * 3 * D), ("eb2", 96, 3 * D), ("ws1", 128, 2 * H), ("bs1", H, 1),
          ("ws2", H, 3 * D), ("bs2", 96, 3 * D), ("wf1", 128, 2 * D), ("bf1", 128, 2),
          ("wf2", 128, 2 * D), ("bf2", 128, 1), ("iw", 128, 1), ("mu", 128, 1),
          ("sw", 128, 1), ("sel", E, HT * 128), ("iota", 128, E)]


def columns(layout):
    at, out = 0, {}
    for name, rows, cols in layout:
        out[name] = (rows, at, cols)
        at += cols
    return out, at


def build(nc, d_xtok, d_xT, d_ctxT, d_packA, d_packB, d_a1, d_b1, d_a2, d_b2, d_out):
    F, BF, U32 = mybir.dt.float32, mybir.dt.bfloat16, mybir.dt.uint32
    ALU, ACT, AX = mybir.AluOpType, mybir.ActivationFunctionType, mybir.AxisListType
    colA, nA = columns(PACK_A)
    colB, nB = columns(PACK_B)
    SCALE = 1.0 / float(np.sqrt(np.float32(D)))

    ctx = ExitStack()
    with ctx:
        def sb(name, shape, dt=F):
            return ctx.enter_context(nc.sbuf_tensor(name, shape, dt))

        sems = {}

        def sem(name):
            if name not in sems:
                sems[name] = ctx.enter_context(nc.semaphore(name))
            return sems[name]

        xtok_f = sb("xtok", [128, B * D])
        xtok = xtok_f[:, :].rearrange("p (b d) -> p b d", b=B)
        xT = sb("xT", [128, T])
        ctxT = sb("ctxT", [128, T])
        pA = sb("pA", [128, nA])
        pB = sb("pB", [128, nB])
        a1_f = sb("a1", [128, KC * D])
        b1_f = sb("b1", [128, KC * FF])
        a2_f = sb("a2", [128, KC * FF])
        b2_f = sb("b2", [128, KC * D])
        a1 = a1_f[:, :].rearrange("p (k d) -> p k d", k=KC)
        b1 = b1_f[:, :].rearrange("p (k d) -> p k d", k=KC)
        a2 = a2_f[:, :].rearrange("p (k d) -> p k d", k=KC)
        b2 = b2_f[:, :].rearrange("p (k d) -> p k d", k=KC)

        def A(name, a=0, b=None):
            r, at, n = colA[name]
            return pA[0:r, at + a:at + (n if b is None else b)]

        def W(name, a=0, b=None):
            r, at, n = colB[name]
            return pB[0:r, at + a:at + (n if b is None else b)]

        bank = [ctx.enter_context(nc.psum_tensor(f"bank{i}", [128, 512], F)) for i in range(8)]

        hB_f = sb("hB", [128, 2 * FT * CH])
        blk = hB_f[:, :].rearrange("p (n m) -> p n m", m=128)
        qt = hB_f[:, 0:384].rearrange("p (a b c) -> p a b c", a=3, b=B)
        qk = blk[:, 3:5, :]
        cw = blk[0:NF, 5:7, :]
        fr = blk[0:NF, 7:11, :].rearrange("p (a b) n -> p a b n", a=2)
        junk = blk[0:NF, 11:17, :]
        cor = blk[0:NF, 17:20, :]
        ecor = blk[0:NF, 20:22, :]
        ab_f = blk[0:NF, 22:26, :]
        st = sb("st", [128, B, 6])
        mv = sb("mv", [128, B, 2])
        veps = sb("veps", [128, B])
        rstd = sb("rstd", [128, B])
        mhalf = sb("mhalf", [128, B])
        red = sb("red", [NF, 12])
        ones = sb("ones", [128, 128])
        reB = sb("reB", [NF, 2, NF])
        m8 = sb("m8", [NF, 3, 8])
        yb = sb("yb", [128, 128])
        lg_n = sb("lg_n", [128, 6])
        lg_e = sb("lg_e", [128, 2, PRIM])
        wcol = sb("wcol", [128, 2, KC])
        kT = sb("kT", [128, T])
        vtok_f = sb("vtok", [128, B * D])
        vtok = vtok_f[:, :].rearrange("p (b d) -> p b d", b=B)
        w1 = sb("w1", [128, FF])
        w2 = sb("w2", [128, FT, D])
        lst = sb("lst", [128, 2, BPC, 6])
        lmv = sb("lmv", [128, 2, BPC, 2])
        lve = sb("lve", [128, 2, BPC])
        lrs = sb("lrs", [128, 2, BPC])
        zz = sb("zz", [128, 4 * CH])
        ztok = zz[:, 0:2 * CH].rearrange("p (a b d) -> p a b d", a=2, b=BPC)
        zT = zz[:, 2 * CH:4 * CH].rearrange("p (a n) -> p a n", a=2)
        hB = hB_f[:, :].rearrange("p (a f n) -> p a f n", a=2, f=FT)
        att = a2_f[:, 0:10 * CH].rearrange("p (w a n) -> p w a n", w=5, a=2)
        qT, oT = att[:, 0], att[:, 1]
        bqs = sb("bqs", [128, 1])
        nmax = sb("nmax", [128, 2, BPC])
        nms = sb("nms", [128, 2, BPC])
        prob = att[:, 2].rearrange("p a (b k) -> p a b k", b=BPC)
        psum_ = sb("psum_", [128, 2, BPC])
        prec = sb("prec", [128, 2, BPC])
        pn = att[:, 3].rearrange("p a (b k) -> p a b k", b=BPC)
        pT = att[:, 4].rearrange("p a (b k) -> p a b k", b=BPC)
        xi = sb("xi", [128, T])
        r1 = sb("r1", [33, 2, CH])
        lg = sb("lg", [128, B, E])
        top = sb("top", [128, B, 8])
        tix = sb("tix", [128, B, 8], U32)
        tif = sb("tif", [128, B, 8])
        rt = sb("rt", [128, 5, B])
        swc = sb("swc", [128, 4])
        cf2 = sb("cf2", [128, 2, B])
        mrep = xtok_f[:, 0:B * 96].bitcast(BF).rearrange("p (a b m) -> p a b m", a=2, b=B)
        identb = sb("identb", [128, 128], BF)
        selb = sb("selb", [E, HT * 128], BF)
        m72 = sb("m72", [96, 2, T], BF)
        mexp = b1_f[:, :].bitcast(BF).rearrange("p (a f n) -> p a f n", a=2, f=HT)
        cb = hB_f[:, :].rearrange("p (a n) -> p a n", a=2)
        onesb = sb("onesb", [96, CH], BF)
        bparts = sb("bparts", [96, 2, 3 * D], BF)
        bhi = a1_f[0:96, 0:9 * D].bitcast(BF).rearrange("p (q i n) -> p q i n", q=3, i=2)
        brem = b2_f[0:96, 0:12 * D].rearrange("p (q i n) -> p q i n", q=2, i=2)
        iwh = sb("iwh", [128, 1])
        bh2h = sb("bh2h", [128, 1])
        vT = a1_f
        hid = a2_f[:, 0:HT * CH].rearrange("p (f n) -> p f n", f=HT)
        hs = kT[0:H, 3 * CH:4 * CH]
        hm = a2_f[:, HT * CH:3 * HT * CH].rearrange("p (a f n) -> p a f n", a=2, f=HT)
        ew = a2_f[:, 3 * HT * CH:4 * HT * CH].rearrange("p (f n) -> p f n", f=4)
        pw = xtok_f[:, 0:3 * CH].rearrange("p (f n) -> p f n", f=3)
        ab = vtok_f[:, 0:3 * CH].rearrange("p (f n) -> p f n", f=3)
        ta = ctxT[:, 0:0 + 3 * CH].rearrange("p (f n) -> p f n", f=3)
        tg = kT[:, 0:0 + 3 * CH].rearrange("p (f n) -> p f n", f=3)
        sm = b2_f[:, 0:3 * CH].rearrange("p (f n) -> p f n", f=3)
        xn = xtok_f[:, 3 * CH:4 * CH]
        fh = zz[:, 0:2 * CH].rearrange("p (f n) -> p f n", f=2)
        th = zz[:, 2 * CH:3 * CH]
        h1 = zz[0:32, 3 * CH:4 * CH]
        rr = ctxT[:, 3 * CH:4 * CH]
        res = xT

        def ck(c):
            return slice(c * CH, (c + 1) * CH)

        ident = A("ident")
        block = ctx.enter_context(nc.Block())

        STEPS = ITER * NCH

        @block.sync
        def _(sp):
            for dst, src, name in ((pA[:, :], d_packA, "in_A"), (xtok[:, :, :], d_xtok, "in_xtok"),
                                   (xT[:, :], d_xT, "in_x"), (ctxT[:, :], d_ctxT, "in_ctx"),
                                   (a1[:, :, :], d_a1, "in_a1"), (b1[:, :, :], d_b1, "in_b1"),
                                   (b2[:, :, :], d_b2, "in_b2"), (a2[:, :, :], d_a2, "in_a2"),
                                   (pB[:, :], d_packB, "in_B")):
                sp.dma_start(dst, src).then_inc(sem(name), 16)
            for c in range(NCH):
                sp.wait_ge(sem("res"), c + 1)
                sp.dma_start(d_out[:, ck(c)], res[:, ck(c)]).then_inc(sem("out"), 16)
            sp.wait_ge(sem("out"), 16 * NCH)

        @block.gpsimd
        def _(pool):
            pool.memset(mhalf[:, :], -0.5).then_inc(sem("mhalf"), 1)
            pool.memset(ones[:, :], 1.0).then_inc(sem("ones"), 1)
            pool.memset(onesb[:, :], 1.0).then_inc(sem("onesb"), 1)
            pool.wait_ge(sem("onesb"), 1)
            pool.memset(r1[32:33, :, :], 1.0).then_inc(sem("r1one"), 1)
            pool.wait_ge(sem("r1one"), 1)
            pool.wait_ge(sem("mhalf"), 1)
            pool.wait_ge(sem("veps"), 1)
            pool.tensor_tensor(rstd[:, :], veps[:, :], mhalf[:, :], ALU.pow).then_inc(sem("rstd"), 1)
            pool.memset(mrep[:, :, :, :], 0.0).then_inc(sem("mrep0"), 1)
            pool.wait_ge(sem("mrep0"), 1)
            for n in range(3 * NCH):
                pool.wait_ge(sem("lve"), n + 1)
                pool.tensor_tensor(lrs[:, n % 2, :], lve[:, n % 2, :], mhalf[:, 0:BPC], ALU.pow)\
                    .then_inc(sem("lrs"), 1)
            for s in range(STEPS):
                c = s % NCH
                pool.wait_ge(sem("e0"), s + 1)
                if s >= 1:
                    pool.wait_ge(sem("w"), 3 * s)
                for k in range(2):
                    pool.tensor_tensor(ew[:, 2 + k, :], ew[:, 0, :], cb[:, k, ck(c)], ALU.mult)\
                        .then_inc(sem("ew"), 1)
                if s >= NCH:
                    pool.wait_ge(sem("v1"), c + 1)
                    if s > NCH:
                        pool.wait_ge(sem("u"), 3 * (s - NCH))
                    for k in range(2):
                        pool.tensor_tensor(pw[:, 1 + k, :], vT[:, ck(c)], cb[:, k, ck(c)], ALU.mult)\
                            .then_inc(sem("pw"), 1)

        @block.scalar
        def _(act):
            act.wait_ge(sem("lgn"), 2)
            for i, n in enumerate(("log1", "log2")):
                act.activation(lg_e[:, i, :], A(n), ACT.Exp, bias=lg_n[:, i:i + 1],
                               accum_out=lg_n[:, 2 + i:3 + i]).then_inc(sem("lge"), 1)
            act.wait_ge(sem("cw_ps"), 1)
            act.activation(cw[:, :, :], bank[1][0:NF, 0:2 * D].rearrange("p (a d) -> p a d", a=2),
                           ACT.Copy).then_inc(sem("cw"), 1)
            for c in range(NCH):
                act.wait_ge(sem("k_ps"), c + 1)
                act.activation(kT[:, ck(c)], bank[2 + c % 2][:, :], ACT.Identity, bias=A("bk"))\
                    .then_inc(sem("k"), 1)
            for c in range(NCH):
                act.wait_ge(sem("v_ps"), c + 1)
                act.activation(vtok[:, c * BPC:(c + 1) * BPC, :],
                               bank[2 + c % 2][:, :].rearrange("p (a d) -> p a d", a=BPC), ACT.Copy)\
                    .then_inc(sem("v"), 1)
            act.wait_ge(sem("negmax"), 1)
            act.activation(ecor[:, 0, :], cor[:, 0, :], ACT.Exp, bias=red[:, 6:7]).then_inc(sem("ecor"), 1)
            act.wait_ge(sem("w1_ps"), 1)
            act.activation(w1[:, :], bank[6][:, :], ACT.Copy).then_inc(sem("w1"), 1)
            act.wait_ge(sem("y_ps"), 1)
            act.activation(yb[:, :], bank[4][:, 0:128], ACT.Identity, bias=A("bout")).then_inc(sem("yb"), 1)
            act.wait_ge(sem("w2_ps"), 1)
            act.activation(w2[:, :, :], bank[7][:, :].rearrange("p (a d) -> p a d", a=FT), ACT.Copy)\
                .then_inc(sem("w2"), 1)

            def ln_evac(n, dst):
                act.wait_ge(sem("zt_ps"), n + 1)
                act.activation(dst, bank[6][:, :], ACT.Copy).then_inc(sem("z"), 1)

            for c in range(NCH):
                if c >= 2:
                    act.wait_ge(sem("fh_ps"), FT * (c - 1))
                ln_evac(c, zT[:, c % 2, :])
                for f in range(FT):
                    n = FT * c + f
                    act.wait_ge(sem("fh_ps"), n + 1)
                    if c >= 2:
                        act.wait_ge(sem("fo_ps"), c - 1)
                    act.activation(hB[:, c % 2, f, :], bank[2 + f % 2][:, :], ACT.Gelu_apprx_tanh)\
                        .then_inc(sem("fh"), 1)
            act.wait_ge(sem("bqs"), 1)

            def att1(c):
                if c >= 2:
                    act.wait_ge(sem("q_ps"), c - 1)
                else:
                    act.wait_ge(sem("fh_ps"), FT * NCH)
                ln_evac(NCH + c, zT[:, c % 2, :])
                act.wait_ge(sem("q_ps"), c + 1)
                act.activation(qT[:, c % 2, :], bank[2][:, :], ACT.Identity, bias=bqs[:, 0:1], scale=SCALE)\
                    .then_inc(sem("q"), 1)
                act.wait_ge(sem("nmax"), c + 1)
                if c >= 2:
                    act.wait_ge(sem("pn"), c - 1)
                for j in range(BPC):
                    act.activation(prob[:, c % 2, j, :], bank[3][:, j * S:(j + 1) * S], ACT.Exp,
                                   bias=nmax[:, c % 2, j:j + 1], accum_out=psum_[:, c % 2, j:j + 1])\
                        .then_inc(sem("prob"), 1)

            def att2(c):
                act.wait_ge(sem("o_ps"), c + 1)
                if c >= 2:
                    act.wait_ge(sem("x3_ps"), c - 1)
                act.activation(oT[:, c % 2, :], bank[5][:, :], ACT.Identity, bias=W("bv"))\
                    .then_inc(sem("o"), 1)
            for c in range(NCH + 1):
                if c < NCH:
                    att1(c)
                if c >= 1:
                    att2(c - 1)
            for c in range(NCH):
                ln_evac(2 * NCH + c, xi[:, ck(c)])
                act.wait_ge(sem("r1_ps"), c + 1)
                if c >= 2:
                    act.wait_ge(sem("lg_ps"), c - 1)
                act.activation(r1[0:32, c % 2, :], bank[2][0:32, :], ACT.Gelu, bias=W("br1"))\
                    .then_inc(sem("r1"), 1)
            act.wait_ge(sem("dl"), 1)
            act.activation(rt[:, 1, :], rt[:, 0, :], ACT.Exp).then_inc(sem("de"), 1)
            act.activation(swc[:, 0:1], W("sw"), ACT.Exp, scale=-1.0).then_inc(sem("swe"), 1)
            for n in range(2 * NCH):
                k, c = n // NCH, n % NCH
                act.wait_ge(sem("m_ps"), n + 1)
                act.activation(m72[:, k, ck(c)], bank[n % 2][0:96, :], ACT.Copy).then_inc(sem("m72"), 1)
            for n in range(HT * NCH):
                j, c = n // NCH, n % NCH
                act.wait_ge(sem("me_ps0"), n + 1)
                act.activation(mexp[:, 0, j, ck(c)], bank[2 + n % 2][:, :], ACT.Copy).then_inc(sem("me0"), 1)

            def refine1(s):
                for j in range(2):
                    act.wait_ge(sem("f1_ps"), 2 * s + j + 1)
                    if s >= 1:
                        act.wait_ge(sem("f2_ps"), s)
                    act.activation(fh[:, j, :], bank[6 + (j + 1) % 2][:, :], ACT.Gelu,
                                   bias=W("bf1", j, j + 1)).then_inc(sem("fhg"), 1)
                act.wait_ge(sem("h1_ps"), s + 1)
                if s >= 1:
                    act.wait_ge(sem("h2_ps"), s)
                act.activation(h1, bank[7][0:32, :], ACT.Gelu, bias=W("bh1")).then_inc(sem("h1"), 1)

            def refine2(s):
                act.wait_ge(sem("h2_ps"), s + 1)
                if s >= 1:
                    act.wait_ge(sem("rr"), 2 * s)
                act.activation(th, bank[7][:, :], ACT.Tanh, bias=bh2h[:, 0:1], scale=0.5)\
                    .then_inc(sem("th"), 1)

            for s in range(STEPS + 1):
                it2 = s >= NCH
                if s < STEPS:
                    for j in range(HT):
                        act.wait_ge(sem("hid_ps"), 5 * s + j + 1)
                        if s >= 1:
                            act.wait_ge(sem("hm"), 8 * (s - 1) + 2 * j + 2)
                        act.activation(hid[:, j, :], bank[6 + j % 2][:, :], ACT.Gelu,
                                       bias=W("eb1", j, j + 1)).then_inc(sem("hid"), 1)
                    act.wait_ge(sem("hid_ps"), 5 * s + 5)
                    if s >= 1:
                        act.wait_ge(sem("g_ps"), 3 * (s - 1) + 1)
                    act.activation(hs, bank[6][0:H, :], ACT.Gelu, bias=W("bs1")).then_inc(sem("hs"), 1)
                if s >= 1:
                    refine1(s - 1)
                    refine2(s - 1)
                if s == STEPS:
                    break
                for k in range(3):
                    if s >= 1:
                        act.wait_ge(sem("sp"), 3 * (s - 1) + k + 1)
                    act.wait_ge(sem("b_ps"), 3 * s + k + 1)
                    act.activation(ab[:, k, :], bank[3 + k][:, :], ACT.Abs).then_inc(sem("ab"), 1)
                act.wait_ge(sem("ab"), 3 * s + 3)
                act.activation(ab[:, :, :], ab[:, :, :], ACT.Exp, scale=-1.0).then_inc(sem("ex"), 1)
                act.wait_ge(sem("ex"), s + 1)
                act.activation(ab[:, :, :], ab[:, :, :], ACT.Ln, bias=1.0).then_inc(sem("ln"), 1)
                for k in range(3):
                    r = 0
                    if it2:
                        q = s - NCH
                        act.wait_ge(sem("a_ps"), 3 * q + k + 1)
                        if q >= 1:
                            act.wait_ge(sem("y"), 3 * s)
                        act.activation(ta[:, k, :], bank[(2 * k) % 3][:, :], ACT.Tanh, scale=0.5)\
                            .then_inc(sem("ta"), 1)
                    act.wait_ge(sem("g_ps"), 3 * s + k + 1)
                    if s >= 1:
                        act.wait_ge(sem("xn"), s)
                    act.activation(tg[:, k, :], bank[(2 * k + 1) % 3][:, :], ACT.Tanh, scale=0.5)\
                        .then_inc(sem("tg"), 1)

        @block.vector
        def _(dve):
            chain = [0]

            def link(ins):
                chain[0] += 1
                ins.then_inc(sem("dve_chain"), 1)
                dve.wait_ge(sem("dve_chain"), chain[0])

            dve.wait_ge(sem("in_A"), 16)
            for i, n in enumerate(("log1", "log2")):
                dve.tensor_reduce(lg_n[:, i:i + 1], A(n), AX.X, ALU.max, negate=True)\
                    .then_inc(sem("lgn"), 1)
            dve.wait_ge(sem("in_xtok"), 16)
            for b in range(B):
                dve.bn_stats(st[:, b, :], xtok[:, b, :]).then_inc(sem("st"), 1)
            for b in range(B):
                dve.wait_ge(sem("st"), b + 1)
                dve.bn_aggr(mv[:, b, :], st[:, b, :]).then_inc(sem("mv"), 1)
            dve.wait_ge(sem("mv"), B)
            dve.tensor_scalar(veps[:, :], mv[:, :, 1], EPS, None, ALU.add).then_inc(sem("veps"), 1)
            dve.wait_ge(sem("lge"), 2)
            link(dve.reciprocal(lg_n[:, 4:6], lg_n[:, 2:4]))
            for i in range(2):
                for half in range(2):
                    p = slice(64 * half, 64 * half + 64)
                    dve.tensor_scalar(wcol[p, i, :], lg_e[p, i, half:PRIM:2], lg_n[p, 4 + i:5 + i], None,
                                      ALU.mult).then_inc(sem("wcol"), 1)
            dve.wait_ge(sem("qk_ps"), 1)
            qps = bank[0][:, 0:128].rearrange("p (b c) -> p b c", c=DH)
            kps = bank[0][:, 128:256].rearrange("p (b c) -> p b c", c=DH)
            colsum = bank[0][:, 256:264].unsqueeze(1).to_broadcast([128, B, DH])
            mean = mv[:, :, 0:1].to_broadcast([128, B, DH])
            bq_b = A("bq8").unsqueeze(1).to_broadcast([128, B, DH])
            link(dve.tensor_tensor(qt[:, 0], colsum, mean, ALU.mult))
            link(dve.tensor_tensor(qt[:, 1], qps, qt[:, 0], ALU.subtract))
            dve.wait_ge(sem("rstd"), 1)
            link(dve.tensor_tensor(qt[:, 2], qt[:, 1], rstd[:, :].unsqueeze(2).to_broadcast([128, B, DH]),
                                   ALU.mult))
            dve.tensor_tensor(qk[:, 0, :].rearrange("p (b c) -> p b c", c=DH), qt[:, 2], bq_b, ALU.add)\
                .then_inc(sem("qk"), 1)
            dve.tensor_tensor(qk[:, 1, :].rearrange("p (b c) -> p b c", c=DH), kps, bq_b, ALU.add)\
                .then_inc(sem("qk"), 1)
            dve.wait_ge(sem("dft_ps"), 1)
            link(dve.tensor_copy(fr[:, :, :, :],
                                 bank[4][0:NF, :].rearrange("p (a b n) -> p a b n", a=2, b=2)))
            for n, (i, j) in enumerate(((0, 0), (1, 1), (0, 1), (1, 0))):
                last = dve.tensor_tensor_reduce(out=junk[:, n, :], in0=fr[:, i, 0, :], in1=fr[:, j, 1, :],
                                                scale=1.0, scalar=0.0, op0=ALU.mult, op1=ALU.add,
                                                accum_out=red[:, n:n + 1])
                last.then_inc(sem("spec"), 1)
            dve.wait_ge(sem("spec"), 4)
            dve.tensor_scalar(red[:, 4:5], red[:, 0:1], red[:, 1:2], A("a1"), ALU.add, ALU.mult)\
                .then_inc(sem("spec"), 1)
            dve.tensor_scalar(red[:, 5:6], red[:, 3:4], red[:, 2:3], A("a1"), ALU.subtract, ALU.mult)\
                .then_inc(sem("spec"), 1)
            dve.wait_ge(sem("ones"), 1)
            dve.wait_ge(sem("spec"), 6)
            for n in range(2):
                dve.tensor_scalar(reB[:, n, :], ones[0:NF, 0:NF], red[:, 4 + n:5 + n], None, ALU.mult)\
                    .then_inc(sem("reB"), 1)
            dve.wait_ge(sem("wcol"), 4)
            dve.wait_ge(sem("in_a1"), 16)
            dve.tensor_tensor(a1[:, :, :], a1[:, :, :], wcol[:, 0, :].unsqueeze(2).to_broadcast([128, KC, D]),
                              ALU.mult).then_inc(sem("a1s"), 1)
            dve.wait_ge(sem("cor_ps"), 1)
            link(dve.tensor_copy(cor[:, 0, :], bank[5][0:NF, 0:128]))
            link(dve.max(m8[:, 0, :], cor[:, 0, :]))
            dve.tensor_scalar(red[:, 6:7], m8[:, 0, 0:1], -1.0, None, ALU.mult).then_inc(sem("negmax"), 1)
            link(dve.match_replace(cor[:, 1, :], m8[:, 0, :], cor[:, 0, :], NEG))
            link(dve.max(m8[:, 1, :], cor[:, 1, :]))
            link(dve.memset(m8[:, 2, :], NEG))
            link(dve.tensor_copy(m8[:, 2, 0:TOPK - 8], m8[:, 1, 0:TOPK - 8]))
            link(dve.match_replace(cor[:, 2, :], m8[:, 2, :], cor[:, 1, :], NEG))
            link(dve.tensor_scalar(junk[:, 4, :], cor[:, 2, :], NEG, None, ALU.is_equal))
            dve.wait_ge(sem("ecor"), 1)
            link(dve.tensor_tensor_reduce(out=ecor[:, 1, :], in0=ecor[:, 0, :], in1=junk[:, 4, :],
                                          scale=1.0, scalar=0.0, op0=ALU.mult, op1=ALU.add,
                                          accum_out=red[:, 7:8]))
            dve.reciprocal(red[:, 8:9], red[:, 7:8]).then_inc(sem("wspec"), 1)
            for n, name in enumerate(("cf", "sf")):
                dve.tensor_tensor_reduce(out=junk[:, n, :], in0=ecor[:, 1, :], in1=A(name),
                                         scale=1.0, scalar=0.0, op0=ALU.mult, op1=ALU.add,
                                         accum_out=red[:, 9 + n:10 + n]).then_inc(sem("wspec"), 1)
            dve.wait_ge(sem("wspec"), 3)
            link(dve.tensor_scalar(red[:, 0:2], red[:, 9:11], red[:, 8:9], A("a2"), ALU.mult, ALU.mult))
            wc, ws = red[:, 0:1], red[:, 1:2]
            vc, vs = fr[:, 0, 1, :], fr[:, 1, 1, :]
            dve.tensor_scalar(ab_f[:, 0, :], vs, ws, None, ALU.mult).then_inc(sem("spc"), 1)
            dve.tensor_scalar(ab_f[:, 1, :], vc, ws, None, ALU.mult).then_inc(sem("spc"), 1)
            dve.wait_ge(sem("spc"), 2)
            dve.scalar_tensor_tensor(ab_f[:, 2, :], vc, wc, ab_f[:, 0, :], ALU.mult, ALU.add)\
                .then_inc(sem("abf"), 1)
            dve.scalar_tensor_tensor(ab_f[:, 3, :], vs, wc, ab_f[:, 1, :], ALU.mult, ALU.subtract)\
                .then_inc(sem("abf"), 1)
            dve.wait_ge(sem("in_b2"), 16)
            dve.tensor_tensor(b2[:, :, :], b2[:, :, :], wcol[:, 1, :].unsqueeze(2).to_broadcast([128, KC, D]),
                              ALU.mult).then_inc(sem("b2s"), 1)
            dve.wait_ge(sem("yb"), 1)
            dve.wait_ge(sem("in_x"), 16)
            dve.wait_ge(sem("qk_ps"), 1)
            for c in range(NCH):
                xv = xT[:, ck(c)].rearrange("p (b h c) -> p b h c", b=BPC, h=HEADS)
                yv = yb[:, c * BPC * DH:(c + 1) * BPC * DH].rearrange("p (b c) -> p b c", b=BPC)\
                    .unsqueeze(2).to_broadcast([128, BPC, HEADS, DH])
                dve.tensor_tensor(xv, xv, yv, ALU.add).then_inc(sem("x1"), 1)

            def ln_stats(n):
                t = bank[n % 2]
                dve.wait_ge(sem("tok_ps"), n + 1)
                if n >= 2:
                    dve.wait_ge(sem("ztok"), BPC * (n - 1))
                for j in range(BPC):
                    dve.bn_stats(lst[:, n % 2, j, :], t[:, j * D:(j + 1) * D]).then_inc(sem("lst"), 1)
                for j in range(BPC):
                    dve.wait_ge(sem("lst"), BPC * n + j + 1)
                    dve.bn_aggr(lmv[:, n % 2, j, :], lst[:, n % 2, j, :]).then_inc(sem("lmv"), 1)
                dve.wait_ge(sem("lmv"), BPC * (n + 1))
                if n >= 2:
                    dve.wait_ge(sem("lrs"), n - 1)
                dve.tensor_scalar(lve[:, n % 2, :], lmv[:, n % 2, :, 1], EPS, None, ALU.add)\
                    .then_inc(sem("lve"), 1)

            def ln_scale(n):
                t = bank[n % 2]
                dve.wait_ge(sem("lrs"), n + 1)
                if n >= 2:
                    dve.wait_ge(sem("zt_ps"), n - 1)
                for j in range(BPC):
                    dve.tensor_scalar(ztok[:, n % 2, j, :], t[:, j * D:(j + 1) * D], lmv[:, n % 2, j, 0:1],
                                      lrs[:, n % 2, j:j + 1], ALU.subtract, ALU.mult)\
                        .then_inc(sem("ztok"), 1)

            def ffn_add(c):
                dve.wait_ge(sem("fo_ps"), c + 1)
                dve.tensor_tensor(xT[:, ck(c)], bank[4 + c % 2][:, :], xT[:, ck(c)], ALU.add)\
                    .then_inc(sem("x2"), 1)
            ln_stats(0)
            for c in range(NCH):
                ln_scale(c)
                if c + 1 < NCH:
                    ln_stats(c + 1)
                if c >= 1:
                    ffn_add(c - 1)
            ffn_add(NCH - 1)
            dve.wait_ge(sem("in_B"), 16)
            dve.tensor_scalar(bqs[:, :], W("bq"), SCALE, None, ALU.mult).then_inc(sem("bqs"), 1)
            dve.tensor_scalar(iwh[:, :], W("iw"), 0.5, None, ALU.mult).then_inc(sem("consts"), 1)
            dve.tensor_scalar(bh2h[:, :], W("bh2"), 0.5, None, ALU.mult).then_inc(sem("consts"), 1)
            dve.tensor_copy(identb[:, :], ident).then_inc(sem("identb"), 1)
            dve.tensor_copy(selb[:, :], W("sel")).then_inc(sem("selb"), 1)
            for i, n in enumerate(("eb2", "bs2")):
                link(dve.tensor_copy(bhi[:, 0, i, :], W(n)))
                link(dve.tensor_tensor(brem[:, 0, i, :], W(n), bhi[:, 0, i, :], ALU.subtract))
                link(dve.tensor_copy(bhi[:, 1, i, :], brem[:, 0, i, :]))
                link(dve.tensor_tensor(brem[:, 1, i, :], brem[:, 0, i, :], bhi[:, 1, i, :], ALU.subtract))
                link(dve.tensor_copy(bhi[:, 2, i, :], brem[:, 1, i, :]))
                for q in range(3):
                    p = slice(32 * q, 32 * q + 32)
                    dve.tensor_copy(bparts[p, i, :], bhi[p, q, i, :]).then_inc(sem("bparts"), 1)

            def att_max(c):
                dve.wait_ge(sem("s_ps"), c + 1)
                if c >= 2:
                    dve.wait_ge(sem("prob"), BPC * (c - 1))
                dve.tensor_reduce(nmax[:, c % 2, :], bank[3][:, :].rearrange("p (b k) -> p b k", b=BPC),
                                  AX.X, ALU.max, negate=True).then_inc(sem("nmax"), 1)

            def att_norm(c):
                dve.wait_ge(sem("prob"), BPC * (c + 1))
                link(dve.reciprocal(prec[:, c % 2, :], psum_[:, c % 2, :]))
                if c >= 2:
                    dve.wait_ge(sem("pt_ps"), c - 1)
                dve.tensor_tensor(pn[:, c % 2], prob[:, c % 2],
                                  prec[:, c % 2, :].unsqueeze(2).to_broadcast([128, BPC, S]), ALU.mult)\
                    .then_inc(sem("pn"), 1)

            def att_pt(c):
                dve.wait_ge(sem("pt_ps"), c + 1)
                if c >= 2:
                    dve.wait_ge(sem("o_ps"), c - 1)
                dve.tensor_copy(pT[:, c % 2], bank[4][:, :].rearrange("p (b k) -> p b k", b=BPC))\
                    .then_inc(sem("pT"), 1)

            def att_add(c):
                dve.wait_ge(sem("x3_ps"), c + 1)
                dve.scalar_tensor_tensor(xT[:, ck(c)], bank[7][:, :], W("bo"), xT[:, ck(c)],
                                         ALU.add, ALU.add).then_inc(sem("x3"), 1)
            ln_stats(NCH)
            for c in range(NCH + 1):
                if c < NCH:
                    ln_scale(NCH + c)
                    if c + 1 < NCH:
                        ln_stats(NCH + c + 1)
                    att_max(c)
                if c >= 1:
                    att_pt(c - 1)
                    att_add(c - 1)
                if c < NCH:
                    att_norm(c)
            ln_stats(2 * NCH)
            for c in range(NCH):
                ln_scale(2 * NCH + c)
                if c + 1 < NCH:
                    ln_stats(2 * NCH + c + 1)
                dve.wait_ge(sem("lg_ps"), c + 1)
                t = slice(c * BPC, (c + 1) * BPC)
                dve.tensor_copy(lg[:, t, :], bank[3][:, 0:BPC * E].rearrange("p (b e) -> p b e", b=BPC))\
                    .then_inc(sem("lg"), 1)
            dve.wait_ge(sem("lg"), NCH)
            for b in range(B):
                dve.max(top[:, b, :], lg[:, b, :]).then_inc(sem("top"), 1)
            for b in range(B):
                dve.wait_ge(sem("top"), b + 1)
                dve.max_index(tix[:, b, :], top[:, b, :], lg[:, b, :]).then_inc(sem("tix"), 1)
            dve.tensor_tensor(rt[:, 0, :], top[:, :, 1], top[:, :, 0], ALU.subtract).then_inc(sem("dl"), 1)
            dve.wait_ge(sem("tix"), B)
            link(dve.tensor_copy(tif[:, :, :], tix[:, :, :]))
            dve.wait_ge(sem("mrep0"), 1)
            iota = W("iota").unsqueeze(1).to_broadcast([128, B, E])
            for k in range(2):
                for q in range(3):
                    dve.tensor_tensor(mrep[:, k, :, 32 * q:32 * q + E], iota,
                                      tif[:, :, k:k + 1].to_broadcast([128, B, E]), ALU.is_equal)\
                        .then_inc(sem("mrep"), 1)
            dve.wait_ge(sem("de"), 1)
            dve.wait_ge(sem("swe"), 1)
            link(dve.tensor_scalar(rt[:, 2, :], rt[:, 1, :], 1.0, None, ALU.add))
            link(dve.reciprocal(rt[:, 3, :], rt[:, 2, :]))
            link(dve.tensor_tensor(rt[:, 4, :], rt[:, 1, :], rt[:, 3, :], ALU.mult))
            link(dve.tensor_scalar(swc[:, 1:2], swc[:, 0:1], 1.0, None, ALU.add))
            link(dve.reciprocal(swc[:, 2:3], swc[:, 1:2]))
            link(dve.tensor_scalar(swc[:, 3:4], swc[:, 2:3], -1.0, 1.0, ALU.mult, ALU.add))
            for k in range(2):
                dve.tensor_scalar(cf2[:, k, :], rt[:, 3 + k, :], swc[:, 3:4], None, ALU.mult)\
                    .then_inc(sem("cf2"), 1)
            for n in range(2 * NCH):
                k, c = n // NCH, n % NCH
                dve.wait_ge(sem("c_ps"), n + 1)
                dve.tensor_copy(cb[:, k, ck(c)], bank[6 + n % 2][:, :]).then_inc(sem("cb"), 1)
            for n in range(HT * NCH):
                j, c = n // NCH, n % NCH
                dve.wait_ge(sem("me_ps1"), n + 1)
                dve.tensor_copy(mexp[:, 1, j, ck(c)], bank[4 + n % 2][:, :]).then_inc(sem("me1"), 1)
            dve.wait_ge(sem("me0"), HT * NCH)
            dve.wait_ge(sem("me1"), HT * NCH)
            dve.wait_ge(sem("consts"), 2)

            def refine(s):
                c = s % NCH
                dve.wait_ge(sem("f2_ps"), s + 1)
                dve.tensor_scalar(rr, bank[6][:, :], W("bf2"), iwh[:, 0:1], ALU.add, ALU.mult)\
                    .then_inc(sem("rr"), 1)
                dve.wait_ge(sem("rr"), 2 * s + 1)
                dve.wait_ge(sem("th"), s + 1)
                dve.scalar_tensor_tensor(rr, th, 1.0, rr, ALU.add, ALU.mult)\
                    .then_inc(sem("rr"), 1)
                dve.wait_ge(sem("rr"), 2 * s + 2)
                dve.tensor_tensor(xi[:, ck(c)], xi[:, ck(c)], rr, ALU.add).then_inc(sem("xi"), 1)
                if s >= NCH:
                    dve.wait_ge(sem("xi"), s + 1)
                    dve.tensor_tensor(res[:, ck(c)], xi[:, ck(c)], xT[:, ck(c)], ALU.add)\
                        .then_inc(sem("res"), 1)

            for s in range(STEPS):
                c = s % NCH
                it2 = s >= NCH
                if s == 0:
                    dve.wait_ge(sem("z"), 3 * NCH)
                if s >= 1:
                    dve.wait_ge(sem("ew"), 2 * s)
                dve.tensor_scalar(ew[:, 0, :], xi[:, ck(c)], W("mu"), None, ALU.subtract).then_inc(sem("e0"), 1)
                if it2:
                    dve.tensor_scalar(pw[:, 0, :], vT[:, ck(c)], swc[:, 2:3], None, ALU.mult)\
                        .then_inc(sem("pw0"), 1)
                dve.wait_ge(sem("e0"), s + 1)
                dve.tensor_scalar(ew[:, 1, :], ew[:, 0, :], swc[:, 2:3], None, ALU.mult).then_inc(sem("e1"), 1)
                for j in range(HT):
                    dve.wait_ge(sem("hid"), HT * s + j + 1)
                    if s >= 1 and j == 0:
                        dve.wait_ge(sem("g_ps"), 3 * s)
                    for k in range(2):
                        dve.tensor_tensor(hm[:, k, j, :], hid[:, j, :], mexp[:, k, j, ck(c)], ALU.mult)\
                            .then_inc(sem("hm"), 1)
                if s >= 1:
                    refine(s - 1)
                dve.wait_ge(sem("ln"), s + 1)
                for k in range(3):
                    dve.scalar_tensor_tensor(sm[:, k, :], bank[3 + k][:, :], 0.0, ab[:, k, :],
                                             ALU.max, ALU.add).then_inc(sem("sp"), 1)
                dve.wait_ge(sem("e1"), s + 1)
                dve.wait_ge(sem("ew"), 2 * s + 2)
                for k in range(3):
                    dve.wait_ge(sem("sp"), 3 * s + k + 1)
                    dve.tensor_tensor(sm[:, k, :], sm[:, k, :], ew[:, 1 + k, :], ALU.mult)\
                        .then_inc(sem("w"), 1)
                dve.wait_ge(sem("w"), 3 * s + 3)
                if it2:
                    q = s - NCH
                    dve.wait_ge(sem("pw0"), q + 1)
                    dve.wait_ge(sem("pw"), 2 * q + 2)
                    for k in range(3):
                        dve.wait_ge(sem("ta"), 3 * q + k + 1)
                        dve.scalar_tensor_tensor(ta[:, k, :], ta[:, k, :], 1.0, pw[:, k, :],
                                                 ALU.add, ALU.mult).then_inc(sem("u"), 1)
                        dve.wait_ge(sem("u"), 3 * q + k + 1)
                        dve.scalar_tensor_tensor(ta[:, k, :], ta[:, k, :], 0.5, sm[:, k, :],
                                                 ALU.mult, ALU.subtract).then_inc(sem("vv"), 1)
                        dve.wait_ge(sem("tg"), 3 * s + k + 1)
                        dve.wait_ge(sem("vv"), 3 * q + k + 1)
                        dve.scalar_tensor_tensor(tg[:, k, :], tg[:, k, :], 1.0, ta[:, k, :],
                                                 ALU.add, ALU.mult).then_inc(sem("y"), 1)
                else:
                    for k in range(3):
                        dve.wait_ge(sem("tg"), 3 * s + k + 1)
                        dve.scalar_tensor_tensor(tg[:, k, :], tg[:, k, :], 1.0, sm[:, k, :],
                                                 ALU.add, ALU.mult).then_inc(sem("y"), 1)
                    dve.wait_ge(sem("y"), 3 * s + 3)
                    link(dve.tensor_tensor(sm[:, 0, :], sm[:, 0, :], sm[:, 1, :], ALU.add))
                    dve.scalar_tensor_tensor(vT[:, ck(c)], sm[:, 0, :], -1.0, sm[:, 2, :],
                                             ALU.mult, ALU.subtract).then_inc(sem("v1"), 1)
                dve.wait_ge(sem("y"), 3 * s + 3)
                link(dve.tensor_tensor(tg[:, 0, :], tg[:, 0, :], tg[:, 1, :], ALU.add))
                link(dve.tensor_tensor(tg[:, 0, :], tg[:, 0, :], tg[:, 2, :], ALU.add))
                if s >= 1:
                    dve.wait_ge(sem("h1_ps"), s)
                dve.scalar_tensor_tensor(xn, tg[:, 0, :], 0.05 if it2 else -0.05, xi[:, ck(c)],
                                         ALU.mult, ALU.add).then_inc(sem("xn"), 1)
            refine(STEPS - 1)

        @block.tensor
        def _(pe):
            def mm(out, lhsT, rhs, start=True, stop=True):
                return pe.matmul(out, lhsT, rhs, start=start, stop=stop)

            pe.wait_ge(sem("ones"), 1)
            pe.wait_ge(sem("in_A"), 16)
            mm(bank[1][0:NF, 0:D], A("cl"), A("wout"))
            mm(bank[1][0:NF, D:2 * D], A("sl"), A("wout")).then_inc(sem("cw_ps"), 1)
            mm(bank[0][:, 256:264], ones[:, :], A("wq8"))
            pe.wait_ge(sem("in_x"), 16)
            for b in range(B):
                mm(bank[0][:, b * DH:(b + 1) * DH], xT[:, b * S:(b + 1) * S], A("wq8"))
            pe.wait_ge(sem("in_ctx"), 16)
            for b in range(B):
                last = mm(bank[0][:, 128 + b * DH:128 + (b + 1) * DH], ctxT[:, b * S:(b + 1) * S], A("wq8"))
            last.then_inc(sem("qk_ps"), 1)
            for c in range(NCH):
                if c >= 2:
                    pe.wait_ge(sem("k"), c - 1)
                mm(bank[2 + c % 2][:, :], A("wk"), ctxT[:, ck(c)]).then_inc(sem("k_ps"), 1)
            pe.wait_ge(sem("qk"), 2)
            mm(bank[4][0:NF, 0:256], A("cl"), qk[:, :, :])
            mm(bank[4][0:NF, 256:512], A("sl"), qk[:, :, :]).then_inc(sem("dft_ps"), 1)
            for c in range(NCH):
                pe.wait_ge(sem("k"), min(c + 3, NCH))
                if c >= 2:
                    pe.wait_ge(sem("v"), c - 1)
                for j in range(BPC):
                    b = c * BPC + j
                    last = mm(bank[2 + c % 2][:, j * D:(j + 1) * D], ctxT[:, b * S:(b + 1) * S], A("wv"))
                last.then_inc(sem("v_ps"), 1)
            pe.wait_ge(sem("reB"), 2)
            mm(bank[5][0:NF, 0:128], reB[:, 0, :], A("cf"), stop=False)
            mm(bank[5][0:NF, 0:128], reB[:, 1, :], A("sf"), start=False).then_inc(sem("cor_ps"), 1)
            pe.wait_ge(sem("a1s"), 1)
            pe.wait_ge(sem("in_b1"), 16)
            for k in range(KC):
                last = mm(bank[6][:, :], a1[:, k, :], b1[:, k, :], start=k == 0, stop=k == KC - 1)
            last.then_inc(sem("w1_ps"), 1)
            pe.wait_ge(sem("abf"), 2)
            pe.wait_ge(sem("cw"), 1)
            mm(bank[4][:, 0:128], cw[:, 0, :], ab_f[:, 2, :], stop=False)
            mm(bank[4][:, 0:128], cw[:, 1, :], ab_f[:, 3, :], start=False).then_inc(sem("y_ps"), 1)
            pe.wait_ge(sem("b2s"), 1)
            pe.wait_ge(sem("in_a2"), 16)
            for f in range(FT):
                for k in range(KC):
                    last = mm(bank[7][:, f * D:(f + 1) * D], a2[:, k, f * 128:(f + 1) * 128], b2[:, k, :],
                              start=k == 0, stop=k == KC - 1)
            last.then_inc(sem("w2_ps"), 1)

            def ln_tok(n, ready):
                pe.wait_ge(sem(ready), n % NCH + 1)
                if n >= 2:
                    pe.wait_ge(sem("ztok"), BPC * (n - 1))
                for j in range(BPC):
                    t = (n % NCH) * BPC + j
                    last = pe.transpose(bank[n % 2][:, j * 128:(j + 1) * 128], xT[:, t * 128:(t + 1) * 128],
                                        ident)
                last.then_inc(sem("tok_ps"), 1)

            def ln_zt(n):
                pe.wait_ge(sem("ztok"), BPC * (n + 1))
                if n == 0:
                    pe.wait_ge(sem("w1"), 1)
                else:
                    pe.wait_ge(sem("z"), n)
                for j in range(BPC):
                    last = pe.transpose(bank[6][:, j * 128:(j + 1) * 128], ztok[:, n % 2, j, :], ident)
                last.then_inc(sem("zt_ps"), 1)

            pe.wait_ge(sem("cw"), 1)
            pe.wait_ge(sem("v"), NCH)
            pe.wait_ge(sem("w2"), 1)
            ln_tok(0, "x1")
            ln_zt(0)
            for c in range(NCH):
                if c + 1 < NCH:
                    ln_tok(c + 1, "x1")
                pe.wait_ge(sem("z"), c + 1)
                for f in range(FT):
                    n = FT * c + f
                    if n >= 2:
                        pe.wait_ge(sem("fh"), n - 1)
                    mm(bank[2 + f % 2][:, :], w1[:, f * 128:(f + 1) * 128], zT[:, c % 2, :])\
                        .then_inc(sem("fh_ps"), 1)
                if c + 1 < NCH:
                    ln_zt(c + 1)
                if c >= 2:
                    pe.wait_ge(sem("x2"), c - 1)
                for f in range(FT):
                    pe.wait_ge(sem("fh"), FT * c + f + 1)
                    last = mm(bank[4 + c % 2][:, :], w2[:, f, :], hB[:, c % 2, f, :],
                              start=f == 0, stop=f == FT - 1)
                last.then_inc(sem("fo_ps"), 1)
            pe.wait_ge(sem("in_B"), 16)

            def att1(c):
                ln_zt(NCH + c)
                pe.wait_ge(sem("z"), NCH + c + 1)
                pe.wait_ge(sem("fh"), FT * NCH)
                if c >= 1:
                    pe.wait_ge(sem("q"), c)
                mm(bank[2][:, :], W("wq"), zT[:, c % 2, :]).then_inc(sem("q_ps"), 1)
                if c + 1 < NCH:
                    ln_tok(NCH + c + 1, "x2")
                pe.wait_ge(sem("q"), c + 1)
                if c >= 1:
                    pe.wait_ge(sem("prob"), BPC * c)
                for j in range(BPC):
                    b = c * BPC + j
                    last = mm(bank[3][:, j * S:(j + 1) * S], qT[:, c % 2, j * S:(j + 1) * S],
                              kT[:, b * S:(b + 1) * S])
                last.then_inc(sem("s_ps"), 1)

            def att2(c):
                pe.wait_ge(sem("pn"), c + 1)
                pe.wait_ge(sem("x2"), NCH)
                if c >= 1:
                    pe.wait_ge(sem("pT"), c)
                for j in range(BPC):
                    last = pe.transpose(bank[4][:, j * S:(j + 1) * S], pn[:, c % 2, j, :], ident)
                last.then_inc(sem("pt_ps"), 1)
                pe.wait_ge(sem("pT"), c + 1)
                if c >= 1:
                    pe.wait_ge(sem("o"), c)
                for j in range(BPC):
                    b = c * BPC + j
                    last = mm(bank[5][:, j * S:(j + 1) * S], vtok[:, b, :], pT[:, c % 2, j, :])
                last.then_inc(sem("o_ps"), 1)
                pe.wait_ge(sem("o"), c + 1)
                if c >= 1:
                    pe.wait_ge(sem("x3"), c)
                mm(bank[7][:, :], W("wo"), oT[:, c % 2, :]).then_inc(sem("x3_ps"), 1)
            ln_tok(NCH, "x2")
            for c in range(NCH + 1):
                if c < NCH:
                    att1(c)
                if c >= 1:
                    att2(c - 1)
            pe.wait_ge(sem("r1one"), 1)
            ln_tok(2 * NCH, "x3")
            for c in range(NCH):
                ln_zt(2 * NCH + c)
                if c + 1 < NCH:
                    ln_tok(2 * NCH + c + 1, "x3")
                pe.wait_ge(sem("z"), 2 * NCH + c + 1)
                if c >= 1:
                    pe.wait_ge(sem("r1"), c)
                mm(bank[2][0:32, :], W("wr1"), xi[:, ck(c)]).then_inc(sem("r1_ps"), 1)
                pe.wait_ge(sem("r1"), c + 1)
                if c >= 1:
                    pe.wait_ge(sem("lg"), c)
                else:
                    pe.wait_ge(sem("prob"), BPC * NCH)
                for j in range(BPC):
                    last = mm(bank[3][:, j * E:(j + 1) * E], r1[:, c % 2, j * 128:(j + 1) * 128], W("wr2"))
                last.then_inc(sem("lg_ps"), 1)
            pe.wait_ge(sem("mrep"), 6)
            pe.wait_ge(sem("identb"), 1)
            pe.wait_ge(sem("selb"), 1)
            pe.wait_ge(sem("lg"), NCH)
            for n in range(2 * NCH):
                k, c = n // NCH, n % NCH
                if n >= 2:
                    pe.wait_ge(sem("m72"), n - 1)
                for j in range(BPC):
                    last = mm(bank[n % 2][0:96, j * 128:(j + 1) * 128], mrep[:, k, c * BPC + j, :], identb[:, :])
                last.then_inc(sem("m_ps"), 1)
            pe.wait_ge(sem("cf2"), 2)
            pe.wait_ge(sem("z"), 3 * NCH)
            pe.wait_ge(sem("x3"), NCH)
            for n in range(2 * NCH):
                k, c = n // NCH, n % NCH
                if n >= 2:
                    pe.wait_ge(sem("cb"), n - 1)
                for j in range(BPC):
                    t = c * BPC + j
                    last = pe.transpose(bank[6 + n % 2][:, j * 128:(j + 1) * 128],
                                        cf2[:, k, t:t + 1].to_broadcast([128, 128]), ident)
                last.then_inc(sem("c_ps"), 1)
            pe.wait_ge(sem("m72"), 2 * NCH)
            for n in range(HT * NCH):
                j, c = n // NCH, n % NCH
                for k in range(2):
                    if n >= 2:
                        pe.wait_ge(sem(f"me{k}"), n - 1)
                    mm(bank[2 + 2 * k + n % 2][:, :], selb[:, j * 128:(j + 1) * 128], m72[0:E, k, ck(c)])\
                        .then_inc(sem(f"me_ps{k}"), 1)
            pe.wait_ge(sem("bparts"), 6)
            pe.wait_ge(sem("me0"), HT * NCH)
            pe.wait_ge(sem("me1"), HT * NCH)
            pe.wait_ge(sem("cb"), 2 * NCH)
            pe.wait_ge(sem("m72"), 2 * NCH)

            def expert_out(s, k, part, out, last_of=None):
                c = s % NCH
                cols = slice(part * D, (part + 1) * D)
                src = m72[:, k - 1, ck(c)] if k else onesb[:, :]
                mm(out, bparts[:, 0 if k else 1, cols], src, stop=False)
                if k == 0:
                    return mm(out, W("ws2", part * D, (part + 1) * D), hs, start=False)
                for j in range(HT):
                    last = mm(out, W("ew2", j * 3 * D + part * D, j * 3 * D + (part + 1) * D),
                              hm[:, k - 1, j, :], start=False, stop=j == HT - 1)
                return last

            def refine_a(s):
                pe.wait_ge(sem("xn"), s + 1)
                for j in range(2):
                    pe.wait_ge(sem("hid"), HT * min(s + 2, STEPS))
                    if j == 1:
                        pe.wait_ge(sem("hs"), min(s + 2, STEPS))
                    mm(bank[6 + (j + 1) % 2][:, :], W("wf1", j * 128, (j + 1) * 128), xn)\
                        .then_inc(sem("f1_ps"), 1)
                pe.wait_ge(sem("fhg"), 2 * s + 1)
                mm(bank[7][0:32, :], W("wh1"), xn).then_inc(sem("h1_ps"), 1)

            def refine_b(s):
                pe.wait_ge(sem("fhg"), 2 * s + 2)
                for j in range(2):
                    last = mm(bank[6][:, :], W("wf2", j * 128, (j + 1) * 128), fh[:, j, :],
                              start=j == 0, stop=j == 1)
                last.then_inc(sem("f2_ps"), 1)
                pe.wait_ge(sem("h1"), s + 1)
                mm(bank[7][:, :], W("wh2").to_broadcast([32, 128]), h1).then_inc(sem("h2_ps"), 1)

            for s in range(STEPS):
                c, it2 = s % NCH, s >= NCH
                if it2:
                    pe.wait_ge(sem("xi"), s - NCH + 1)
                    pe.wait_ge(sem("v1"), s - NCH + 1)
                for j in range(HT + 1):
                    out = bank[6 + j % 2][:, :] if j < HT else bank[6][0:H, :]
                    name, wd, M = ("ew1", E * H, 128) if j < HT else ("ws1", H, H)
                    o = j * 128 if j < HT else 0
                    if j >= 2:
                        pe.wait_ge(sem("hid"), HT * s + j - 1)
                    elif s >= 2:
                        if j == 0:
                            pe.wait_ge(sem("rr"), 2 * (s - 1) - 1)
                        else:
                            pe.wait_ge(sem("th"), s - 1)
                    last = mm(out, W(name, o, o + M), xi[:, ck(c)], stop=not it2)
                    if it2:
                        last = mm(out, W(name, wd + o, wd + o + M), vT[:, ck(c)], start=False)
                    last.then_inc(sem("hid_ps"), 1)
                if s >= 1:
                    refine_a(s - 1)
                pe.wait_ge(sem("hs"), s + 1)
                for k in range(3):
                    if s >= 1:
                        pe.wait_ge(sem("sp"), 3 * (s - 1) + k + 1)
                    if k:
                        pe.wait_ge(sem("hm"), 8 * s + (8 if k == 2 else 7))
                    expert_out(s, k, 1, bank[3 + k][:, :]).then_inc(sem("b_ps"), 1)
                    if k == 1 and s >= 1:
                        refine_b(s - 1)
                for k in range(3):
                    if it2:
                        q = s - NCH
                        if k == 0:
                            pe.wait_ge(sem("tg"), 3 * s)
                        elif k == 1:
                            pe.wait_ge(sem("tg"), 3 * s)
                        else:
                            pe.wait_ge(sem("tg"), 3 * s + 1)
                        expert_out(s, k, 0, bank[(2 * k) % 3][:, :]).then_inc(sem("a_ps"), 1)
                        if k == 0:
                            pe.wait_ge(sem("tg"), 3 * s)
                        elif k == 1:
                            pe.wait_ge(sem("ta"), 3 * q + 1)
                        else:
                            pe.wait_ge(sem("ta"), 3 * q + 2)
                    elif s >= 1:
                        pe.wait_ge(sem("tg"), 3 * (s - 1) + k + 1)
                    expert_out(s, k, 2, bank[(2 * k + 1) % 3][:, :]).then_inc(sem("g_ps"), 1)
            refine_a(STEPS - 1)
            refine_b(STEPS - 1)


def kernel(**inputs):
    import concourse.bacc as bacc
    from concourse.bass_utils import run_bass_kernel_spmd

    f32 = np.float32
    g = {k: np.asarray(v) for k, v in inputs.items()}

    def col(a, rows=128):
        return np.ascontiguousarray(a.reshape(-1, rows).T)

    def rep(a):
        return np.ascontiguousarray(np.broadcast_to(a.reshape(1, -1), (128, a.size)))

    f = np.arange(NF)[:, None]
    n = np.arange(S)[None, :]
    ang = 2 * np.pi * ((f * n) % S) / S
    twice = np.where((f == 0) | (f == S // 2), 1.0, 2.0)
    shape_only = {"cl": np.cos(ang).T, "sl": np.sin(ang).T, "cf": np.cos(ang), "sf": np.sin(ang),
                  "a1": twice / (S * B * DH), "a2": twice / S, "ident": np.eye(128),
                  "sel": np.kron(np.eye(E), np.ones((1, H))), "iota": np.tile(np.arange(E), (128, 1))}
    shape_only = {k: v.astype(f32) for k, v in shape_only.items()}

    def thrice(a):
        out = np.zeros((96, a.shape[1]), f32)
        for q in range(3):
            out[32 * q:32 * q + a.shape[0]] = a
        return out

    x = lambda k: g["L1_ffn_" + k]
    parts = dict(shape_only)
    parts.update(
        wq8=g["L0_xattn_Wq"], bq8=rep(g["L0_xattn_bq"]), log1=rep(g["L0_ffn_fc1_logits"]),
        log2=rep(g["L0_ffn_fc2_logits"]), wout=g["L0_xattn_Wout"], bout=col(g["L0_xattn_bout"]),
        wq=g["L1_xattn_Wq"], wk=g["L1_xattn_Wk"], wv=g["L1_xattn_Wv"], wo=g["L1_xattn_Wo"],
        bq=col(g["L1_xattn_bq"]), bk=col(g["L1_xattn_bk"]), bv=col(g["L1_xattn_bv"]), bo=col(g["L1_xattn_bo"]),
        wr1=x("w_r1"), br1=col(x("b_r1"), 32), wr2=np.concatenate([x("w_r2"), x("b_r2")[None]], 0),
        wh1=x("w_h1"), bh1=col(x("b_h1"), 32), wh2=x("w_h2"), bh2=rep(x("b_h2")),
        ew1=x("expert_w1").reshape(E, 2, D, H).transpose(2, 1, 0, 3).reshape(D, -1),
        eb1=col(x("expert_b1")),
        ew2=x("expert_w2").reshape(HT, 128, 3 * D).transpose(1, 0, 2).reshape(128, -1),
        eb2=thrice(x("expert_b2")),
        ws1=x("w_s1").reshape(2, D, H).transpose(1, 0, 2).reshape(D, -1), bs1=col(x("b_s1"), H),
        ws2=x("w_s2"), bs2=thrice(x("b_s2")[None]), wf1=x("w_f1"), bf1=col(x("b_f1")),
        wf2=x("w_f2").reshape(2, 128, D).transpose(1, 0, 2).reshape(128, -1), bf2=col(x("b_f2")),
        iw=col(x("integration_weight")), mu=col(x("mu")), sw=rep(x("shared_weight")))

    def pack(layout):
        at, total = columns(layout)
        out = np.zeros((128, total), f32)
        for name, (rows, a, cols) in at.items():
            out[0:rows, a:a + cols] = parts[name]
        return out

    def rows(a):
        return np.ascontiguousarray(a.reshape(KC, 128, -1).transpose(1, 0, 2))

    arrays = {
        "xtok": np.ascontiguousarray(g["x"].transpose(1, 0, 2)),
        "xT": np.ascontiguousarray(g["x"].transpose(2, 0, 1).reshape(D, T)),
        "ctxT": np.ascontiguousarray(g["ctx_1024"].transpose(2, 0, 1).reshape(D, T)),
        "packA": pack(PACK_A), "packB": pack(PACK_B),
        "fc1a": rows(g["L0_ffn_fc1_A"].transpose(0, 2, 1).reshape(PRIM * RANK, D)),
        "fc1b": rows(g["L0_ffn_fc1_B"].reshape(PRIM * RANK, FF)),
        "fc2a": rows(g["L0_ffn_fc2_A"].transpose(0, 2, 1).reshape(PRIM * RANK, FF)),
        "fc2b": rows(g["L0_ffn_fc2_B"].reshape(PRIM * RANK, D)),
    }
    arrays = {"in_" + k: v for k, v in arrays.items()}
    nc = bacc.Bacc("TRN2", target_bir_lowering=False, num_devices=1)
    args = [nc.dram_tensor(k, a.shape, mybir.dt.from_np(a.dtype), kind="ExternalInput").ap()
            for k, a in arrays.items()]
    out = nc.dram_tensor("outT", (D, T), mybir.dt.float32, kind="ExternalOutput").ap()
    build(nc, *args, out)
    r = run_bass_kernel_spmd(nc, [arrays], core_ids=[0])
    got = np.asarray(r.results[0]["outT"])
    return np.ascontiguousarray(got.reshape(D, B, S).transpose(1, 2, 0))
```

```python
import numpy as np
import concourse.bass as bass
from concourse import mybir
from contextlib import ExitStack

B, S, D = 16, 128, 128
T = B * S
CH = 512
NCH = T // CH
BPC = CH // S
DH, HEADS = 8, 16
NF = S // 2 + 1
TOPK = int(2 * np.log(256))
PRIM, RANK, FF = 32, 64, 512
KC = PRIM * RANK // 128
FT = FF // 128
E, H, HT = 8, 64, 4
ITER = 2
EPS = 1e-5
NEG = -3.0e38

PACK_A = [("wv", 128, D), ("wq8", 128, DH), ("bq8", 128, DH), ("log1", 128, PRIM), ("log2", 128, PRIM),
          ("wout", 128, D), ("cl", 128, NF), ("sl", 128, NF), ("cf", NF, S), ("sf", NF, S),
          ("a1", NF, 1), ("a2", NF, 1), ("bout", 128, 1), ("ident", 128, 128),
          ("bk", 128, 1), ("wk", 128, D)]
VK = D + DH
VB = CH // VK
VG = -(-B // VB)
PACK_B = [("wq", 128, D), ("wo", 128, D), ("bq", 128, 1), ("bv", 128, 1), ("bo", 128, 1),
          ("wr1", 128, 32), ("br1", 32, 1), ("wr2", 33, E), ("wh1", 128, 32), ("bh1", 32, 1),
          ("wh2", 32, 1), ("bh2", 128, 1), ("ew1", 128, 2 * E * H), ("eb1", 128, HT),
          ("ew2", 128, HT * 3 * D), ("eb2", 96, 3 * D), ("ws1", 128, 2 * H), ("bs1", H, 1),
          ("ws2", H, 3 * D), ("bs2", 96, 3 * D), ("wf1", 128, 2 * D), ("bf1", 128, 2),
          ("wf2", 128, 2 * D), ("bf2", 128, 1), ("iw", 128, 1), ("mu", 128, 1),
          ("sw", 128, 1), ("tile_expert", 128, HT), ("bias_expert", 96, 1)]


def columns(layout):
    at, out = 0, {}
    for name, rows, cols in layout:
        out[name] = (rows, at, cols)
        at += cols
    return out, at


def build(nc, d_xtok, d_xT, d_ctxT, d_packA, d_packB, d_a1, d_b1, d_a2, d_b2, d_out):
    F, BF, U32 = mybir.dt.float32, mybir.dt.bfloat16, mybir.dt.uint32
    ALU, ACT, AX = mybir.AluOpType, mybir.ActivationFunctionType, mybir.AxisListType
    colA, nA = columns(PACK_A)
    colB, nB = columns(PACK_B)
    SCALE = 1.0 / float(np.sqrt(np.float32(D)))

    ctx = ExitStack()
    with ctx:
        def sb(name, shape, dt=F):
            return ctx.enter_context(nc.sbuf_tensor(name, shape, dt))

        sems = {}

        def sem(name):
            if name not in sems:
                sems[name] = ctx.enter_context(nc.semaphore(name))
            return sems[name]

        xtok_f = sb("xtok", [128, B * D])
        xtok = xtok_f[:, :].rearrange("p (b d) -> p b d", b=B)
        xT = sb("xT", [128, T])
        ctxT = sb("ctxT", [128, T])
        pA = sb("pA", [128, nA])
        pB = sb("pB", [128, nB])
        a1_f = sb("a1", [128, KC * D])
        b1_f = sb("b1", [128, KC * FF])
        a2_f = sb("a2", [128, KC * FF])
        b2_f = sb("b2", [128, KC * D])
        a1 = a1_f[:, :].rearrange("p (k d) -> p k d", k=KC)
        b1 = b1_f[:, :].rearrange("p (k d) -> p k d", k=KC)
        a2 = a2_f[:, :].rearrange("p (k d) -> p k d", k=KC)
        b2 = b2_f[:, :].rearrange("p (k d) -> p k d", k=KC)

        def A(name, a=0, b=None):
            r, at, n = colA[name]
            return pA[0:r, at + a:at + (n if b is None else b)]

        def W(name, a=0, b=None):
            r, at, n = colB[name]
            return pB[0:r, at + a:at + (n if b is None else b)]

        bank = [ctx.enter_context(nc.psum_tensor(f"bank{i}", [128, 512], F)) for i in range(8)]

        hB_f = sb("hB", [128, 2 * FT * CH])
        blk = hB_f[:, :].rearrange("p (n m) -> p n m", m=128)
        qt = hB_f[:, 0:384].rearrange("p (a b c) -> p a b c", a=3, b=B)
        qk = blk[:, 3:5, :]
        cw = blk[0:NF, 5:7, :]
        fr = blk[0:NF, 7:11, :].rearrange("p (a b) n -> p a b n", a=2)
        junk = blk[0:NF, 11:17, :]
        cor = blk[0:NF, 17:20, :]
        ecor = blk[0:NF, 20:22, :]
        ab_f = blk[0:NF, 22:26, :]
        st = sb("st", [128, B, 6])
        mv = sb("mv", [128, B, 2])
        veps = sb("veps", [128, B])
        rstd = sb("rstd", [128, B])
        mhalf = sb("mhalf", [128, B])
        red = sb("red", [NF, 12])
        ones = sb("ones", [128, 128])
        reB = sb("reB", [NF, 2, NF])
        m8 = sb("m8", [NF, 3, 8])
        yb = sb("yb", [128, 128])
        lg_n = sb("lg_n", [128, 6])
        lg_e = sb("lg_e", [128, 2, PRIM])
        wcol = sb("wcol", [128, 2, KC])
        kT = sb("kT", [128, T])
        vtok_f = sb("vtok", [128, B * D])
        vtok = vtok_f[:, :].rearrange("p (b d) -> p b d", b=B)
        w1 = sb("w1", [128, FF])
        w2 = sb("w2", [128, FT, D])
        lst = sb("lst", [128, 2, BPC, 6])
        lmv = sb("lmv", [128, 2, BPC, 2])
        lve = sb("lve", [128, 2, BPC])
        lrs = sb("lrs", [128, 2, BPC])
        zz = sb("zz", [128, 4 * CH])
        ztok = zz[:, 0:2 * CH].rearrange("p (a b d) -> p a b d", a=2, b=BPC)
        zT = zz[:, 2 * CH:4 * CH].rearrange("p (a n) -> p a n", a=2)
        z3 = sb("z3", [128, CH])
        hB = hB_f[:, :].rearrange("p (a f n) -> p a f n", a=2, f=FT)
        att = a2_f[:, 0:10 * CH].rearrange("p (w a n) -> p w a n", w=5, a=2)
        qT, oT = att[:, 0], att[:, 1]
        bqs = sb("bqs", [128, 1])
        nmax = sb("nmax", [128, 2, BPC])
        nms = sb("nms", [128, 2, BPC])
        prob = att[:, 2].rearrange("p a (b k) -> p a b k", b=BPC)
        psum_ = sb("psum_", [128, 2, BPC])
        prec = sb("prec", [128, 2, BPC])
        pn = att[:, 3].rearrange("p a (b k) -> p a b k", b=BPC)
        pT = att[:, 4].rearrange("p a (b k) -> p a b k", b=BPC)
        xi = sb("xi", [128, T])
        r1 = sb("r1", [33, 2, CH])
        lg = sb("lg", [128, B, E])
        top = sb("top", [128, B, 8])
        tix = sb("tix", [128, B, 8], U32)
        tif = sb("tif", [128, B, 8])
        rt = sb("rt", [128, 5, B])
        swc = sb("swc", [128, 4])
        cf2 = sb("cf2", [128, 2, B])
        idxb = b1_f[:, 0:2 * T].rearrange("p (c a n) -> p c a n", c=NCH, a=2)
        m72 = sb("m72", [96, 2, T], BF)
        cb = hB_f[:, :].rearrange("p (c a n) -> p c a n", c=NCH, a=2)
        onesb = sb("onesb", [96, CH], BF)
        bparts = sb("bparts", [96, 2, 3 * D], BF)
        bhi = b1_f[0:96, 2 * T:2 * T + 9 * D].bitcast(BF).rearrange("p (q i n) -> p q i n", q=3, i=2)
        brem = b1_f[0:96, 2 * T + 9 * D:2 * T + 21 * D].rearrange("p (q i n) -> p q i n", q=2, i=2)
        iwh = sb("iwh", [128, 1])
        bh2h = sb("bh2h", [128, 1])
        vT = a1_f
        hid = a2_f[:, 0:HT * CH].rearrange("p (f n) -> p f n", f=HT)
        hs = kT[0:H, 3 * CH:4 * CH]
        hm = a2_f[:, HT * CH:3 * HT * CH].rearrange("p (a f n) -> p a f n", a=2, f=HT)
        ew = a2_f[:, 3 * HT * CH:4 * HT * CH].rearrange("p (f n) -> p f n", f=4)
        pw = xtok_f[:, 0:3 * CH].rearrange("p (f n) -> p f n", f=3)
        ab = vtok_f[:, 0:3 * CH].rearrange("p (f n) -> p f n", f=3)
        ta = ctxT[:, 0:0 + 3 * CH].rearrange("p (f n) -> p f n", f=3)
        tg = kT[:, 0:0 + 3 * CH].rearrange("p (f n) -> p f n", f=3)
        sm = b2_f[:, 0:3 * CH].rearrange("p (f n) -> p f n", f=3)
        xn = xtok_f[:, 3 * CH:4 * CH]
        fh = zz[:, 0:2 * CH].rearrange("p (f n) -> p f n", f=2)
        th = zz[:, 2 * CH:3 * CH]
        h1 = zz[0:32, 3 * CH:4 * CH]
        rr = ctxT[:, 3 * CH:4 * CH]
        res = xT

        def ck(c):
            return slice(c * CH, (c + 1) * CH)

        ident = A("ident")
        block = ctx.enter_context(nc.Block())

        def hid_bank(s, j):
            return bank[7 if j % 2 else (5 if s == 0 else 6)]

        def vk_bank(g):
            return bank[2 + g % 2][:, 0:VB * VK].rearrange("p (b n) -> p b n", b=VB)

        STEPS = ITER * NCH

        SLOTS = NCH + 2
        LN = {}
        for t in range(-1, SLOTS):
            for which, c in (("att", t - 1), ("ffn", t + 1), ("rt", t - 2)):
                if 0 <= c < NCH:
                    LN[which, c] = len(LN)

        half = KC // 2

        @block.sync
        def _(sp):
            for dst, src, name in ((pA[:, :], d_packA, "in_A"), (ctxT[:, :], d_ctxT, "in_ctx"),
                                   (xtok[:, :, :], d_xtok, "in_xtok"), (xT[:, :], d_xT, "in_x"),
                                   (a1[:, :, :], d_a1, "in_a1"),
                                   (b1[:, 0:half, :], d_b1[:, 0:half, :], "in_b1_0"),
                                   (b1[:, half:KC, :], d_b1[:, half:KC, :], "in_b1_1"),
                                   (b2[:, :, :], d_b2, "in_b2")):
                sp.dma_start(dst, src).then_inc(sem(name), 16)
            for f in range(FT):
                cols = slice(f * 128, (f + 1) * 128)
                sp.dma_start(a2[:, :, cols], d_a2[:, :, cols]).then_inc(sem(f"in_a2_{f}"), 16)
            sp.dma_start(pB[:, :], d_packB).then_inc(sem("in_B"), 16)
            for c in range(NCH):
                sp.wait_ge(sem("res"), c + 1)
                sp.dma_start(d_out[:, ck(c)], res[:, ck(c)]).then_inc(sem("out"), 16)
            sp.wait_ge(sem("out"), 16 * NCH)

        @block.gpsimd
        def _(pool):
            pool.memset(mhalf[:, :], -0.5).then_inc(sem("mhalf"), 1)
            pool.memset(ones[:, :], 1.0).then_inc(sem("ones"), 1)
            pool.memset(onesb[:, :], 1.0).then_inc(sem("onesb"), 1)
            pool.wait_ge(sem("onesb"), 1)
            pool.memset(r1[32:33, :, :], 1.0).then_inc(sem("r1one"), 1)
            pool.wait_ge(sem("r1one"), 1)
            pool.wait_ge(sem("mhalf"), 1)
            pool.wait_ge(sem("veps"), 1)
            pool.tensor_tensor(rstd[:, :], veps[:, :], mhalf[:, :], ALU.pow).then_inc(sem("rstd"), 1)
            for n in range(3 * NCH):
                pool.wait_ge(sem("lve"), n + 1)
                pool.tensor_tensor(lrs[:, n % 2, :], lve[:, n % 2, :], mhalf[:, 0:BPC], ALU.pow)\
                    .then_inc(sem("lrs"), 1)
            for s in range(STEPS):
                c = s % NCH
                pool.wait_ge(sem("e0"), s + 1)
                if s >= 1:
                    pool.wait_ge(sem("w"), 3 * s)
                for k in range(2):
                    pool.tensor_tensor(ew[:, 2 + k, :], ew[:, 0, :], cb[:, c, k, :], ALU.mult)\
                        .then_inc(sem("ew"), 1)
                if s >= NCH:
                    pool.wait_ge(sem("v1"), c + 1)
                    if s > NCH:
                        pool.wait_ge(sem("u"), 3 * (s - NCH))
                    for k in range(2):
                        pool.tensor_tensor(pw[:, 1 + k, :], vT[:, ck(c)], cb[:, c, k, :], ALU.mult)\
                            .then_inc(sem("pw"), 1)

        @block.scalar
        def _(act):
            act.wait_ge(sem("lgn"), 2)
            for i, n in enumerate(("log1", "log2")):
                act.activation(lg_e[:, i, :], A(n), ACT.Exp, bias=lg_n[:, i:i + 1],
                               accum_out=lg_n[:, 2 + i:3 + i]).then_inc(sem("lge"), 1)
            act.wait_ge(sem("cw_ps"), 1)
            act.activation(cw[:, :, :], bank[1][0:NF, 0:2 * D].rearrange("p (a d) -> p a d", a=2),
                           ACT.Copy).then_inc(sem("cw"), 1)
            for g in range(VG):
                b0, nb = g * VB, min(VB, B - g * VB)
                act.wait_ge(sem("v_ps"), g + 1)
                act.wait_ge(sem("k8"), g + 1)
                act.activation(vtok[:, b0:b0 + nb, :], vk_bank(g)[:, 0:nb, 0:D], ACT.Copy)\
                    .then_inc(sem("v"), 1)
            for c in range(NCH):
                act.wait_ge(sem("k_ps"), c + 1)
                act.activation(kT[:, ck(c)], bank[6 + c % 2][:, :], ACT.Identity, bias=A("bk"))\
                    .then_inc(sem("k"), 1)
            act.wait_ge(sem("negmax"), 1)
            act.activation(ecor[:, 0, :], cor[:, 0, :], ACT.Exp, bias=red[:, 6:7]).then_inc(sem("ecor"), 1)
            act.wait_ge(sem("w1_ps"), 1)
            act.activation(w1[:, :], bank[6][:, :], ACT.Copy).then_inc(sem("w1"), 1)
            act.wait_ge(sem("y_ps"), 1)
            act.activation(yb[:, :], bank[4][:, 0:128], ACT.Identity, bias=A("bout")).then_inc(sem("yb"), 1)
            def ln_evac(which, c, dst):
                act.wait_ge(sem("zt_ps"), LN[which, c] + 1)
                act.activation(dst, bank[6][:, :], ACT.Copy).then_inc(sem("z"), 1)

            def z_ffn(c):
                if c >= 2:
                    act.wait_ge(sem("fh_ps"), FT * (c - 1))
                ln_evac("ffn", c, zT[:, c % 2, :])

            def z_att(c):
                if c >= 1:
                    act.wait_ge(sem("q_ps"), c)
                ln_evac("att", c, z3[:, :])

            def gelus(c, tiles):
                for f in tiles:
                    act.wait_ge(sem("fh_ps"), FT * c + f + 1)
                    if c >= 2:
                        act.wait_ge(sem("fo_ps"), c - 1)
                    act.activation(hB[:, c % 2, f, :], bank[2 + f % 2][:, :], ACT.Gelu_apprx_tanh)\
                        .then_inc(sem("fh"), 1)

            def q_evac(c):
                act.wait_ge(sem("q_ps"), c + 1)
                if c == 0:
                    act.wait_ge(sem("bqs"), 1)
                if c >= 2:
                    act.wait_ge(sem("s_ps"), c - 1)
                act.activation(qT[:, c % 2, :], bank[5][:, :], ACT.Identity, bias=bqs[:, 0:1], scale=SCALE)\
                    .then_inc(sem("q"), 1)

            def exps(c):
                act.wait_ge(sem("nmax"), c + 1)
                if c >= 2:
                    act.wait_ge(sem("pn"), c - 1)
                for j in range(BPC):
                    act.activation(prob[:, c % 2, j, :], bank[7][:, j * S:(j + 1) * S], ACT.Exp,
                                   bias=nmax[:, c % 2, j:j + 1], accum_out=psum_[:, c % 2, j:j + 1])\
                        .then_inc(sem("prob"), 1)

            def o_evac(c):
                act.wait_ge(sem("o_ps"), c + 1)
                if c >= 2:
                    act.wait_ge(sem("x3_ps"), c - 1)
                act.activation(oT[:, c % 2, :], bank[7][:, :], ACT.Identity, bias=W("bv"))\
                    .then_inc(sem("o"), 1)

            def r1_gelu(c):
                act.wait_ge(sem("r1_ps"), c + 1)
                if c >= 2:
                    act.wait_ge(sem("lg_ps"), c - 1)
                act.activation(r1[0:32, c % 2, :], bank[4][0:32, :], ACT.Gelu, bias=W("br1"))\
                    .then_inc(sem("r1"), 1)

            def second_exp(c):
                act.wait_ge(sem("dl"), c + 1)
                t = slice(c * BPC, (c + 1) * BPC)
                act.activation(rt[:, 1, t], rt[:, 0, t], ACT.Exp).then_inc(sem("de"), 1)

            def expand_evac(c, ba, bb):
                for k in range(2):
                    act.wait_ge(sem("idx_ps"), 2 * c + k + 1)
                    act.activation(idxb[:, c, k, :], bank[(ba, bb)[k]][:, :], ACT.Copy)\
                        .then_inc(sem("idx"), 1)

            def hidden_gelus(s):
                for j in range(HT):
                    act.wait_ge(sem("hid_ps"), 5 * s + j + 1)
                    if s >= 1:
                        act.wait_ge(sem("hm"), 8 * (s - 1) + 2 * j + 2)
                    act.activation(hid[:, j, :], hid_bank(s, j)[:, :], ACT.Gelu,
                                   bias=W("eb1", j, j + 1)).then_inc(sem("hid"), 1)
                act.wait_ge(sem("hid_ps"), 5 * s + 5)
                if s >= 1:
                    act.wait_ge(sem("g_ps"), 3 * (s - 1) + 1)
                act.activation(hs, hid_bank(s, 0)[0:H, :], ACT.Gelu, bias=W("bs1")).then_inc(sem("hs"), 1)

            z_ffn(0)
            gelus(0, (0, 1))
            act.wait_ge(sem("w2_ps"), 1)
            act.activation(w2[:, :, :], bank[7][:, :].rearrange("p (a d) -> p a d", a=FT), ACT.Copy)\
                .then_inc(sem("w2"), 1)
            gelus(0, (2, 3))
            act.wait_ge(sem("in_B"), 16)
            act.activation(swc[:, 0:1], W("sw"), ACT.Exp, scale=-1.0).then_inc(sem("swe"), 1)
            for t in range(SLOTS):
                f, a, q, x = (0 <= t - i < NCH for i in range(4))
                if x and not f:
                    expand_evac(t - 3, 2, 3)
                if f and t:
                    gelus(t, (0, 1))
                if q:
                    o_evac(t - 2)
                if a:
                    z_att(t - 1)
                if f and t:
                    gelus(t, (2,))
                if a:
                    q_evac(t - 1)
                if f and t:
                    gelus(t, (3,))
                if t + 1 < NCH:
                    z_ffn(t + 1)
                if a:
                    exps(t - 1)
                if x:
                    second_exp(t - 3)
                if x and f:
                    expand_evac(t - 3, 2, 3)
                if t == SLOTS - 1:
                    hidden_gelus(0)
                if q:
                    ln_evac("rt", t - 2, xi[:, ck(t - 2)])
                    r1_gelu(t - 2)
            second_exp(NCH - 1)

            def refine1(s):
                for j in range(2):
                    act.wait_ge(sem("f1_ps"), 2 * s + j + 1)
                    if s >= 1:
                        act.wait_ge(sem("f2_ps"), s)
                    act.activation(fh[:, j, :], bank[6 + (j + 1) % 2][:, :], ACT.Gelu,
                                   bias=W("bf1", j, j + 1)).then_inc(sem("fhg"), 1)
                act.wait_ge(sem("h1_ps"), s + 1)
                if s >= 1:
                    act.wait_ge(sem("h2_ps"), s)
                act.activation(h1, bank[7][0:32, :], ACT.Gelu, bias=W("bh1")).then_inc(sem("h1"), 1)

            def refine2(s):
                act.wait_ge(sem("h2_ps"), s + 1)
                if s >= 1:
                    act.wait_ge(sem("rr"), 2 * s)
                act.activation(th, bank[7][:, :], ACT.Tanh, bias=bh2h[:, 0:1], scale=0.5)\
                    .then_inc(sem("th"), 1)

            for s in range(STEPS + 1):
                it2 = s >= NCH
                if s < STEPS:
                    if s >= 1:
                        hidden_gelus(s)
                if s == 0:
                    expand_evac(NCH - 1, 0, 1)
                else:
                    refine1(s - 1)
                    refine2(s - 1)
                if s == STEPS:
                    break
                for k in range(3):
                    if s >= 1:
                        act.wait_ge(sem("sp"), 3 * (s - 1) + k + 1)
                    act.wait_ge(sem("b_ps"), 3 * s + k + 1)
                    act.activation(ab[:, k, :], bank[3 + k][:, :], ACT.Abs).then_inc(sem("ab"), 1)
                act.wait_ge(sem("ab"), 3 * s + 3)
                act.activation(ab[:, :, :], ab[:, :, :], ACT.Exp, scale=-1.0).then_inc(sem("ex"), 1)
                act.wait_ge(sem("ex"), s + 1)
                act.activation(ab[:, :, :], ab[:, :, :], ACT.Ln, bias=1.0).then_inc(sem("ln"), 1)
                for k in range(3):
                    r = 0
                    if it2:
                        q = s - NCH
                        act.wait_ge(sem("a_ps"), 3 * q + k + 1)
                        if q >= 1:
                            act.wait_ge(sem("y"), 3 * s)
                        act.activation(ta[:, k, :], bank[(2 * k) % 3][:, :], ACT.Tanh, scale=0.5)\
                            .then_inc(sem("ta"), 1)
                    act.wait_ge(sem("g_ps"), 3 * s + k + 1)
                    if s >= 1:
                        act.wait_ge(sem("xn"), s)
                    act.activation(tg[:, k, :], bank[(2 * k + 1) % 3][:, :], ACT.Tanh, scale=0.5)\
                        .then_inc(sem("tg"), 1)

        @block.vector
        def _(dve):
            chain = [0]

            def link(ins):
                chain[0] += 1
                ins.then_inc(sem("dve_chain"), 1)
                dve.wait_ge(sem("dve_chain"), chain[0])

            dve.wait_ge(sem("in_A"), 16)
            for i, n in enumerate(("log1", "log2")):
                dve.tensor_reduce(lg_n[:, i:i + 1], A(n), AX.X, ALU.max, negate=True)\
                    .then_inc(sem("lgn"), 1)
            for g in range(VG):
                b0, nb = g * VB, min(VB, B - g * VB)
                dve.wait_ge(sem("v_ps"), g + 1)
                dve.tensor_tensor(qk[:, 1, b0 * DH:(b0 + nb) * DH].rearrange("p (b c) -> p b c", c=DH),
                                  vk_bank(g)[:, 0:nb, D:VK],
                                  A("bq8").unsqueeze(1).to_broadcast([128, nb, DH]), ALU.add)\
                    .then_inc(sem("k8"), 1)
            dve.wait_ge(sem("in_xtok"), 16)
            for b in range(B):
                dve.bn_stats(st[:, b, :], xtok[:, b, :]).then_inc(sem("st"), 1)
            for b in range(B):
                dve.wait_ge(sem("st"), b + 1)
                dve.bn_aggr(mv[:, b, :], st[:, b, :]).then_inc(sem("mv"), 1)
            dve.wait_ge(sem("mv"), B)
            dve.tensor_scalar(veps[:, :], mv[:, :, 1], EPS, None, ALU.add).then_inc(sem("veps"), 1)
            dve.wait_ge(sem("lge"), 2)
            link(dve.reciprocal(lg_n[:, 4:6], lg_n[:, 2:4]))
            for i in range(2):
                for half in range(2):
                    p = slice(64 * half, 64 * half + 64)
                    dve.tensor_scalar(wcol[p, i, :], lg_e[p, i, half:PRIM:2], lg_n[p, 4 + i:5 + i], None,
                                      ALU.mult).then_inc(sem("wcol"), 1)
            dve.wait_ge(sem("q8_ps"), 1)
            qps = bank[0][:, 0:128].rearrange("p (b c) -> p b c", c=DH)
            colsum = bank[0][:, 256:264].unsqueeze(1).to_broadcast([128, B, DH])
            mean = mv[:, :, 0:1].to_broadcast([128, B, DH])
            bq_b = A("bq8").unsqueeze(1).to_broadcast([128, B, DH])
            link(dve.tensor_tensor(qt[:, 0], colsum, mean, ALU.mult))
            link(dve.tensor_tensor(qt[:, 1], qps, qt[:, 0], ALU.subtract))
            dve.wait_ge(sem("rstd"), 1)
            link(dve.tensor_tensor(qt[:, 2], qt[:, 1], rstd[:, :].unsqueeze(2).to_broadcast([128, B, DH]),
                                   ALU.mult))
            dve.tensor_tensor(qk[:, 0, :].rearrange("p (b c) -> p b c", c=DH), qt[:, 2], bq_b, ALU.add)\
                .then_inc(sem("q8"), 1)
            dve.wait_ge(sem("dft_ps"), 1)
            link(dve.tensor_copy(fr[:, :, :, :],
                                 bank[4][0:NF, :].rearrange("p (a b n) -> p a b n", a=2, b=2)))
            for n, (i, j) in enumerate(((0, 0), (1, 1), (0, 1), (1, 0))):
                last = dve.tensor_tensor_reduce(out=junk[:, n, :], in0=fr[:, i, 0, :], in1=fr[:, j, 1, :],
                                                scale=1.0, scalar=0.0, op0=ALU.mult, op1=ALU.add,
                                                accum_out=red[:, n:n + 1])
                last.then_inc(sem("spec"), 1)
            dve.wait_ge(sem("spec"), 4)
            dve.tensor_scalar(red[:, 4:5], red[:, 0:1], red[:, 1:2], A("a1"), ALU.add, ALU.mult)\
                .then_inc(sem("spec"), 1)
            dve.tensor_scalar(red[:, 5:6], red[:, 3:4], red[:, 2:3], A("a1"), ALU.subtract, ALU.mult)\
                .then_inc(sem("spec"), 1)
            dve.wait_ge(sem("ones"), 1)
            dve.wait_ge(sem("spec"), 6)
            for n in range(2):
                dve.tensor_scalar(reB[:, n, :], ones[0:NF, 0:NF], red[:, 4 + n:5 + n], None, ALU.mult)\
                    .then_inc(sem("reB"), 1)
            dve.wait_ge(sem("wcol"), 4)
            dve.wait_ge(sem("in_a1"), 16)
            dve.tensor_tensor(a1[:, :, :], a1[:, :, :], wcol[:, 0, :].unsqueeze(2).to_broadcast([128, KC, D]),
                              ALU.mult).then_inc(sem("a1s"), 1)
            dve.wait_ge(sem("cor_ps"), 1)
            link(dve.tensor_copy(cor[:, 0, :], bank[5][0:NF, 0:128]))
            link(dve.max(m8[:, 0, :], cor[:, 0, :]))
            dve.tensor_scalar(red[:, 6:7], m8[:, 0, 0:1], -1.0, None, ALU.mult).then_inc(sem("negmax"), 1)
            link(dve.match_replace(cor[:, 1, :], m8[:, 0, :], cor[:, 0, :], NEG))
            link(dve.max(m8[:, 1, :], cor[:, 1, :]))
            link(dve.memset(m8[:, 2, :], NEG))
            link(dve.tensor_copy(m8[:, 2, 0:TOPK - 8], m8[:, 1, 0:TOPK - 8]))
            link(dve.match_replace(cor[:, 2, :], m8[:, 2, :], cor[:, 1, :], NEG))
            link(dve.tensor_scalar(junk[:, 4, :], cor[:, 2, :], NEG, None, ALU.is_equal))
            dve.wait_ge(sem("ecor"), 1)
            link(dve.tensor_tensor_reduce(out=ecor[:, 1, :], in0=ecor[:, 0, :], in1=junk[:, 4, :],
                                          scale=1.0, scalar=0.0, op0=ALU.mult, op1=ALU.add,
                                          accum_out=red[:, 7:8]))
            dve.reciprocal(red[:, 8:9], red[:, 7:8]).then_inc(sem("wspec"), 1)
            for n, name in enumerate(("cf", "sf")):
                dve.tensor_tensor_reduce(out=junk[:, n, :], in0=ecor[:, 1, :], in1=A(name),
                                         scale=1.0, scalar=0.0, op0=ALU.mult, op1=ALU.add,
                                         accum_out=red[:, 9 + n:10 + n]).then_inc(sem("wspec"), 1)
            dve.wait_ge(sem("wspec"), 3)
            link(dve.tensor_scalar(red[:, 0:2], red[:, 9:11], red[:, 8:9], A("a2"), ALU.mult, ALU.mult))
            wc, ws = red[:, 0:1], red[:, 1:2]
            vc, vs = fr[:, 0, 1, :], fr[:, 1, 1, :]
            dve.tensor_scalar(ab_f[:, 0, :], vs, ws, None, ALU.mult).then_inc(sem("spc"), 1)
            dve.tensor_scalar(ab_f[:, 1, :], vc, ws, None, ALU.mult).then_inc(sem("spc"), 1)
            dve.wait_ge(sem("spc"), 2)
            dve.scalar_tensor_tensor(ab_f[:, 2, :], vc, wc, ab_f[:, 0, :], ALU.mult, ALU.add)\
                .then_inc(sem("abf"), 1)
            dve.scalar_tensor_tensor(ab_f[:, 3, :], vs, wc, ab_f[:, 1, :], ALU.mult, ALU.subtract)\
                .then_inc(sem("abf"), 1)
            dve.wait_ge(sem("in_b2"), 16)
            dve.tensor_tensor(b2[:, :, :], b2[:, :, :], wcol[:, 1, :].unsqueeze(2).to_broadcast([128, KC, D]),
                              ALU.mult).then_inc(sem("b2s"), 1)
            dve.wait_ge(sem("yb"), 1)
            dve.wait_ge(sem("in_x"), 16)
            for c in range(NCH):
                xv = xT[:, ck(c)].rearrange("p (b h c) -> p b h c", b=BPC, h=HEADS)
                yv = yb[:, c * BPC * DH:(c + 1) * BPC * DH].rearrange("p (b c) -> p b c", b=BPC)\
                    .unsqueeze(2).to_broadcast([128, BPC, HEADS, DH])
                dve.tensor_tensor(xv, xv, yv, ALU.add).then_inc(sem("x1"), 1)

            def ln_stats(which, c):
                n = LN[which, c]
                t = bank[n % 2]
                dve.wait_ge(sem("tok_ps"), n + 1)
                for j in range(BPC):
                    dve.bn_stats(lst[:, n % 2, j, :], t[:, j * D:(j + 1) * D]).then_inc(sem("lst"), 1)
                for j in range(BPC):
                    dve.wait_ge(sem("lst"), BPC * n + j + 1)
                    dve.bn_aggr(lmv[:, n % 2, j, :], lst[:, n % 2, j, :]).then_inc(sem("lmv"), 1)
                dve.wait_ge(sem("lmv"), BPC * (n + 1))
                dve.tensor_scalar(lve[:, n % 2, :], lmv[:, n % 2, :, 1], EPS, None, ALU.add)\
                    .then_inc(sem("lve"), 1)

            def ln_scale(which, c):
                n = LN[which, c]
                t = bank[n % 2]
                dve.wait_ge(sem("lrs"), n + 1)
                if n >= 2:
                    dve.wait_ge(sem("zt_ps"), n - 1)
                for j in range(BPC):
                    dve.tensor_scalar(ztok[:, n % 2, j, :], t[:, j * D:(j + 1) * D], lmv[:, n % 2, j, 0:1],
                                      lrs[:, n % 2, j:j + 1], ALU.subtract, ALU.mult)\
                        .then_inc(sem("ztok"), 1)

            def ffn_add(c):
                dve.wait_ge(sem("fo_ps"), c + 1)
                dve.tensor_tensor(xT[:, ck(c)], bank[4][:, :], xT[:, ck(c)], ALU.add)\
                    .then_inc(sem("x2"), 1)

            def att_max(c):
                dve.wait_ge(sem("s_ps"), c + 1)
                dve.tensor_reduce(nmax[:, c % 2, :], bank[7][:, :].rearrange("p (b k) -> p b k", b=BPC),
                                  AX.X, ALU.max, negate=True).then_inc(sem("nmax"), 1)

            def att_norm(c):
                dve.wait_ge(sem("prob"), BPC * (c + 1))
                link(dve.reciprocal(prec[:, c % 2, :], psum_[:, c % 2, :]))
                if c >= 2:
                    dve.wait_ge(sem("pt_ps"), c - 1)
                dve.tensor_tensor(pn[:, c % 2], prob[:, c % 2],
                                  prec[:, c % 2, :].unsqueeze(2).to_broadcast([128, BPC, S]), ALU.mult)\
                    .then_inc(sem("pn"), 1)

            def att_pt(c):
                dve.wait_ge(sem("pt_ps"), c + 1)
                if c >= 2:
                    dve.wait_ge(sem("o_ps"), c - 1)
                dve.tensor_copy(pT[:, c % 2], bank[5][:, :].rearrange("p (b k) -> p b k", b=BPC))\
                    .then_inc(sem("pT"), 1)

            def att_add(c):
                dve.wait_ge(sem("x3_ps"), c + 1)
                dve.scalar_tensor_tensor(xT[:, ck(c)], bank[5][:, :], W("bo"), xT[:, ck(c)],
                                         ALU.add, ALU.add).then_inc(sem("x3"), 1)

            def route(c):
                t = slice(c * BPC, (c + 1) * BPC)
                dve.wait_ge(sem("lg_ps"), c + 1)
                dve.tensor_copy(lg[:, t, :], bank[4][:, 0:BPC * E].rearrange("p (b e) -> p b e", b=BPC))\
                    .then_inc(sem("lg"), 1)
                dve.wait_ge(sem("lg"), c + 1)
                for b in range(c * BPC, (c + 1) * BPC):
                    dve.max(top[:, b, :], lg[:, b, :]).then_inc(sem("top"), 1)
                for b in range(c * BPC, (c + 1) * BPC):
                    dve.wait_ge(sem("top"), b + 1)
                    dve.max_index(tix[:, b, :], top[:, b, :], lg[:, b, :]).then_inc(sem("tix"), 1)
                dve.tensor_tensor(rt[:, 0, t], top[:, t, 1], top[:, t, 0], ALU.subtract).then_inc(sem("dl"), 1)
                dve.wait_ge(sem("tix"), (c + 1) * BPC)
                dve.tensor_copy(tif[:, t, :], tix[:, t, :]).then_inc(sem("tif"), 1)

            def weigh(c):
                t = slice(c * BPC, (c + 1) * BPC)
                dve.wait_ge(sem("de"), c + 1)
                link(dve.tensor_scalar(rt[:, 2, t], rt[:, 1, t], 1.0, None, ALU.add))
                link(dve.reciprocal(rt[:, 3, t], rt[:, 2, t]))
                link(dve.tensor_tensor(rt[:, 4, t], rt[:, 1, t], rt[:, 3, t], ALU.mult))
                for k in range(2):
                    dve.tensor_scalar(cf2[:, k, t], rt[:, 3 + k, t], swc[:, 3:4], None, ALU.mult)\
                        .then_inc(sem("cf2"), 1)

            def slot_masks(c):
                for k in range(2):
                    dve.wait_ge(sem("idx"), 2 * c + k + 1)
                    dve.tensor_scalar(m72[:, k, ck(c)], idxb[0:96, c, k, :], W("bias_expert"), None,
                                      ALU.is_equal).then_inc(sem("m72"), 1)

            def slot_weights(c, ba, bb):
                for k in range(2):
                    dve.wait_ge(sem("c_ps"), 2 * c + k + 1)
                    dve.tensor_copy(cb[:, c, k, :], bank[(ba, bb)[k]][:, :]).then_inc(sem("cb"), 1)

            def hidden_masked(s):
                c = s % NCH
                dve.wait_ge(sem("idx"), 2 * (c + 1))
                for j in range(HT):
                    dve.wait_ge(sem("hid"), HT * s + j + 1)
                    if s >= 1 and j == 0:
                        dve.wait_ge(sem("g_ps"), 3 * s)
                    for k in range(2):
                        dve.scalar_tensor_tensor(hm[:, k, j, :], idxb[:, c, k, :], W("tile_expert", j, j + 1),
                                                 hid[:, j, :], ALU.is_equal, ALU.mult)\
                            .then_inc(sem("hm"), 1)

            ln_stats("ffn", 0)
            ln_scale("ffn", 0)
            def consts():
                dve.wait_ge(sem("in_B"), 16)
                dve.tensor_scalar(bqs[:, :], W("bq"), SCALE, None, ALU.mult).then_inc(sem("bqs"), 1)
                dve.tensor_scalar(iwh[:, :], W("iw"), 0.5, None, ALU.mult).then_inc(sem("consts"), 1)
                dve.tensor_scalar(bh2h[:, :], W("bh2"), 0.5, None, ALU.mult).then_inc(sem("consts"), 1)

            def shared_share():
                dve.wait_ge(sem("swe"), 1)
                link(dve.tensor_scalar(swc[:, 1:2], swc[:, 0:1], 1.0, None, ALU.add))
                link(dve.reciprocal(swc[:, 2:3], swc[:, 1:2]))
                link(dve.tensor_scalar(swc[:, 3:4], swc[:, 2:3], -1.0, 1.0, ALU.mult, ALU.add))

            def bias_parts():
                for i, n in enumerate(("eb2", "bs2")):
                    link(dve.tensor_copy(bhi[:, 0, i, :], W(n)))
                    link(dve.tensor_tensor(brem[:, 0, i, :], W(n), bhi[:, 0, i, :], ALU.subtract))
                    link(dve.tensor_copy(bhi[:, 1, i, :], brem[:, 0, i, :]))
                    link(dve.tensor_tensor(brem[:, 1, i, :], brem[:, 0, i, :], bhi[:, 1, i, :], ALU.subtract))
                    link(dve.tensor_copy(bhi[:, 2, i, :], brem[:, 1, i, :]))
                    for q in range(3):
                        p = slice(32 * q, 32 * q + 32)
                        dve.tensor_copy(bparts[p, i, :], bhi[p, q, i, :]).then_inc(sem("bparts"), 1)

            consts()
            bias_parts()
            for t in range(SLOTS):
                f, a, q, x = (0 <= t - i < NCH for i in range(4))
                if q:
                    att_pt(t - 2)
                if a:
                    ln_stats("att", t - 1)
                    ln_scale("att", t - 1)
                if t + 1 < NCH:
                    ln_stats("ffn", t + 1)
                    ln_scale("ffn", t + 1)
                if x and not f:
                    slot_masks(t - 3)
                if q:
                    att_add(t - 2)
                    ln_stats("rt", t - 2)
                if a:
                    att_max(t - 1)
                if q:
                    ln_scale("rt", t - 2)
                if a:
                    att_norm(t - 1)
                if x and f:
                    slot_masks(t - 3)
                if x:
                    weigh(t - 3)
                if f:
                    ffn_add(t)
                if t == 0:
                    shared_share()
                if t == SLOTS - 1:
                    hidden_masked(0)
                if x:
                    slot_weights(t - 3, 2, 3)
                if q:
                    route(t - 2)
            weigh(NCH - 1)
            slot_masks(NCH - 1)
            slot_weights(NCH - 1, 0, 1)
            dve.wait_ge(sem("consts"), 2)

            def refine(s):
                c = s % NCH
                dve.wait_ge(sem("f2_ps"), s + 1)
                dve.tensor_scalar(rr, bank[6][:, :], W("bf2"), iwh[:, 0:1], ALU.add, ALU.mult)\
                    .then_inc(sem("rr"), 1)
                dve.wait_ge(sem("rr"), 2 * s + 1)
                dve.wait_ge(sem("th"), s + 1)
                dve.scalar_tensor_tensor(rr, th, 1.0, rr, ALU.add, ALU.mult)\
                    .then_inc(sem("rr"), 1)
                dve.wait_ge(sem("rr"), 2 * s + 2)
                dve.tensor_tensor(xi[:, ck(c)], xi[:, ck(c)], rr, ALU.add).then_inc(sem("xi"), 1)
                if s >= NCH:
                    dve.wait_ge(sem("xi"), s + 1)
                    dve.tensor_tensor(res[:, ck(c)], xi[:, ck(c)], xT[:, ck(c)], ALU.add)\
                        .then_inc(sem("res"), 1)

            for s in range(STEPS):
                c = s % NCH
                it2 = s >= NCH
                if s >= 1:
                    dve.wait_ge(sem("ew"), 2 * s)
                dve.tensor_scalar(ew[:, 0, :], xi[:, ck(c)], W("mu"), None, ALU.subtract).then_inc(sem("e0"), 1)
                if it2:
                    dve.tensor_scalar(pw[:, 0, :], vT[:, ck(c)], swc[:, 2:3], None, ALU.mult)\
                        .then_inc(sem("pw0"), 1)
                dve.wait_ge(sem("e0"), s + 1)
                dve.tensor_scalar(ew[:, 1, :], ew[:, 0, :], swc[:, 2:3], None, ALU.mult).then_inc(sem("e1"), 1)
                if s >= 1:
                    hidden_masked(s)
                if s >= 1:
                    refine(s - 1)
                dve.wait_ge(sem("ln"), s + 1)
                for k in range(3):
                    dve.scalar_tensor_tensor(sm[:, k, :], bank[3 + k][:, :], 0.0, ab[:, k, :],
                                             ALU.max, ALU.add).then_inc(sem("sp"), 1)
                dve.wait_ge(sem("e1"), s + 1)
                dve.wait_ge(sem("ew"), 2 * s + 2)
                for k in range(3):
                    dve.wait_ge(sem("sp"), 3 * s + k + 1)
                    dve.tensor_tensor(sm[:, k, :], sm[:, k, :], ew[:, 1 + k, :], ALU.mult)\
                        .then_inc(sem("w"), 1)
                dve.wait_ge(sem("w"), 3 * s + 3)
                if it2:
                    q = s - NCH
                    dve.wait_ge(sem("pw0"), q + 1)
                    dve.wait_ge(sem("pw"), 2 * q + 2)
                    for k in range(3):
                        dve.wait_ge(sem("ta"), 3 * q + k + 1)
                        dve.scalar_tensor_tensor(ta[:, k, :], ta[:, k, :], 1.0, pw[:, k, :],
                                                 ALU.add, ALU.mult).then_inc(sem("u"), 1)
                        dve.wait_ge(sem("u"), 3 * q + k + 1)
                        dve.scalar_tensor_tensor(ta[:, k, :], ta[:, k, :], 0.5, sm[:, k, :],
                                                 ALU.mult, ALU.subtract).then_inc(sem("vv"), 1)
                        dve.wait_ge(sem("tg"), 3 * s + k + 1)
                        dve.wait_ge(sem("vv"), 3 * q + k + 1)
                        dve.scalar_tensor_tensor(tg[:, k, :], tg[:, k, :], 1.0, ta[:, k, :],
                                                 ALU.add, ALU.mult).then_inc(sem("y"), 1)
                else:
                    for k in range(3):
                        dve.wait_ge(sem("tg"), 3 * s + k + 1)
                        dve.scalar_tensor_tensor(tg[:, k, :], tg[:, k, :], 1.0, sm[:, k, :],
                                                 ALU.add, ALU.mult).then_inc(sem("y"), 1)
                    dve.wait_ge(sem("y"), 3 * s + 3)
                    link(dve.tensor_tensor(sm[:, 0, :], sm[:, 0, :], sm[:, 1, :], ALU.add))
                    dve.scalar_tensor_tensor(vT[:, ck(c)], sm[:, 0, :], -1.0, sm[:, 2, :],
                                             ALU.mult, ALU.subtract).then_inc(sem("v1"), 1)
                dve.wait_ge(sem("y"), 3 * s + 3)
                link(dve.tensor_tensor(tg[:, 0, :], tg[:, 0, :], tg[:, 1, :], ALU.add))
                link(dve.tensor_tensor(tg[:, 0, :], tg[:, 0, :], tg[:, 2, :], ALU.add))
                if s >= 1:
                    dve.wait_ge(sem("h1_ps"), s)
                dve.scalar_tensor_tensor(xn, tg[:, 0, :], 0.05 if it2 else -0.05, xi[:, ck(c)],
                                         ALU.mult, ALU.add).then_inc(sem("xn"), 1)
            refine(STEPS - 1)

        @block.tensor
        def _(pe):
            def mm(out, lhsT, rhs, start=True, stop=True):
                return pe.matmul(out, lhsT, rhs, start=start, stop=stop)

            pe.wait_ge(sem("ones"), 1)
            pe.wait_ge(sem("in_A"), 16)
            mm(bank[1][0:NF, 0:D], A("cl"), A("wout"))
            mm(bank[1][0:NF, D:2 * D], A("sl"), A("wout")).then_inc(sem("cw_ps"), 1)
            mm(bank[0][:, 256:264], ones[:, :], A("wq8"))
            pe.wait_ge(sem("in_ctx"), 16)
            for g in range(VG):
                if g >= 2:
                    pe.wait_ge(sem("v"), g - 1)
                    pe.wait_ge(sem("k8"), g - 1)
                for j in range(min(VB, B - g * VB)):
                    b = g * VB + j
                    last = mm(vk_bank(g)[:, j, :], ctxT[:, b * S:(b + 1) * S],
                              pA[:, colA["wv"][1]:colA["wv"][1] + VK])
                last.then_inc(sem("v_ps"), 1)
            for c in range(NCH):
                if c >= 2:
                    pe.wait_ge(sem("k"), c - 1)
                mm(bank[6 + c % 2][:, :], A("wk"), ctxT[:, ck(c)]).then_inc(sem("k_ps"), 1)
            pe.wait_ge(sem("in_x"), 16)
            for b in range(B):
                last = mm(bank[0][:, b * DH:(b + 1) * DH], xT[:, b * S:(b + 1) * S], A("wq8"))
            last.then_inc(sem("q8_ps"), 1)
            pe.wait_ge(sem("k8"), VG)
            pe.wait_ge(sem("q8"), 1)
            mm(bank[4][0:NF, 0:256], A("cl"), qk[:, :, :])
            mm(bank[4][0:NF, 256:512], A("sl"), qk[:, :, :]).then_inc(sem("dft_ps"), 1)
            pe.wait_ge(sem("reB"), 2)
            mm(bank[5][0:NF, 0:128], reB[:, 0, :], A("cf"), stop=False)
            mm(bank[5][0:NF, 0:128], reB[:, 1, :], A("sf"), start=False).then_inc(sem("cor_ps"), 1)
            pe.wait_ge(sem("a1s"), 1)
            pe.wait_ge(sem("k"), NCH)
            for k in range(KC):
                if k % half == 0:
                    pe.wait_ge(sem(f"in_b1_{k // half}"), 16)
                last = mm(bank[6][:, :], a1[:, k, :], b1[:, k, :], start=k == 0, stop=k == KC - 1)
            last.then_inc(sem("w1_ps"), 1)
            pe.wait_ge(sem("abf"), 2)
            pe.wait_ge(sem("cw"), 1)
            mm(bank[4][:, 0:128], cw[:, 0, :], ab_f[:, 2, :], stop=False)
            mm(bank[4][:, 0:128], cw[:, 1, :], ab_f[:, 3, :], start=False).then_inc(sem("y_ps"), 1)

            def compose_w2(f):
                pe.wait_ge(sem(f"in_a2_{f}"), 16)
                for k in range(KC):
                    last = mm(bank[7][:, f * D:(f + 1) * D], a2[:, k, f * 128:(f + 1) * 128], b2[:, k, :],
                              start=k == 0, stop=k == KC - 1)
                if f == FT - 1:
                    last.then_inc(sem("w2_ps"), 1)

            def ln_tok(which, c, ready):
                n = LN[which, c]
                pe.wait_ge(sem(ready), c + 1)
                if n >= 2:
                    pe.wait_ge(sem("ztok"), BPC * (n - 1))
                for j in range(BPC):
                    t = c * BPC + j
                    last = pe.transpose(bank[n % 2][:, j * 128:(j + 1) * 128], xT[:, t * 128:(t + 1) * 128],
                                        ident)
                last.then_inc(sem("tok_ps"), 1)

            def ln_zt(which, c):
                n = LN[which, c]
                pe.wait_ge(sem("ztok"), BPC * (n + 1))
                if n == 0:
                    pe.wait_ge(sem("w1"), 1)
                else:
                    pe.wait_ge(sem("z"), n)
                for j in range(BPC):
                    last = pe.transpose(bank[6][:, j * 128:(j + 1) * 128], ztok[:, n % 2, j, :], ident)
                last.then_inc(sem("zt_ps"), 1)

            def ffn_up(c, tiles):
                pe.wait_ge(sem("z"), LN["ffn", c] + 1)
                for f in tiles:
                    n = FT * c + f
                    if n >= 2:
                        pe.wait_ge(sem("fh"), n - 1)
                    mm(bank[2 + f % 2][:, :], w1[:, f * 128:(f + 1) * 128], zT[:, c % 2, :])\
                        .then_inc(sem("fh_ps"), 1)

            def ffn_down(c):
                if c >= 1:
                    pe.wait_ge(sem("x2"), c)
                if c >= 3:
                    pe.wait_ge(sem("lg"), c - 2)
                for f in range(FT):
                    pe.wait_ge(sem("fh"), FT * c + f + 1)
                    last = mm(bank[4][:, :], w2[:, f, :], hB[:, c % 2, f, :],
                              start=f == 0, stop=f == FT - 1)
                last.then_inc(sem("fo_ps"), 1)

            def q_proj(c):
                pe.wait_ge(sem("z"), LN["att", c] + 1)
                if c >= 1:
                    pe.wait_ge(sem("x3"), c)
                mm(bank[5][:, :], W("wq"), z3[:, :]).then_inc(sem("q_ps"), 1)

            def scores(c):
                pe.wait_ge(sem("q"), c + 1)
                if c >= 1:
                    pe.wait_ge(sem("o"), c)
                for j in range(BPC):
                    b = c * BPC + j
                    last = mm(bank[7][:, j * S:(j + 1) * S], qT[:, c % 2, j * S:(j + 1) * S],
                              kT[:, b * S:(b + 1) * S])
                last.then_inc(sem("s_ps"), 1)

            def probs_t(c):
                pe.wait_ge(sem("pn"), c + 1)
                for j in range(BPC):
                    last = pe.transpose(bank[5][:, j * S:(j + 1) * S], pn[:, c % 2, j, :], ident)
                last.then_inc(sem("pt_ps"), 1)

            def att_v(c):
                pe.wait_ge(sem("pT"), c + 1)
                for j in range(BPC):
                    b = c * BPC + j
                    last = mm(bank[7][:, j * S:(j + 1) * S], vtok[:, b, :], pT[:, c % 2, j, :])
                last.then_inc(sem("o_ps"), 1)

            def att_out(c):
                pe.wait_ge(sem("o"), c + 1)
                mm(bank[5][:, :], W("wo"), oT[:, c % 2, :]).then_inc(sem("x3_ps"), 1)

            def router1(c):
                pe.wait_ge(sem("z"), LN["rt", c] + 1)
                pe.wait_ge(sem("x2"), min(c + 3, NCH))
                if c >= 1:
                    pe.wait_ge(sem("lg"), c)
                mm(bank[4][0:32, :], W("wr1"), xi[:, ck(c)]).then_inc(sem("r1_ps"), 1)

            def router2(c):
                pe.wait_ge(sem("r1"), c + 1)
                for j in range(BPC):
                    last = mm(bank[4][:, j * E:(j + 1) * E], r1[:, c % 2, j * 128:(j + 1) * 128], W("wr2"))
                last.then_inc(sem("lg_ps"), 1)

            def expand(c, ba, bb):
                pe.wait_ge(sem("tif"), c + 1)
                for k in range(2):
                    for j in range(BPC):
                        t = c * BPC + j
                        last = pe.transpose(bank[(ba, bb)[k]][:, j * 128:(j + 1) * 128],
                                            tif[:, t, k:k + 1].to_broadcast([128, 128]), ident)
                    last.then_inc(sem("idx_ps"), 1)

            def expand_weights(c, ba, bb):
                pe.wait_ge(sem("cf2"), 2 * (c + 1))
                for k in range(2):
                    pe.wait_ge(sem("idx"), 2 * c + k + 1)
                    for j in range(BPC):
                        t = c * BPC + j
                        last = pe.transpose(bank[(ba, bb)[k]][:, j * 128:(j + 1) * 128],
                                            cf2[:, k, t:t + 1].to_broadcast([128, 128]), ident)
                    last.then_inc(sem("c_ps"), 1)

            def hidden(s):
                c, it2 = s % NCH, s >= NCH
                if it2:
                    pe.wait_ge(sem("xi"), s - NCH + 1)
                    pe.wait_ge(sem("v1"), s - NCH + 1)
                for j in range(HT + 1):
                    out = hid_bank(s, j)[:, :] if j < HT else hid_bank(s, 0)[0:H, :]
                    name, wd, M = ("ew1", E * H, 128) if j < HT else ("ws1", H, H)
                    o = j * 128 if j < HT else 0
                    if j >= 2:
                        pe.wait_ge(sem("hid"), HT * s + j - 1)
                    elif s == 1:
                        pe.wait_ge(sem("z"), 3 * NCH)
                    elif s >= 2:
                        if j == 0:
                            pe.wait_ge(sem("rr"), 2 * (s - 1) - 1)
                        else:
                            pe.wait_ge(sem("th"), s - 1)
                    last = mm(out, W(name, o, o + M), xi[:, ck(c)], stop=not it2)
                    if it2:
                        last = mm(out, W(name, wd + o, wd + o + M), vT[:, ck(c)], start=False)
                    last.then_inc(sem("hid_ps"), 1)

            pe.wait_ge(sem("cw"), 1)
            pe.wait_ge(sem("v"), VG)
            pe.wait_ge(sem("b2s"), 1)
            compose_w2(0)
            ln_tok("ffn", 0, "x1")
            compose_w2(1)
            ln_zt("ffn", 0)
            ln_tok("ffn", 1, "x1")
            compose_w2(2)
            ffn_up(0, (0, 1))
            compose_w2(3)
            ffn_up(0, (2, 3))
            pe.wait_ge(sem("w2"), 1)
            for t in range(SLOTS):
                f, a, q, x = (0 <= t - i < NCH for i in range(4))
                if t == 1:
                    pe.wait_ge(sem("in_B"), 16)
                if t == 2:
                    pe.wait_ge(sem("r1one"), 1)
                if q:
                    probs_t(t - 2)
                if a:
                    ln_tok("att", t - 1, "x2")
                if t and t + 1 < NCH:
                    ln_tok("ffn", t + 1, "x1")
                if x and not f:
                    pe.wait_ge(sem("cb"), 2 * (t - 3))
                    expand(t - 3, 2, 3)
                if f and t:
                    ffn_up(t, (0, 1))
                if q:
                    att_v(t - 2)
                if a:
                    ln_zt("att", t - 1)
                if q:
                    att_out(t - 2)
                if f and t:
                    ffn_up(t, (2,))
                if a:
                    q_proj(t - 1)
                if f and t:
                    ffn_up(t, (3,))
                if t + 1 < NCH:
                    ln_zt("ffn", t + 1)
                if q:
                    ln_tok("rt", t - 2, "x3")
                if a:
                    scores(t - 1)
                if x and f:
                    pe.wait_ge(sem("fh"), FT * NCH)
                    expand(t - 3, 2, 3)
                if f:
                    ffn_down(t)
                if t == SLOTS - 1:
                    hidden(0)
                if x:
                    expand_weights(t - 3, 2, 3)
                if q:
                    ln_zt("rt", t - 2)
                if q:
                    router1(t - 2)
                    router2(t - 2)
            pe.wait_ge(sem("z"), 3 * NCH)
            pe.wait_ge(sem("x3"), NCH)
            pe.wait_ge(sem("lg"), NCH)
            pe.wait_ge(sem("x2"), NCH)
            pe.wait_ge(sem("bparts"), 6)
            def expert_out(s, k, part, out, last_of=None):
                c = s % NCH
                cols = slice(part * D, (part + 1) * D)
                src = m72[:, k - 1, ck(c)] if k else onesb[:, :]
                mm(out, bparts[:, 0 if k else 1, cols], src, stop=False)
                if k == 0:
                    return mm(out, W("ws2", part * D, (part + 1) * D), hs, start=False)
                for j in range(HT):
                    last = mm(out, W("ew2", j * 3 * D + part * D, j * 3 * D + (part + 1) * D),
                              hm[:, k - 1, j, :], start=False, stop=j == HT - 1)
                return last

            def refine_a(s):
                pe.wait_ge(sem("xn"), s + 1)
                for j in range(2):
                    pe.wait_ge(sem("hid"), HT * min(s + 2, STEPS))
                    if j == 1:
                        pe.wait_ge(sem("hs"), min(s + 2, STEPS))
                    mm(bank[6 + (j + 1) % 2][:, :], W("wf1", j * 128, (j + 1) * 128), xn)\
                        .then_inc(sem("f1_ps"), 1)
                pe.wait_ge(sem("fhg"), 2 * s + 1)
                mm(bank[7][0:32, :], W("wh1"), xn).then_inc(sem("h1_ps"), 1)

            def refine_b(s):
                pe.wait_ge(sem("fhg"), 2 * s + 2)
                for j in range(2):
                    last = mm(bank[6][:, :], W("wf2", j * 128, (j + 1) * 128), fh[:, j, :],
                              start=j == 0, stop=j == 1)
                last.then_inc(sem("f2_ps"), 1)
                pe.wait_ge(sem("h1"), s + 1)
                mm(bank[7][:, :], W("wh2").to_broadcast([32, 128]), h1).then_inc(sem("h2_ps"), 1)

            for s in range(STEPS):
                c, it2 = s % NCH, s >= NCH
                if s >= 1:
                    hidden(s)
                if s >= 1:
                    refine_a(s - 1)
                else:
                    expand(NCH - 1, 0, 1)
                    pe.wait_ge(sem("cb"), 2 * (NCH - 1))
                pe.wait_ge(sem("hs"), s + 1)
                for k in range(3):
                    if s >= 1:
                        pe.wait_ge(sem("sp"), 3 * (s - 1) + k + 1)
                    if k:
                        pe.wait_ge(sem("hm"), 8 * s + (8 if k == 2 else 7))
                    expert_out(s, k, 1, bank[3 + k][:, :]).then_inc(sem("b_ps"), 1)
                    if k == 1 and s >= 1:
                        refine_b(s - 1)
                if s == 0:
                    expand_weights(NCH - 1, 0, 1)
                    pe.wait_ge(sem("cb"), 2 * NCH)
                for k in range(3):
                    if it2:
                        q = s - NCH
                        if k == 0:
                            pe.wait_ge(sem("tg"), 3 * s)
                        elif k == 1:
                            pe.wait_ge(sem("tg"), 3 * s)
                        else:
                            pe.wait_ge(sem("tg"), 3 * s + 1)
                        expert_out(s, k, 0, bank[(2 * k) % 3][:, :]).then_inc(sem("a_ps"), 1)
                        if k == 0:
                            pe.wait_ge(sem("tg"), 3 * s)
                        elif k == 1:
                            pe.wait_ge(sem("ta"), 3 * q + 1)
                        else:
                            pe.wait_ge(sem("ta"), 3 * q + 2)
                    elif s >= 1:
                        pe.wait_ge(sem("tg"), 3 * (s - 1) + k + 1)
                    expert_out(s, k, 2, bank[(2 * k + 1) % 3][:, :]).then_inc(sem("g_ps"), 1)
            refine_a(STEPS - 1)
            refine_b(STEPS - 1)


def kernel(**inputs):
    import concourse.bacc as bacc
    from concourse.bass_utils import run_bass_kernel_spmd

    f32 = np.float32
    g = {k: np.asarray(v) for k, v in inputs.items()}

    def col(a, rows=128):
        return np.ascontiguousarray(a.reshape(-1, rows).T)

    def rep(a):
        return np.ascontiguousarray(np.broadcast_to(a.reshape(1, -1), (128, a.size)))

    f = np.arange(NF)[:, None]
    n = np.arange(S)[None, :]
    ang = 2 * np.pi * ((f * n) % S) / S
    twice = np.where((f == 0) | (f == S // 2), 1.0, 2.0)
    shape_only = {"cl": np.cos(ang).T, "sl": np.sin(ang).T, "cf": np.cos(ang), "sf": np.sin(ang),
                  "a1": twice / (S * B * DH), "a2": twice / S, "ident": np.eye(128),
                  "tile_expert": 2 * np.arange(HT)[None, :] + (np.arange(128)[:, None] >= H),
                  "bias_expert": np.arange(96)[:, None] % 32}
    shape_only = {k: v.astype(f32) for k, v in shape_only.items()}

    def thrice(a):
        out = np.zeros((96, a.shape[1]), f32)
        for q in range(3):
            out[32 * q:32 * q + a.shape[0]] = a
        return out

    x = lambda k: g["L1_ffn_" + k]
    parts = dict(shape_only)
    parts.update(
        wq8=g["L0_xattn_Wq"], bq8=rep(g["L0_xattn_bq"]), log1=rep(g["L0_ffn_fc1_logits"]),
        log2=rep(g["L0_ffn_fc2_logits"]), wout=g["L0_xattn_Wout"], bout=col(g["L0_xattn_bout"]),
        wq=g["L1_xattn_Wq"], wk=g["L1_xattn_Wk"], wv=g["L1_xattn_Wv"], wo=g["L1_xattn_Wo"],
        bq=col(g["L1_xattn_bq"]), bk=col(g["L1_xattn_bk"]), bv=col(g["L1_xattn_bv"]), bo=col(g["L1_xattn_bo"]),
        wr1=x("w_r1"), br1=col(x("b_r1"), 32), wr2=np.concatenate([x("w_r2"), x("b_r2")[None]], 0),
        wh1=x("w_h1"), bh1=col(x("b_h1"), 32), wh2=x("w_h2"), bh2=rep(x("b_h2")),
        ew1=x("expert_w1").reshape(E, 2, D, H).transpose(2, 1, 0, 3).reshape(D, -1),
        eb1=col(x("expert_b1")),
        ew2=x("expert_w2").reshape(HT, 128, 3 * D).transpose(1, 0, 2).reshape(128, -1),
        eb2=thrice(x("expert_b2")),
        ws1=x("w_s1").reshape(2, D, H).transpose(1, 0, 2).reshape(D, -1), bs1=col(x("b_s1"), H),
        ws2=x("w_s2"), bs2=thrice(x("b_s2")[None]), wf1=x("w_f1"), bf1=col(x("b_f1")),
        wf2=x("w_f2").reshape(2, 128, D).transpose(1, 0, 2).reshape(128, -1), bf2=col(x("b_f2")),
        iw=col(x("integration_weight")), mu=col(x("mu")), sw=rep(x("shared_weight")))

    def pack(layout):
        at, total = columns(layout)
        out = np.zeros((128, total), f32)
        for name, (rows, a, cols) in at.items():
            out[0:rows, a:a + cols] = parts[name]
        return out

    def rows(a):
        return np.ascontiguousarray(a.reshape(KC, 128, -1).transpose(1, 0, 2))

    arrays = {
        "xtok": np.ascontiguousarray(g["x"].transpose(1, 0, 2)),
        "xT": np.ascontiguousarray(g["x"].transpose(2, 0, 1).reshape(D, T)),
        "ctxT": np.ascontiguousarray(g["ctx_1024"].transpose(2, 0, 1).reshape(D, T)),
        "packA": pack(PACK_A), "packB": pack(PACK_B),
        "fc1a": rows(g["L0_ffn_fc1_A"].transpose(0, 2, 1).reshape(PRIM * RANK, D)),
        "fc1b": rows(g["L0_ffn_fc1_B"].reshape(PRIM * RANK, FF)),
        "fc2a": rows(g["L0_ffn_fc2_A"].transpose(0, 2, 1).reshape(PRIM * RANK, FF)),
        "fc2b": rows(g["L0_ffn_fc2_B"].reshape(PRIM * RANK, D)),
    }
    arrays = {"in_" + k: v for k, v in arrays.items()}
    nc = bacc.Bacc("TRN2", target_bir_lowering=False, num_devices=1)
    args = [nc.dram_tensor(k, a.shape, mybir.dt.from_np(a.dtype), kind="ExternalInput").ap()
            for k, a in arrays.items()]
    out = nc.dram_tensor("outT", (D, T), mybir.dt.float32, kind="ExternalOutput").ap()
    build(nc, *args, out)
    r = run_bass_kernel_spmd(nc, [arrays], core_ids=[0])
    got = np.asarray(r.results[0]["outT"])
    return np.ascontiguousarray(got.reshape(D, B, S).transpose(1, 2, 0))
```

```python
import numpy as np
import concourse.bass as bass
from concourse import mybir
from contextlib import ExitStack

B, S, D = 16, 128, 128
T = B * S
CH = 512
NCH = T // CH
BPC = CH // S
DH, HEADS = 8, 16
NF = S // 2 + 1
TOPK = int(2 * np.log(256))
PRIM, RANK, FF = 32, 64, 512
KC = PRIM * RANK // 128
FT = FF // 128
E, H, HT = 8, 64, 4
ITER = 2
EPS = 1e-5
NEG = -3.0e38

PACK_A = [("wv", 128, D), ("wq8", 128, DH), ("bq8", 128, DH), ("log1", 128, PRIM), ("log2", 128, PRIM),
          ("wout", 128, D), ("cl", 128, NF), ("sl", 128, NF), ("cf", NF, S), ("sf", NF, S),
          ("a1", NF, 1), ("a2", NF, 1), ("bout", 128, 1), ("ident", 128, 128),
          ("bk", 128, 1), ("wk", 128, D)]
VK = D + DH
VB = CH // VK
VG = -(-B // VB)
PACK_B = [("wq", 128, D), ("wo", 128, D), ("bq", 128, 1), ("bv", 128, 1), ("bo", 128, 1),
          ("wr1", 128, 32), ("br1", 32, 1), ("wr2", 33, E), ("wh1", 128, 32), ("bh1", 32, 1),
          ("wh2", 32, 1), ("bh2", 128, 1), ("ew1", 128, 2 * E * H), ("eb1", 128, HT),
          ("eb2", 96, 3 * D), ("ws1", 128, 2 * H), ("bs1", H, 1),
          ("ws2", H, 3 * D), ("bs2", 96, 3 * D), ("wf1", 128, 2 * D), ("bf1", 128, 2),
          ("wf2", 128, 2 * D), ("bf2", 128, 1), ("iw", 128, 1), ("mu", 128, 1),
          ("sw", 128, 1), ("bs2c", 128, 3), ("tile_expert", 128, HT), ("bias_expert", 96, 1)]


def columns(layout):
    at, out = 0, {}
    for name, rows, cols in layout:
        out[name] = (rows, at, cols)
        at += cols
    return out, at


def build(nc, d_xtok, d_xT, d_ctxT, d_packA, d_packB, d_ew2, d_a1, d_b1, d_a2, d_b2, d_out):
    F, BF, U32 = mybir.dt.float32, mybir.dt.bfloat16, mybir.dt.uint32
    FR = mybir.dt.float32r
    ALU, ACT, AX = mybir.AluOpType, mybir.ActivationFunctionType, mybir.AxisListType
    colA, nA = columns(PACK_A)
    colB, nB = columns(PACK_B)
    SCALE = 1.0 / float(np.sqrt(np.float32(D)))

    ctx = ExitStack()
    with ctx:
        def sb(name, shape, dt=F):
            return ctx.enter_context(nc.sbuf_tensor(name, shape, dt))

        sems = {}

        def sem(name):
            if name not in sems:
                sems[name] = ctx.enter_context(nc.semaphore(name))
            return sems[name]

        xtok_f = sb("xtok", [128, B * D])
        xtok = xtok_f[:, :].rearrange("p (b d) -> p b d", b=B)
        xT = sb("xT", [128, T])
        ctxT = sb("ctxT", [128, T])
        pA = sb("pA", [128, nA])
        pB = sb("pB", [128, nB])
        a1_f = sb("a1", [128, KC * D])
        b2_f = sb("b2", [128, KC * D])
        a1 = a1_f[:, :].rearrange("p (k d) -> p k d", k=KC)
        b2 = b2_f[:, :].rearrange("p (k d) -> p k d", k=KC)
        PIECE = KC * 128
        ring = sb("ring", [128, 5 * PIECE])

        def b1_piece(i):
            return ring[:, i * PIECE:(i + 1) * PIECE].rearrange("p (k n) -> p k n", n=FF)

        def a2_piece(f):
            at = (f + 4) % 5
            return ring[:, at * PIECE:(at + 1) * PIECE].rearrange("p (k n) -> p k n", k=KC)

        KP = PIECE // FF

        def A(name, a=0, b=None):
            r, at, n = colA[name]
            return pA[0:r, at + a:at + (n if b is None else b)]

        def W(name, a=0, b=None):
            r, at, n = colB[name]
            return pB[0:r, at + a:at + (n if b is None else b)]

        bank = [ctx.enter_context(nc.psum_tensor(f"bank{i}", [128, 512], F)) for i in range(8)]

        hB_f = sb("hB", [128, 2 * FT * CH])
        blk = hB_f[:, :].rearrange("p (n m) -> p n m", m=128)
        qt = hB_f[:, 0:384].rearrange("p (a b c) -> p a b c", a=3, b=B)
        qk = blk[:, 3:5, :]
        cw = blk[0:NF, 5:7, :]
        fr = blk[0:NF, 7:11, :].rearrange("p (a b) n -> p a b n", a=2)
        junk = blk[0:NF, 11:17, :]
        cor = blk[0:NF, 17:20, :]
        ecor = blk[0:NF, 20:22, :]
        ab_f = blk[0:NF, 22:26, :]
        st = sb("st", [128, B, 6])
        mv = sb("mv", [128, B, 2])
        veps = sb("veps", [128, B])
        rstd = sb("rstd", [128, B])
        mhalf = sb("mhalf", [128, B])
        red = sb("red", [NF, 12])
        ones = sb("ones", [128, 128])
        reB = sb("reB", [NF, 2, NF])
        m8 = sb("m8", [NF, 3, 8])
        yb = sb("yb", [128, 128])
        lg_n = sb("lg_n", [128, 6])
        lg_e = sb("lg_e", [128, 2, PRIM])
        wcol = sb("wcol", [128, 2, KC])
        kT = sb("kT", [128, T])
        vtok_f = sb("vtok", [128, B * D])
        vtok = vtok_f[:, :].rearrange("p (b d) -> p b d", b=B)
        wz = sb("wz", [128, 3 * CH])
        w1 = wz[:, 0:CH]
        w2 = wz[:, CH:2 * CH].rearrange("p (a d) -> p a d", a=FT)
        z3 = wz[:, 2 * CH:3 * CH]
        lst = sb("lst", [128, 2, BPC, 6])
        lmv = sb("lmv", [128, 2, BPC, 2])
        lve = sb("lve", [128, 2, BPC])
        lrs = sb("lrs", [128, 2, BPC])
        zz = sb("zz", [128, 4 * CH])
        ztok = zz[:, 0:2 * CH].rearrange("p (a b d) -> p a b d", a=2, b=BPC)
        zT = zz[:, 2 * CH:4 * CH].rearrange("p (a n) -> p a n", a=2)
        hB = hB_f[:, :].rearrange("p (a f n) -> p a f n", a=2, f=FT)
        att = ring[:, 0:10 * CH].rearrange("p (w a n) -> p w a n", w=5, a=2)
        qT, oT = att[:, 0], att[:, 1]
        bqs = sb("bqs", [128, 1])
        nmax = sb("nmax", [128, 2, BPC])
        prob = att[:, 2].rearrange("p a (b k) -> p a b k", b=BPC)
        psum_ = sb("psum_", [128, 2, BPC])
        prec = sb("prec", [128, 2, BPC])
        pn = att[:, 3].rearrange("p a (b k) -> p a b k", b=BPC)
        pT = att[:, 4].rearrange("p a (b k) -> p a b k", b=BPC)
        xi = sb("xi", [128, T])
        r1 = ctxT[0:33, 0:2 * CH].rearrange("p (a n) -> p a n", a=2)
        lg = sb("lg", [128, B, E])
        top = sb("top", [128, B, 8])
        tix = sb("tix", [128, B, 8], U32)
        tif = sb("tif", [128, B, 8])
        rt = sb("rt", [128, 5, B])
        swc = sb("swc", [128, 4])
        cf2 = sb("cf2", [128, 2, B])
        idxb = ring[:, 10 * CH:10 * CH + 2 * T].rearrange("p (c a n) -> p c a n", c=NCH, a=2)
        m72 = xtok_f[0:96, :].bitcast(BF).rearrange("p (a n) -> p a n", a=2)
        cb = hB_f[:, :].rearrange("p (c a n) -> p c a n", c=NCH, a=2)
        onesb = sb("onesb", [96, CH], BF)
        bparts = sb("bparts", [96, 2, 3 * D], BF)
        bhi = ring[0:96, 3 * PIECE:3 * PIECE + 9 * D].bitcast(BF).rearrange("p (q i n) -> p q i n", q=3, i=2)
        brem = xtok_f[0:96, 0:12 * D].rearrange("p (q i n) -> p q i n", q=2, i=2)
        iwh = sb("iwh", [128, 1])
        bh2h = sb("bh2h", [128, 1])
        half_col = sb("half_col", [128, 1])
        bs2h = sb("bs2h", [128, 3])
        vT = a1_f
        hid = ring[:, 0:HT * CH].rearrange("p (f n) -> p f n", f=HT)
        hs = kT[0:H, 3 * CH:4 * CH]
        hm = (ring[:, 8 * CH:9 * CH], ring[:, 9 * CH:10 * CH])
        hm_hi = sb("hm_hi", [128, 2, HT, CH], FR)
        hm_lo = sb("hm_lo", [128, 2, HT, CH], FR)
        ew2 = b2_f[:, 0:HT * 3 * D]
        ew2_hi = sb("ew2_hi", [128, HT * 3 * D], FR)
        ew2_lo = sb("ew2_lo", [128, HT * 3 * D], FR)
        ew = ring[:, 4 * CH:8 * CH].rearrange("p (f n) -> p f n", f=4)
        pw = wz[:, 0:3 * CH].rearrange("p (f n) -> p f n", f=3)
        ab = vtok_f[:, 0:3 * CH].rearrange("p (f n) -> p f n", f=3)
        ta = ctxT[:, 0:0 + 3 * CH].rearrange("p (f n) -> p f n", f=3)
        ta_odd = (ring[:, 18 * CH:19 * CH], sb("ta_odd", [128, CH])[:, :])
        tg_odd = (ring[:, 19 * CH:20 * CH], b2_f[:, 3 * CH:4 * CH])
        tg = kT[:, 0:0 + 3 * CH].rearrange("p (f n) -> p f n", f=3)
        sm = b2_f[:, 0:3 * CH].rearrange("p (f n) -> p f n", f=3)
        xn = vtok_f[:, 3 * CH:4 * CH]
        fh = zz[:, 0:2 * CH].rearrange("p (f n) -> p f n", f=2)
        th = zz[:, 2 * CH:3 * CH]
        h1 = zz[0:32, 3 * CH:4 * CH]
        rr = ctxT[:, 3 * CH:4 * CH]
        res = xT

        def ck(c):
            return slice(c * CH, (c + 1) * CH)

        ident = A("ident")
        block = ctx.enter_context(nc.Block())

        def ta_of(s, k):
            return ta_odd[k] if k < 2 and s % 2 else ta[:, k, :]

        def tg_of(s, k):
            return tg_odd[k] if k < 2 and s % 2 else tg[:, k, :]

        def hid_bank(s, j):
            return bank[7 if j % 2 else (5 if s == 0 else 6)]

        def vk_bank(g):
            return bank[2 + g % 2][:, 0:VB * VK].rearrange("p (b n) -> p b n", b=VB)

        STEPS = ITER * NCH

        SLOTS = NCH + 2
        LN = {("ffn", 0): 0, ("ffn", 1): 1}
        for t in range(SLOTS):
            for which, c in (("att", t - 1), ("ffn", t + 2), ("rt", t - 2)):
                if 0 <= c < NCH:
                    LN[which, c] = len(LN)

        @block.sync
        def _(sp):
            for dst, src, name in ((pA[:, :], d_packA, "in_A"),
                                   (ctxT[:, 0:T // 2], d_ctxT[:, 0:T // 2], "in_ctx_0"),
                                   (ctxT[:, T // 2:T], d_ctxT[:, T // 2:T], "in_ctx_1"),
                                   (xtok[:, :, :], d_xtok, "in_xtok"), (xT[:, :], d_xT, "in_x"),
                                   (a1[:, :, :], d_a1, "in_a1")):
                sp.dma_start(dst, src).then_inc(sem(name), 16)
            for i in range(4):
                sp.dma_start(b1_piece(i), d_b1[:, i * KP:(i + 1) * KP, :]).then_inc(sem(f"in_b1_{i}"), 16)
            sp.dma_start(b2[:, :, :], d_b2).then_inc(sem("in_b2"), 16)
            for f in range(FT):
                if f:
                    sp.wait_ge(sem("w1_piece"), f)
                sp.dma_start(a2_piece(f), d_a2[:, :, f * 128:(f + 1) * 128]).then_inc(sem(f"in_a2_{f}"), 16)
            sp.dma_start(pB[:, :], d_packB).then_inc(sem("in_B"), 16)
            sp.wait_ge(sem("w2_ps"), 1)
            sp.dma_start(ew2, d_ew2).then_inc(sem("in_ew2"), 16)
            for c in range(NCH):
                sp.wait_ge(sem("res"), c + 1)
                sp.dma_start(d_out[:, ck(c)], res[:, ck(c)]).then_inc(sem("out"), 16)
            sp.wait_ge(sem("out"), 16 * NCH)

        @block.gpsimd
        def _(pool):
            pool.memset(mhalf[:, :], -0.5).then_inc(sem("mhalf"), 1)
            pool.memset(ones[:, :], 1.0).then_inc(sem("ones"), 1)
            pool.memset(onesb[:, :], 1.0).then_inc(sem("onesb"), 1)
            pool.wait_ge(sem("onesb"), 1)
            pool.memset(half_col[:, :], 0.5).then_inc(sem("half_col"), 1)
            pool.wait_ge(sem("half_col"), 1)
            pool.wait_ge(sem("mhalf"), 1)
            pool.wait_ge(sem("veps"), 1)
            pool.tensor_tensor(rstd[:, :], veps[:, :], mhalf[:, :], ALU.pow).then_inc(sem("rstd"), 1)
            pool.wait_ge(sem("rstd"), 1)
            pool.wait_ge(sem("v_ps"), VG)
            pool.wait_ge(sem("k_ps"), NCH)
            pool.memset(r1[32:33, :, :], 1.0).then_inc(sem("r1one"), 1)
            pool.wait_ge(sem("r1one"), 1)
            for n in range(3 * NCH):
                pool.wait_ge(sem("lve"), n + 1)
                pool.tensor_tensor(lrs[:, n % 2, :], lve[:, n % 2, :], mhalf[:, 0:BPC], ALU.pow)\
                    .then_inc(sem("lrs"), 1)
            def refined(s):
                c = s % NCH
                pool.wait_ge(sem("rr"), 2 * s + 2)
                pool.tensor_tensor(xi[:, ck(c)], xi[:, ck(c)], rr, ALU.add).then_inc(sem("xi"), 1)
                if s >= NCH:
                    pool.wait_ge(sem("xi"), s + 1)
                    pool.tensor_tensor(res[:, ck(c)], xi[:, ck(c)], xT[:, ck(c)], ALU.add)\
                        .then_inc(sem("res"), 1)

            for s in range(STEPS):
                c = s % NCH
                if s >= 2:
                    refined(s - 2)
                pool.wait_ge(sem("e0"), s + 1)
                if s >= 1:
                    pool.wait_ge(sem("w"), 3 * s)
                for k in range(2):
                    pool.tensor_tensor(ew[:, 2 + k, :], ew[:, 0, :], cb[:, c, k, :], ALU.mult)\
                        .then_inc(sem("ew"), 1)
                if s < NCH:
                    pool.wait_ge(sem("w"), 3 * s + 3)
                    pool.tensor_tensor(vT[:, ck(c)], sm[:, 0, :], sm[:, 1, :], ALU.add).then_inc(sem("v01"), 1)
                    pool.wait_ge(sem("v01"), s + 1)
                    pool.tensor_tensor(vT[:, ck(c)], vT[:, ck(c)], sm[:, 2, :], ALU.add).then_inc(sem("v1"), 1)
                if s >= NCH:
                    pool.wait_ge(sem("v1"), c + 1)
                    if s > NCH:
                        pool.wait_ge(sem("u"), 3 * (s - NCH))
                    for k in range(2):
                        pool.tensor_tensor(pw[:, 1 + k, :], vT[:, ck(c)], cb[:, c, k, :], ALU.mult)\
                            .then_inc(sem("pw"), 1)

        @block.scalar
        def _(act):
            act.wait_ge(sem("lgn"), 2)
            for i, n in enumerate(("log1", "log2")):
                act.activation(lg_e[:, i, :], A(n), ACT.Exp, bias=lg_n[:, i:i + 1],
                               accum_out=lg_n[:, 2 + i:3 + i]).then_inc(sem("lge"), 1)
            act.wait_ge(sem("cw_ps"), 1)
            act.activation(cw[:, :, :], bank[1][0:NF, 0:2 * D].rearrange("p (a d) -> p a d", a=2),
                           ACT.Copy).then_inc(sem("cw"), 1)
            for g in range(VG):
                b0, nb = g * VB, min(VB, B - g * VB)
                act.wait_ge(sem("v_ps"), g + 1)
                act.wait_ge(sem("k8"), g + 1)
                act.activation(vtok[:, b0:b0 + nb, :], vk_bank(g)[:, 0:nb, 0:D], ACT.Copy)\
                    .then_inc(sem("v"), 1)
            for c in range(NCH):
                act.wait_ge(sem("k_ps"), c + 1)
                act.activation(kT[:, ck(c)], bank[6 + c % 2][:, :], ACT.Identity, bias=A("bk"))\
                    .then_inc(sem("k"), 1)
            act.wait_ge(sem("negmax"), 1)
            act.activation(ecor[:, 0, :], cor[:, 0, :], ACT.Exp, bias=red[:, 6:7]).then_inc(sem("ecor"), 1)
            act.wait_ge(sem("w1_ps"), 1)
            act.activation(w1[:, :], bank[6][:, :], ACT.Copy).then_inc(sem("w1"), 1)
            act.wait_ge(sem("y_ps"), 1)
            act.activation(yb[:, :], bank[4][:, 0:128], ACT.Identity, bias=A("bout")).then_inc(sem("yb"), 1)
            def ln_evac(which, c, dst):
                act.wait_ge(sem("zt_ps"), LN[which, c] + 1)
                act.activation(dst, bank[6][:, :], ACT.Copy).then_inc(sem("z"), 1)

            def z_ffn(c):
                if c >= 2:
                    act.wait_ge(sem("fh_ps"), FT * (c - 1))
                ln_evac("ffn", c, zT[:, c % 2, :])

            def z_att(c):
                if c >= 1:
                    act.wait_ge(sem("q_ps"), c)
                ln_evac("att", c, z3[:, :])

            def gelus(c, tiles):
                for f in tiles:
                    act.wait_ge(sem("fh_ps"), FT * c + f + 1)
                    if c >= 2:
                        act.wait_ge(sem("fo_ps"), c - 1)
                    act.activation(hB[:, c % 2, f, :], bank[2 + f % 2][:, :], ACT.Gelu_apprx_tanh)\
                        .then_inc(sem("fh"), 1)

            def q_evac(c):
                act.wait_ge(sem("q_ps"), c + 1)
                if c == 0:
                    act.wait_ge(sem("bqs"), 1)
                if c >= 2:
                    act.wait_ge(sem("s_ps"), c - 1)
                act.activation(qT[:, c % 2, :], bank[5][:, :], ACT.Identity, bias=bqs[:, 0:1], scale=SCALE)\
                    .then_inc(sem("q"), 1)

            def exps(c):
                act.wait_ge(sem("nmax"), c + 1)
                if c >= 2:
                    act.wait_ge(sem("pn"), c - 1)
                for j in range(BPC):
                    act.activation(prob[:, c % 2, j, :], bank[7][:, j * S:(j + 1) * S], ACT.Exp,
                                   bias=nmax[:, c % 2, j:j + 1], accum_out=psum_[:, c % 2, j:j + 1])\
                        .then_inc(sem("prob"), 1)

            def o_evac(c):
                act.wait_ge(sem("o_ps"), c + 1)
                if c >= 2:
                    act.wait_ge(sem("x3_ps"), c - 1)
                act.activation(oT[:, c % 2, :], bank[7][:, :], ACT.Identity, bias=W("bv"))\
                    .then_inc(sem("o"), 1)

            def r1_gelu(c):
                act.wait_ge(sem("r1_ps"), c + 1)
                if c >= 2:
                    act.wait_ge(sem("lg_ps"), c - 1)
                act.activation(r1[0:32, c % 2, :], bank[4][0:32, :], ACT.Gelu, bias=W("br1"))\
                    .then_inc(sem("r1"), 1)

            def second_exp(c):
                act.wait_ge(sem("dl"), c + 1)
                t = slice(c * BPC, (c + 1) * BPC)
                act.activation(rt[:, 1, t], rt[:, 0, t], ACT.Exp).then_inc(sem("de"), 1)

            def expand_evac(c, ba, bb):
                for k in range(2):
                    act.wait_ge(sem("idx_ps"), 2 * c + k + 1)
                    act.activation(idxb[:, c, k, :], bank[(ba, bb)[k]][:, :], ACT.Copy)\
                        .then_inc(sem("idx"), 1)

            def hidden_gelus(s):
                for j in range(HT):
                    act.wait_ge(sem("hid_ps"), 5 * s + j + 1)
                    if s >= 1:
                        act.wait_ge(sem("hm"), 8 * (s - 1) + HT + j + 1)
                    act.activation(hid[:, j, :], hid_bank(s, j)[:, :], ACT.Gelu,
                                   bias=W("eb1", j, j + 1)).then_inc(sem("hid"), 1)
                act.wait_ge(sem("hid_ps"), 5 * s + 5)
                if s >= 1:
                    act.wait_ge(sem("b_ps"), 3 * (s - 1) + 1)
                act.activation(hs, hid_bank(s, 0)[0:H, :], ACT.Gelu, bias=W("bs1")).then_inc(sem("hs"), 1)
            z_ffn(0)
            gelus(0, (0, 1))
            act.wait_ge(sem("w2_ps"), 1)
            act.activation(w2[:, :, :], bank[7][:, :].rearrange("p (a d) -> p a d", a=FT), ACT.Copy)\
                .then_inc(sem("w2"), 1)
            gelus(0, (2, 3))
            z_ffn(1)
            for t in range(SLOTS):
                f, a, q, x = (0 <= t - i < NCH for i in range(4))
                if f and t:
                    gelus(t, (0, 1))
                if q:
                    o_evac(t - 2)
                if x and not f:
                    expand_evac(t - 3, 2, 3)
                if a:
                    z_att(t - 1)
                if f and t:
                    gelus(t, (2,))
                if a:
                    q_evac(t - 1)
                if f and t:
                    gelus(t, (3,))
                if t + 2 < NCH:
                    z_ffn(t + 2)
                if a:
                    exps(t - 1)
                if t == 0:
                    act.wait_ge(sem("in_ew2"), 16)
                    act.activation(ew2_hi[:, :], ew2, ACT.Copy).then_inc(sem("ew2_hi"), 1)
                if t == 1:
                    act.wait_ge(sem("in_B"), 16)
                    act.activation(swc[:, 0:1], W("sw"), ACT.Exp, scale=-1.0).then_inc(sem("swe"), 1)
                if x:
                    second_exp(t - 3)
                if x and f:
                    expand_evac(t - 3, 2, 3)
                if t == SLOTS - 1:
                    hidden_gelus(0)
                if q:
                    ln_evac("rt", t - 2, xi[:, ck(t - 2)])
                if q:
                    r1_gelu(t - 2)
            second_exp(NCH - 1)

            def refine1(s):
                for j in range(2):
                    act.wait_ge(sem("f1_ps"), 2 * s + j + 1)
                    if s >= 1:
                        act.wait_ge(sem("f2_ps"), s)
                    act.activation(fh[:, j, :], bank[6 + (j + 1) % 2][:, :], ACT.Gelu,
                                   bias=W("bf1", j, j + 1)).then_inc(sem("fhg"), 1)
                act.wait_ge(sem("h1_ps"), s + 1)
                if s >= 1:
                    act.wait_ge(sem("h2_ps"), s)
                act.activation(h1, bank[7][0:32, :], ACT.Gelu, bias=W("bh1")).then_inc(sem("h1"), 1)

            def refine2(s):
                act.wait_ge(sem("h2_ps"), s + 1)
                if s >= 1:
                    act.wait_ge(sem("rr"), 2 * s)
                act.activation(th, bank[7][:, :], ACT.Tanh, bias=bh2h[:, 0:1], scale=0.5)\
                    .then_inc(sem("th"), 1)

            def gates(s, k):
                if s == 0 and k == 0:
                    act.wait_ge(sem("consts"), 3)
                if s >= NCH:
                    q = s - NCH
                    act.wait_ge(sem("a_ps"), 3 * q + k + 1)
                    if k == 2 and q >= 1:
                        act.wait_ge(sem("y"), 3 * s)
                    elif q >= 2:
                        act.wait_ge(sem("y"), 3 * (s - 1))
                    act.activation(ta_of(s, k), bank[(2 * k) % 3][:, :], ACT.Tanh, scale=0.5,
                                   bias=0.0 if k else bs2h[:, 0:1])\
                        .then_inc(sem("ta"), 1)
                act.wait_ge(sem("g_ps"), 3 * s + k + 1)
                if k == 2 and s >= 1:
                    act.wait_ge(sem("xn"), s)
                elif s >= 2:
                    act.wait_ge(sem("xn"), s - 1)
                act.activation(tg_of(s, k), bank[(2 * k + 1) % 3][:, :], ACT.Tanh, scale=0.5,
                               bias=0.0 if k else bs2h[:, 2:3])\
                    .then_inc(sem("tg"), 1)

            def beta_tanh(s, k0, k1):
                for k in range(k0, k1):
                    if s >= 1:
                        act.wait_ge(sem("sp"), 3 * (s - 1) + k + 1)
                    act.wait_ge(sem("b_ps"), 3 * s + k + 1)
                    act.activation(ab[:, k, :], bank[3 + k][:, :], ACT.Abs).then_inc(sem("ab"), 1)
                act.wait_ge(sem("ab"), 3 * s + k1)
                act.activation(ab[:, k0:k1, :], ab[:, k0:k1, :], ACT.Tanh, scale=0.5)\
                    .then_inc(sem("ab_tanh"), k1 - k0)

            def beta_ln(s, k0, k1):
                act.wait_ge(sem("ab_tanh"), 3 * s + k1)
                act.activation(ab[:, k0:k1, :], ab[:, k0:k1, :], ACT.Ln, bias=half_col[:, 0:1], scale=0.5)\
                    .then_inc(sem("ln"), k1 - k0)

            for s in range(STEPS):
                gates(s, 0)
                if s == 0:
                    expand_evac(NCH - 1, 6, 7)
                gates(s, 1)
                if 1 <= s < STEPS - 1:
                    refine1(s - 1)
                if s + 1 < STEPS:
                    hidden_gelus(s + 1)
                if s < STEPS - 1:
                    beta_tanh(s, 0, 3)
                    if s < NCH - 1:
                        beta_ln(s, 0, 3)
                        gates(s, 2)
                    else:
                        gates(s, 2)
                        beta_ln(s, 0, 3)
                else:
                    beta_tanh(s, 0, 2)
                    beta_ln(s, 0, 2)
                    beta_tanh(s, 2, 3)
                    beta_ln(s, 2, 3)
                    gates(s, 2)
                    refine1(s - 1)
                if s >= 1:
                    refine2(s - 1)
            refine1(STEPS - 1)
            refine2(STEPS - 1)

        @block.vector
        def _(dve):
            chain = [0]

            def link(ins):
                chain[0] += 1
                ins.then_inc(sem("dve_chain"), 1)
                dve.wait_ge(sem("dve_chain"), chain[0])

            dve.wait_ge(sem("in_A"), 16)
            for i, n in enumerate(("log1", "log2")):
                dve.tensor_reduce(lg_n[:, i:i + 1], A(n), AX.X, ALU.max, negate=True)\
                    .then_inc(sem("lgn"), 1)
            for g in range(VG):
                b0, nb = g * VB, min(VB, B - g * VB)
                dve.wait_ge(sem("v_ps"), g + 1)
                dve.tensor_tensor(qk[:, 1, b0 * DH:(b0 + nb) * DH].rearrange("p (b c) -> p b c", c=DH),
                                  vk_bank(g)[:, 0:nb, D:VK],
                                  A("bq8").unsqueeze(1).to_broadcast([128, nb, DH]), ALU.add)\
                    .then_inc(sem("k8"), 1)
            dve.wait_ge(sem("in_xtok"), 16)
            for b in range(B):
                dve.bn_stats(st[:, b, :], xtok[:, b, :]).then_inc(sem("st"), 1)
            for b in range(B):
                dve.wait_ge(sem("st"), b + 1)
                dve.bn_aggr(mv[:, b, :], st[:, b, :]).then_inc(sem("mv"), 1)
            dve.wait_ge(sem("mv"), B)
            dve.tensor_scalar(veps[:, :], mv[:, :, 1], EPS, None, ALU.add).then_inc(sem("veps"), 1)
            dve.wait_ge(sem("lge"), 2)
            link(dve.reciprocal(lg_n[:, 4:6], lg_n[:, 2:4]))
            for i in range(2):
                for half in range(2):
                    p = slice(64 * half, 64 * half + 64)
                    dve.tensor_scalar(wcol[p, i, :], lg_e[p, i, half:PRIM:2], lg_n[p, 4 + i:5 + i], None,
                                      ALU.mult).then_inc(sem("wcol"), 1)
            dve.wait_ge(sem("wcol"), 4)
            dve.wait_ge(sem("in_a1"), 16)
            dve.tensor_tensor(a1[:, :, :], a1[:, :, :], wcol[:, 0, :].unsqueeze(2).to_broadcast([128, KC, D]),
                              ALU.mult).then_inc(sem("a1s"), 1)
            dve.wait_ge(sem("q8_ps"), 1)
            qps = bank[0][:, 0:128].rearrange("p (b c) -> p b c", c=DH)
            colsum = bank[0][:, 256:264].unsqueeze(1).to_broadcast([128, B, DH])
            mean = mv[:, :, 0:1].to_broadcast([128, B, DH])
            bq_b = A("bq8").unsqueeze(1).to_broadcast([128, B, DH])
            link(dve.tensor_tensor(qt[:, 0], colsum, mean, ALU.mult))
            link(dve.tensor_tensor(qt[:, 1], qps, qt[:, 0], ALU.subtract))
            dve.wait_ge(sem("rstd"), 1)
            link(dve.tensor_tensor(qt[:, 2], qt[:, 1], rstd[:, :].unsqueeze(2).to_broadcast([128, B, DH]),
                                   ALU.mult))
            dve.tensor_tensor(qk[:, 0, :].rearrange("p (b c) -> p b c", c=DH), qt[:, 2], bq_b, ALU.add)\
                .then_inc(sem("q8"), 1)
            dve.wait_ge(sem("dft_ps"), 1)
            link(dve.tensor_copy(fr[:, :, :, :],
                                 bank[4][0:NF, :].rearrange("p (a b n) -> p a b n", a=2, b=2)))
            for n, (i, j) in enumerate(((0, 0), (1, 1), (0, 1), (1, 0))):
                last = dve.tensor_tensor_reduce(out=junk[:, n, :], in0=fr[:, i, 0, :], in1=fr[:, j, 1, :],
                                                scale=1.0, scalar=0.0, op0=ALU.mult, op1=ALU.add,
                                                accum_out=red[:, n:n + 1])
                last.then_inc(sem("spec"), 1)
            dve.wait_ge(sem("spec"), 4)
            dve.tensor_scalar(red[:, 4:5], red[:, 0:1], red[:, 1:2], A("a1"), ALU.add, ALU.mult)\
                .then_inc(sem("spec"), 1)
            dve.tensor_scalar(red[:, 5:6], red[:, 3:4], red[:, 2:3], A("a1"), ALU.subtract, ALU.mult)\
                .then_inc(sem("spec"), 1)
            dve.wait_ge(sem("ones"), 1)
            dve.wait_ge(sem("spec"), 6)
            for n in range(2):
                dve.tensor_scalar(reB[:, n, :], ones[0:NF, 0:NF], red[:, 4 + n:5 + n], None, ALU.mult)\
                    .then_inc(sem("reB"), 1)
            dve.wait_ge(sem("cor_ps"), 1)
            link(dve.tensor_copy(cor[:, 0, :], bank[5][0:NF, 0:128]))
            link(dve.max(m8[:, 0, :], cor[:, 0, :]))
            dve.tensor_scalar(red[:, 6:7], m8[:, 0, 0:1], -1.0, None, ALU.mult).then_inc(sem("negmax"), 1)
            link(dve.match_replace(cor[:, 1, :], m8[:, 0, :], cor[:, 0, :], NEG))
            link(dve.max(m8[:, 1, :], cor[:, 1, :]))
            link(dve.memset(m8[:, 2, :], NEG))
            link(dve.tensor_copy(m8[:, 2, 0:TOPK - 8], m8[:, 1, 0:TOPK - 8]))
            link(dve.match_replace(cor[:, 2, :], m8[:, 2, :], cor[:, 1, :], NEG))
            link(dve.tensor_scalar(junk[:, 4, :], cor[:, 2, :], NEG, None, ALU.is_equal))
            dve.wait_ge(sem("ecor"), 1)
            link(dve.tensor_tensor_reduce(out=ecor[:, 1, :], in0=ecor[:, 0, :], in1=junk[:, 4, :],
                                          scale=1.0, scalar=0.0, op0=ALU.mult, op1=ALU.add,
                                          accum_out=red[:, 7:8]))
            dve.reciprocal(red[:, 8:9], red[:, 7:8]).then_inc(sem("wspec"), 1)
            for n, name in enumerate(("cf", "sf")):
                dve.tensor_tensor_reduce(out=junk[:, n, :], in0=ecor[:, 1, :], in1=A(name),
                                         scale=1.0, scalar=0.0, op0=ALU.mult, op1=ALU.add,
                                         accum_out=red[:, 9 + n:10 + n]).then_inc(sem("wspec"), 1)
            dve.wait_ge(sem("wspec"), 3)
            link(dve.tensor_scalar(red[:, 0:2], red[:, 9:11], red[:, 8:9], A("a2"), ALU.mult, ALU.mult))
            wc, ws = red[:, 0:1], red[:, 1:2]
            vc, vs = fr[:, 0, 1, :], fr[:, 1, 1, :]
            dve.tensor_scalar(ab_f[:, 0, :], vs, ws, None, ALU.mult).then_inc(sem("spc"), 1)
            dve.tensor_scalar(ab_f[:, 1, :], vc, ws, None, ALU.mult).then_inc(sem("spc"), 1)
            dve.wait_ge(sem("spc"), 2)
            dve.scalar_tensor_tensor(ab_f[:, 2, :], vc, wc, ab_f[:, 0, :], ALU.mult, ALU.add)\
                .then_inc(sem("abf"), 1)
            dve.scalar_tensor_tensor(ab_f[:, 3, :], vs, wc, ab_f[:, 1, :], ALU.mult, ALU.subtract)\
                .then_inc(sem("abf"), 1)
            dve.wait_ge(sem("in_b2"), 16)
            dve.tensor_tensor(b2[:, :, :], b2[:, :, :], wcol[:, 1, :].unsqueeze(2).to_broadcast([128, KC, D]),
                              ALU.mult).then_inc(sem("b2s"), 1)
            dve.wait_ge(sem("yb"), 1)
            dve.wait_ge(sem("in_x"), 16)
            for c in range(NCH):
                xv = xT[:, ck(c)].rearrange("p (b h c) -> p b h c", b=BPC, h=HEADS)
                yv = yb[:, c * BPC * DH:(c + 1) * BPC * DH].rearrange("p (b c) -> p b c", b=BPC)\
                    .unsqueeze(2).to_broadcast([128, BPC, HEADS, DH])
                dve.tensor_tensor(xv, xv, yv, ALU.add).then_inc(sem("x1"), 1)

            def ln_stats(which, c):
                n = LN[which, c]
                t = bank[n % 2]
                dve.wait_ge(sem("tok_ps"), n + 1)
                for j in range(BPC):
                    dve.bn_stats(lst[:, n % 2, j, :], t[:, j * D:(j + 1) * D]).then_inc(sem("lst"), 1)
                for j in range(BPC):
                    dve.wait_ge(sem("lst"), BPC * n + j + 1)
                    dve.bn_aggr(lmv[:, n % 2, j, :], lst[:, n % 2, j, :]).then_inc(sem("lmv"), 1)
                dve.wait_ge(sem("lmv"), BPC * (n + 1))
                dve.tensor_scalar(lve[:, n % 2, :], lmv[:, n % 2, :, 1], EPS, None, ALU.add)\
                    .then_inc(sem("lve"), 1)

            def ln_scale(which, c):
                n = LN[which, c]
                t = bank[n % 2]
                dve.wait_ge(sem("lrs"), n + 1)
                if n >= 2:
                    dve.wait_ge(sem("zt_ps"), n - 1)
                for j in range(BPC):
                    dve.tensor_scalar(ztok[:, n % 2, j, :], t[:, j * D:(j + 1) * D], lmv[:, n % 2, j, 0:1],
                                      lrs[:, n % 2, j:j + 1], ALU.subtract, ALU.mult)\
                        .then_inc(sem("ztok"), 1)

            def ffn_add(c):
                dve.wait_ge(sem("fo_ps"), c + 1)
                dve.tensor_tensor(xT[:, ck(c)], bank[4][:, :], xT[:, ck(c)], ALU.add)\
                    .then_inc(sem("x2"), 1)

            def att_max(c):
                dve.wait_ge(sem("s_ps"), c + 1)
                dve.tensor_reduce(nmax[:, c % 2, :], bank[7][:, :].rearrange("p (b k) -> p b k", b=BPC),
                                  AX.X, ALU.max, negate=True).then_inc(sem("nmax"), 1)

            def att_norm(c):
                dve.wait_ge(sem("prob"), BPC * (c + 1))
                link(dve.reciprocal(prec[:, c % 2, :], psum_[:, c % 2, :]))
                if c >= 2:
                    dve.wait_ge(sem("pt_ps"), c - 1)
                dve.tensor_tensor(pn[:, c % 2], prob[:, c % 2],
                                  prec[:, c % 2, :].unsqueeze(2).to_broadcast([128, BPC, S]), ALU.mult)\
                    .then_inc(sem("pn"), 1)

            def att_pt(c):
                dve.wait_ge(sem("pt_ps"), c + 1)
                if c >= 2:
                    dve.wait_ge(sem("o_ps"), c - 1)
                dve.tensor_copy(pT[:, c % 2], bank[5][:, :].rearrange("p (b k) -> p b k", b=BPC))\
                    .then_inc(sem("pT"), 1)

            def att_add(c):
                dve.wait_ge(sem("x3_ps"), c + 1)
                dve.scalar_tensor_tensor(xT[:, ck(c)], bank[5][:, :], W("bo"), xT[:, ck(c)],
                                         ALU.add, ALU.add).then_inc(sem("x3"), 1)

            def route(c):
                t = slice(c * BPC, (c + 1) * BPC)
                dve.wait_ge(sem("lg_ps"), c + 1)
                dve.tensor_copy(lg[:, t, :], bank[4][:, 0:BPC * E].rearrange("p (b e) -> p b e", b=BPC))\
                    .then_inc(sem("lg"), 1)
                dve.wait_ge(sem("lg"), c + 1)
                for b in range(c * BPC, (c + 1) * BPC):
                    dve.max(top[:, b, :], lg[:, b, :]).then_inc(sem("top"), 1)
                for b in range(c * BPC, (c + 1) * BPC):
                    dve.wait_ge(sem("top"), b + 1)
                    dve.max_index(tix[:, b, :], top[:, b, :], lg[:, b, :]).then_inc(sem("tix"), 1)
                dve.tensor_tensor(rt[:, 0, t], top[:, t, 1], top[:, t, 0], ALU.subtract).then_inc(sem("dl"), 1)
                dve.wait_ge(sem("tix"), (c + 1) * BPC)
                dve.tensor_copy(tif[:, t, :], tix[:, t, :]).then_inc(sem("tif"), 1)

            def weigh(c):
                t = slice(c * BPC, (c + 1) * BPC)
                dve.wait_ge(sem("de"), c + 1)
                link(dve.tensor_scalar(rt[:, 2, t], rt[:, 1, t], 1.0, None, ALU.add))
                link(dve.reciprocal(rt[:, 3, t], rt[:, 2, t]))
                link(dve.tensor_tensor(rt[:, 4, t], rt[:, 1, t], rt[:, 3, t], ALU.mult))
                for k in range(2):
                    dve.tensor_scalar(cf2[:, k, t], rt[:, 3 + k, t], swc[:, 3:4], None, ALU.mult)\
                        .then_inc(sem("cf2"), 1)

            def slot_masks(c):
                for k in range(2):
                    dve.wait_ge(sem("idx"), 2 * c + k + 1)
                    dve.tensor_scalar(m72[:, k, ck(c)], idxb[0:96, c, k, :], W("bias_expert"), None,
                                      ALU.is_equal).then_inc(sem("m72"), 1)

            def slot_weights(c, ba, bb):
                for k in range(2):
                    dve.wait_ge(sem("c_ps"), 2 * c + k + 1)
                    dve.tensor_copy(cb[:, c, k, :], bank[(ba, bb)[k]][:, :]).then_inc(sem("cb"), 1)

            def hidden_masked(s, k, tiles):
                c = s % NCH
                n0 = 8 * s + HT * k

                def kept(j):
                    if k == 0:
                        dve.wait_ge(sem("hid"), HT * s + j + 1)
                    if n0 + j >= 2:
                        dve.wait_ge(sem("hlo"), n0 + j - 1)
                    dve.scalar_tensor_tensor(hm[j % 2], idxb[:, c, k, :], W("tile_expert", j, j + 1),
                                             hid[:, j, :], ALU.is_equal, ALU.mult).then_inc(sem("hm"), 1)

                def upper(j):
                    dve.wait_ge(sem("hm"), n0 + j + 1)
                    dve.tensor_copy(hm_hi[:, k, j, :], hm[j % 2]).then_inc(sem("hhi"), 1)

                def lower(j):
                    dve.wait_ge(sem("hhi"), n0 + j + 1)
                    dve.tensor_tensor(hm_lo[:, k, j, :], hm[j % 2], hm_hi[:, k, j, :].bitcast(F),
                                      ALU.subtract).then_inc(sem("hlo"), 1)

                if tiles[0] == 0:
                    dve.wait_ge(sem("idx"), 2 * (c + 1))
                if tiles[0] == 0 and s >= 1:
                    if k == 0:
                        dve.wait_ge(sem("b_ps"), 3 * (s - 1) + 2)
                    else:
                        dve.wait_ge(sem("g_ps"), 3 * s)
                for stage in (kept, upper, lower):
                    for j in tiles:
                        stage(j)

            ln_stats("ffn", 0)
            ln_scale("ffn", 0)
            def consts():
                dve.wait_ge(sem("in_B"), 16)
                dve.tensor_scalar(bqs[:, :], W("bq"), SCALE, None, ALU.mult).then_inc(sem("bqs"), 1)
                dve.tensor_scalar(iwh[:, :], W("iw"), 0.5, None, ALU.mult).then_inc(sem("consts"), 1)
                dve.tensor_scalar(bh2h[:, :], W("bh2"), 0.5, None, ALU.mult).then_inc(sem("consts"), 1)
                dve.tensor_scalar(bs2h[:, :], W("bs2c"), 0.5, None, ALU.mult).then_inc(sem("consts"), 1)

            def shared_share():
                dve.wait_ge(sem("swe"), 1)
                link(dve.tensor_scalar(swc[:, 1:2], swc[:, 0:1], 1.0, None, ALU.add))
                link(dve.reciprocal(swc[:, 2:3], swc[:, 1:2]))
                link(dve.tensor_scalar(swc[:, 3:4], swc[:, 2:3], -1.0, 1.0, ALU.mult, ALU.add))

            def bias_parts():
                dve.wait_ge(sem("w1_ps"), 1)
                for i, n in enumerate(("eb2", "bs2")):
                    link(dve.tensor_copy(bhi[:, 0, i, :], W(n)))
                    link(dve.tensor_tensor(brem[:, 0, i, :], W(n), bhi[:, 0, i, :], ALU.subtract))
                    link(dve.tensor_copy(bhi[:, 1, i, :], brem[:, 0, i, :]))
                    link(dve.tensor_tensor(brem[:, 1, i, :], brem[:, 0, i, :], bhi[:, 1, i, :], ALU.subtract))
                    link(dve.tensor_copy(bhi[:, 2, i, :], brem[:, 1, i, :]))
                    for q in range(3):
                        p = slice(32 * q, 32 * q + 32)
                        dve.tensor_copy(bparts[p, i, :], bhi[p, q, i, :]).then_inc(sem("bparts"), 1)

            consts()
            bias_parts()
            ln_stats("ffn", 1)
            ln_scale("ffn", 1)
            for t in range(SLOTS):
                f, a, q, x = (0 <= t - i < NCH for i in range(4))
                if t + 2 < NCH:
                    ln_stats("ffn", t + 2)
                if q:
                    att_add(t - 2)
                if t + 2 < NCH:
                    ln_scale("ffn", t + 2)
                if t == 1:
                    dve.wait_ge(sem("ew2_hi"), 1)
                    dve.tensor_tensor(ew2_lo[:, :], ew2, ew2_hi[:, :].bitcast(F), ALU.subtract)\
                        .then_inc(sem("ew2_lo"), 1)
                if x and not f:
                    slot_masks(t - 3)
                if q:
                    ln_stats("rt", t - 2)
                if a:
                    att_max(t - 1)
                if q:
                    ln_scale("rt", t - 2)
                if a:
                    att_norm(t - 1)
                if x and f:
                    slot_masks(t - 3)
                if x:
                    weigh(t - 3)
                if f:
                    ffn_add(t)
                if t == 2:
                    shared_share()
                if a:
                    att_pt(t - 1)
                if x:
                    slot_weights(t - 3, 2, 3)
                if f:
                    ln_stats("att", t)
                if t == SLOTS - 1:
                    hidden_masked(0, 0, (0, 1))
                    hidden_masked(0, 0, (2, 3))
                if q:
                    route(t - 2)
                if f:
                    ln_scale("att", t)
            hidden_masked(0, 1, (0, 1))
            weigh(NCH - 1)
            hidden_masked(0, 1, (2, 3))
            slot_masks(NCH - 1)
            slot_weights(NCH - 1, 6, 7)
            dve.wait_ge(sem("consts"), 3)

            def refine(s):
                c = s % NCH
                dve.wait_ge(sem("f2_ps"), s + 1)
                if s >= 1:
                    dve.wait_ge(sem("xi"), s)
                dve.tensor_scalar(rr, bank[6][:, :], W("bf2"), iwh[:, 0:1], ALU.add, ALU.mult)\
                    .then_inc(sem("rr"), 1)
                dve.wait_ge(sem("rr"), 2 * s + 1)
                dve.wait_ge(sem("th"), s + 1)
                dve.scalar_tensor_tensor(rr, th, 1.0, rr, ALU.add, ALU.mult)\
                    .then_inc(sem("rr"), 1)
                if s < STEPS - 2:
                    return
                dve.wait_ge(sem("rr"), 2 * s + 2)
                dve.wait_ge(sem("xi"), s)
                dve.tensor_tensor(xi[:, ck(c)], xi[:, ck(c)], rr, ALU.add).then_inc(sem("xi"), 1)
                if s >= NCH:
                    dve.wait_ge(sem("res"), s - NCH)
                    dve.wait_ge(sem("xi"), s + 1)
                    dve.tensor_tensor(res[:, ck(c)], xi[:, ck(c)], xT[:, ck(c)], ALU.add)\
                        .then_inc(sem("res"), 1)

            def alpha_v(q, k):
                dve.wait_ge(sem("ta"), 3 * q + k + 1)
                dve.scalar_tensor_tensor(ta_of(q, k), ta_of(q, k), 1.0, pw[:, k, :],
                                         ALU.add, ALU.mult).then_inc(sem("u"), 1)

            for s in range(STEPS):
                c = s % NCH
                it2 = s >= NCH
                if s >= 1:
                    dve.wait_ge(sem("ew"), 2 * s)
                dve.tensor_scalar(ew[:, 0, :], xi[:, ck(c)], W("mu"), -1.0, ALU.subtract, ALU.mult)\
                    .then_inc(sem("e0"), 1)
                if it2:
                    dve.wait_ge(sem("v1"), c + 1)
                    dve.tensor_scalar(pw[:, 0, :], vT[:, ck(c)], swc[:, 2:3], None, ALU.mult)\
                        .then_inc(sem("pw0"), 1)
                dve.wait_ge(sem("e0"), s + 1)
                dve.tensor_scalar(ew[:, 1, :], ew[:, 0, :], swc[:, 2:3], None, ALU.mult).then_inc(sem("e1"), 1)
                if s + 1 < STEPS:
                    hidden_masked(s + 1, 0, (0, 1))
                    hidden_masked(s + 1, 0, (2, 3))
                if it2:
                    q = s - NCH
                    dve.wait_ge(sem("pw0"), q + 1)
                    dve.wait_ge(sem("pw"), 2 * q + 2)
                    for k in range(2):
                        alpha_v(q, k)
                if s + 1 < STEPS:
                    hidden_masked(s + 1, 1, (0, 1))
                if 1 <= s <= NCH:
                    dve.wait_ge(sem("v1"), s)
                for k0, k1 in ((0, 3),) if s < STEPS - 1 else ((0, 2), (2, 3)):
                    streams = range(k0, k1)
                    dve.wait_ge(sem("ln"), 3 * s + k1)
                    for k in streams:
                        dve.scalar_tensor_tensor(sm[:, k, :], bank[3 + k][:, :], 0.0, ab[:, k, :],
                                                 ALU.max, ALU.subtract).then_inc(sem("sp"), 1)
                    if s == STEPS - 2:
                        hidden_masked(s + 1, 1, (2, 3))
                    dve.wait_ge(sem("e1"), s + 1)
                    dve.wait_ge(sem("ew"), 2 * s + 2)
                    for k in streams:
                        dve.wait_ge(sem("sp"), 3 * s + k + 1)
                        dve.tensor_tensor(sm[:, k, :], sm[:, k, :], ew[:, 1 + k, :], ALU.mult)\
                            .then_inc(sem("w"), 1)
                    for k in streams:
                        dve.wait_ge(sem("w"), 3 * s + k + 1)
                        dve.wait_ge(sem("tg"), 3 * s + k + 1)
                        if it2:
                            if k == 2:
                                alpha_v(q, k)
                            dve.wait_ge(sem("u"), 3 * q + k + 1)
                            dve.scalar_tensor_tensor(ta_of(s, k), ta_of(s, k), 0.5, sm[:, k, :],
                                                     ALU.mult, ALU.add).then_inc(sem("vv"), 1)
                            dve.wait_ge(sem("vv"), 3 * q + k + 1)
                        dve.scalar_tensor_tensor(tg_of(s, k), tg_of(s, k), 1.0, ta_of(s, k) if it2 else sm[:, k, :],
                                                 ALU.add, ALU.mult).then_inc(sem("y"), 1)
                        if k:
                            dve.wait_ge(sem("y"), 3 * s + k + 1)
                            link(dve.tensor_tensor(tg_of(s, 0), tg_of(s, 0), tg_of(s, k), ALU.add))
                if s >= 1:
                    dve.wait_ge(sem("h1_ps"), s)
                dve.scalar_tensor_tensor(xn, tg_of(s, 0), 0.05, xi[:, ck(c)],
                                         ALU.mult, ALU.add).then_inc(sem("xn"), 1)
                if s >= 1:
                    refine(s - 1)
                if s + 2 < STEPS:
                    hidden_masked(s + 1, 1, (2, 3))
            refine(STEPS - 1)

        @block.tensor
        def _(pe):
            def mm(out, lhsT, rhs, start=True, stop=True):
                return pe.matmul(out, lhsT, rhs, start=start, stop=stop)

            pe.wait_ge(sem("ones"), 1)
            pe.wait_ge(sem("in_A"), 16)
            mm(bank[1][0:NF, 0:D], A("cl"), A("wout"))
            mm(bank[1][0:NF, D:2 * D], A("sl"), A("wout")).then_inc(sem("cw_ps"), 1)
            mm(bank[0][:, 256:264], ones[:, :], A("wq8"))
            pe.wait_ge(sem("in_ctx_0"), 16)
            for g in range(VG):
                if g * VB + VB > B // 2:
                    pe.wait_ge(sem("in_ctx_1"), 16)
                if g >= 2:
                    pe.wait_ge(sem("v"), g - 1)
                    pe.wait_ge(sem("k8"), g - 1)
                for j in range(min(VB, B - g * VB)):
                    b = g * VB + j
                    last = mm(vk_bank(g)[:, j, :], ctxT[:, b * S:(b + 1) * S],
                              pA[:, colA["wv"][1]:colA["wv"][1] + VK])
                last.then_inc(sem("v_ps"), 1)
            for c in range(NCH):
                if c >= 2:
                    pe.wait_ge(sem("k"), c - 1)
                mm(bank[6 + c % 2][:, :], A("wk"), ctxT[:, ck(c)]).then_inc(sem("k_ps"), 1)
            pe.wait_ge(sem("in_x"), 16)
            for b in range(B):
                last = mm(bank[0][:, b * DH:(b + 1) * DH], xT[:, b * S:(b + 1) * S], A("wq8"))
            last.then_inc(sem("q8_ps"), 1)

            def compose_w1(i):
                pe.wait_ge(sem(f"in_b1_{i}"), 16)
                for k in range(i * KP, (i + 1) * KP):
                    last = mm(bank[6][:, :], a1[:, k, :], b1_piece(i)[:, k % KP, :],
                              start=k == 0, stop=k == KC - 1)
                last.then_inc(sem("w1_ps" if i == KC // KP - 1 else "w1_piece"), 1)

            pe.wait_ge(sem("a1s"), 1)
            pe.wait_ge(sem("k"), NCH)
            compose_w1(0)
            pe.wait_ge(sem("k8"), VG)
            pe.wait_ge(sem("q8"), 1)
            mm(bank[4][0:NF, 0:256], A("cl"), qk[:, :, :])
            mm(bank[4][0:NF, 256:512], A("sl"), qk[:, :, :]).then_inc(sem("dft_ps"), 1)
            compose_w1(1)
            pe.wait_ge(sem("reB"), 2)
            mm(bank[5][0:NF, 0:128], reB[:, 0, :], A("cf"), stop=False)
            mm(bank[5][0:NF, 0:128], reB[:, 1, :], A("sf"), start=False).then_inc(sem("cor_ps"), 1)
            compose_w1(2)
            compose_w1(3)
            pe.wait_ge(sem("abf"), 2)
            pe.wait_ge(sem("cw"), 1)
            mm(bank[4][:, 0:128], cw[:, 0, :], ab_f[:, 2, :], stop=False)
            mm(bank[4][:, 0:128], cw[:, 1, :], ab_f[:, 3, :], start=False).then_inc(sem("y_ps"), 1)

            def compose_w2(f):
                pe.wait_ge(sem(f"in_a2_{f}"), 16)
                for k in range(KC):
                    last = mm(bank[7][:, f * D:(f + 1) * D], a2_piece(f)[:, k, :], b2[:, k, :],
                              start=k == 0, stop=k == KC - 1)
                if f == FT - 1:
                    last.then_inc(sem("w2_ps"), 1)

            def ln_tok(which, c, ready):
                n = LN[which, c]
                pe.wait_ge(sem(ready), c + 1)
                if n >= 2:
                    pe.wait_ge(sem("ztok"), BPC * (n - 1))
                for j in range(BPC):
                    t = c * BPC + j
                    last = pe.transpose(bank[n % 2][:, j * 128:(j + 1) * 128], xT[:, t * 128:(t + 1) * 128],
                                        ident)
                last.then_inc(sem("tok_ps"), 1)

            def ln_zt(which, c):
                n = LN[which, c]
                pe.wait_ge(sem("ztok"), BPC * (n + 1))
                if n == 0:
                    pe.wait_ge(sem("w1"), 1)
                else:
                    pe.wait_ge(sem("z"), n)
                for j in range(BPC):
                    last = pe.transpose(bank[6][:, j * 128:(j + 1) * 128], ztok[:, n % 2, j, :], ident)
                last.then_inc(sem("zt_ps"), 1)

            def ffn_up(c, tiles):
                pe.wait_ge(sem("z"), LN["ffn", c] + 1)
                for f in tiles:
                    n = FT * c + f
                    if n >= 2:
                        pe.wait_ge(sem("fh"), n - 1)
                    mm(bank[2 + f % 2][:, :], w1[:, f * 128:(f + 1) * 128], zT[:, c % 2, :])\
                        .then_inc(sem("fh_ps"), 1)

            def ffn_down(c, tiles):
                if c >= 1:
                    pe.wait_ge(sem("x2"), c)
                if c >= 3:
                    pe.wait_ge(sem("lg"), c - 2)
                for f in tiles:
                    pe.wait_ge(sem("fh"), FT * c + f + 1)
                    last = mm(bank[4][:, :], w2[:, f, :], hB[:, c % 2, f, :],
                              start=f == 0, stop=f == FT - 1)
                if f == FT - 1:
                    last.then_inc(sem("fo_ps"), 1)

            def q_proj(c):
                pe.wait_ge(sem("z"), LN["att", c] + 1)
                if c >= 1:
                    pe.wait_ge(sem("x3"), c)
                mm(bank[5][:, :], W("wq"), z3[:, :]).then_inc(sem("q_ps"), 1)

            def scores(c):
                pe.wait_ge(sem("q"), c + 1)
                if c >= 1:
                    pe.wait_ge(sem("o"), c)
                for j in range(BPC):
                    b = c * BPC + j
                    last = mm(bank[7][:, j * S:(j + 1) * S], qT[:, c % 2, j * S:(j + 1) * S],
                              kT[:, b * S:(b + 1) * S])
                last.then_inc(sem("s_ps"), 1)

            def probs_t(c):
                pe.wait_ge(sem("pn"), c + 1)
                for j in range(BPC):
                    last = pe.transpose(bank[5][:, j * S:(j + 1) * S], pn[:, c % 2, j, :], ident)
                last.then_inc(sem("pt_ps"), 1)

            def att_v(c):
                pe.wait_ge(sem("pT"), c + 1)
                for j in range(BPC):
                    b = c * BPC + j
                    last = mm(bank[7][:, j * S:(j + 1) * S], vtok[:, b, :], pT[:, c % 2, j, :])
                last.then_inc(sem("o_ps"), 1)

            def att_out(c):
                pe.wait_ge(sem("o"), c + 1)
                mm(bank[5][:, :], W("wo"), oT[:, c % 2, :]).then_inc(sem("x3_ps"), 1)

            def router1(c):
                pe.wait_ge(sem("z"), LN["rt", c] + 1)
                pe.wait_ge(sem("x2"), min(c + 3, NCH))
                if c >= 1:
                    pe.wait_ge(sem("lg"), c)
                mm(bank[4][0:32, :], W("wr1"), xi[:, ck(c)]).then_inc(sem("r1_ps"), 1)

            def router2(c):
                pe.wait_ge(sem("r1"), c + 1)
                for j in range(BPC):
                    last = mm(bank[4][:, j * E:(j + 1) * E], r1[:, c % 2, j * 128:(j + 1) * 128], W("wr2"))
                last.then_inc(sem("lg_ps"), 1)

            def expand(c, ba, bb):
                pe.wait_ge(sem("tif"), c + 1)
                for k in range(2):
                    for j in range(BPC):
                        t = c * BPC + j
                        last = pe.transpose(bank[(ba, bb)[k]][:, j * 128:(j + 1) * 128],
                                            tif[:, t, k:k + 1].to_broadcast([128, 128]), ident)
                    last.then_inc(sem("idx_ps"), 1)

            def expand_weights(c, ba, bb):
                pe.wait_ge(sem("cf2"), 2 * (c + 1))
                for k in range(2):
                    pe.wait_ge(sem("idx"), 2 * c + k + 1)
                    for j in range(BPC):
                        t = c * BPC + j
                        last = pe.transpose(bank[(ba, bb)[k]][:, j * 128:(j + 1) * 128],
                                            cf2[:, k, t:t + 1].to_broadcast([128, 128]), ident)
                    last.then_inc(sem("c_ps"), 1)

            def hidden(s):
                c, it2 = s % NCH, s >= NCH
                if it2:
                    pe.wait_ge(sem("xi"), s - NCH + 1)
                    pe.wait_ge(sem("v1"), s - NCH + 1)
                for j in range(HT + 1):
                    out = hid_bank(s, j)[:, :] if j < HT else hid_bank(s, 0)[0:H, :]
                    name, wd, M = ("ew1", E * H, 128) if j < HT else ("ws1", H, H)
                    o = j * 128 if j < HT else 0
                    if j >= 2:
                        pe.wait_ge(sem("hid"), HT * s + j - 1)
                    elif s == 1:
                        pe.wait_ge(sem("cb"), 2 * NCH)
                    elif s >= 2:
                        if j == 0:
                            pe.wait_ge(sem("fhg"), 2 * (s - 1))
                        else:
                            pe.wait_ge(sem("h1"), s - 1)
                    last = mm(out, W(name, o, o + M), xi[:, ck(c)], stop=not it2)
                    if it2:
                        last = mm(out, W(name, wd + o, wd + o + M), vT[:, ck(c)], start=False)
                    last.then_inc(sem("hid_ps"), 1)

            pe.wait_ge(sem("cw"), 1)
            pe.wait_ge(sem("v"), VG)
            pe.wait_ge(sem("b2s"), 1)
            compose_w2(0)
            ln_tok("ffn", 0, "x1")
            compose_w2(1)
            ln_zt("ffn", 0)
            ln_tok("ffn", 1, "x1")
            compose_w2(2)
            ffn_up(0, (0, 1))
            compose_w2(3)
            ffn_up(0, (2, 3))
            ln_zt("ffn", 1)
            pe.wait_ge(sem("w2"), 1)
            for t in range(SLOTS):
                f, a, q, x = (0 <= t - i < NCH for i in range(4))
                if t == 1:
                    pe.wait_ge(sem("in_B"), 16)
                if t == 2:
                    pe.wait_ge(sem("r1one"), 1)
                if t + 2 < NCH:
                    ln_tok("ffn", t + 2, "x1")
                if f and t:
                    ffn_up(t, (0, 1))
                if q:
                    att_v(t - 2)
                if x and not f:
                    pe.wait_ge(sem("cb"), 2 * (t - 3))
                    expand(t - 3, 2, 3)
                if a:
                    ln_zt("att", t - 1)
                if q:
                    att_out(t - 2)
                if f and t:
                    ffn_up(t, (2,))
                if a:
                    q_proj(t - 1)
                if q:
                    ln_tok("rt", t - 2, "x3")
                if f and t:
                    ffn_up(t, (3,))
                if t and t + 2 < NCH:
                    ln_zt("ffn", t + 2)
                if a:
                    scores(t - 1)
                if x and f:
                    pe.wait_ge(sem("fh"), FT * NCH)
                    expand(t - 3, 2, 3)
                if f:
                    ffn_down(t, (0, 1))
                if t == SLOTS - 1:
                    hidden(0)
                    expand_weights(t - 3, 2, 3)
                if q:
                    ln_zt("rt", t - 2)
                if f:
                    ffn_down(t, (2, 3))
                if t == 0:
                    ln_zt("ffn", 2)
                if a:
                    probs_t(t - 1)
                if q:
                    router1(t - 2)
                if x and t < SLOTS - 1:
                    expand_weights(t - 3, 2, 3)
                if f:
                    ln_tok("att", t, "x2")
                if q:
                    router2(t - 2)
            pe.wait_ge(sem("z"), 3 * NCH)
            pe.wait_ge(sem("x3"), NCH)
            pe.wait_ge(sem("x2"), NCH)
            pe.wait_ge(sem("bparts"), 6)
            pe.wait_ge(sem("ew2_lo"), 1)
            def out_bank(s, k, part):
                return bank[{0: (2 * k) % 3, 1: 3 + k, 2: (2 * k + 1) % 3}[part]]

            def bias_out(s, k, part):
                c = s % NCH
                mm(out_bank(s, k, part)[:, :], bparts[:, 0 if k else 1, part * D:(part + 1) * D],
                   m72[:, k - 1, ck(c)] if k else onesb[:, :], stop=False)

            def shared_out(s, part):
                return mm(out_bank(s, 0, part)[:, :], W("ws2", part * D, (part + 1) * D), hs,
                          start=part != 1)

            def routed_out(s, k, part, j):
                w = slice(j * 3 * D + part * D, j * 3 * D + (part + 1) * D)
                out = out_bank(s, k, part)[:, :]
                mm(out, ew2_hi[:, w], hm_hi[:, k - 1, j, :], start=False, stop=False)
                mm(out, ew2_lo[:, w], hm_hi[:, k - 1, j, :], start=False, stop=False)
                return mm(out, ew2_hi[:, w], hm_lo[:, k - 1, j, :], start=False, stop=j == HT - 1)

            def refine_a(s):
                pe.wait_ge(sem("xn"), s + 1)
                for j in range(2):
                    if s == 0:
                        pe.wait_ge(sem("hs" if j else "hid"), 2 if j else 2 * HT)
                    elif j == 0:
                        pe.wait_ge(sem("th"), s)
                    else:
                        pe.wait_ge(sem("rr"), 2 * s - 1)
                    mm(bank[6 + (j + 1) % 2][:, :], W("wf1", j * 128, (j + 1) * 128), xn)\
                        .then_inc(sem("f1_ps"), 1)
                pe.wait_ge(sem("fhg"), 2 * s + 1)
                mm(bank[7][0:32, :], W("wh1"), xn).then_inc(sem("h1_ps"), 1)

            def refine_b(s):
                pe.wait_ge(sem("fhg"), 2 * s + 2)
                if s + 2 < STEPS:
                    pe.wait_ge(sem("hs"), s + 3)
                for j in range(2):
                    last = mm(bank[6][:, :], W("wf2", j * 128, (j + 1) * 128), fh[:, j, :],
                              start=j == 0, stop=j == 1)
                last.then_inc(sem("f2_ps"), 1)
                pe.wait_ge(sem("h1"), s + 1)
                mm(bank[7][:, :], W("wh2").to_broadcast([32, 128]), h1).then_inc(sem("h2_ps"), 1)

            for s in range(STEPS):
                c, it2 = s % NCH, s >= NCH
                if s == 0:
                    pe.wait_ge(sem("cb"), 2 * (NCH - 1))
                parts = (0, 2, 1) if it2 else (2, 1)
                done = {0: "a_ps", 1: "b_ps", 2: "g_ps"}
                pe.wait_ge(sem("hs"), s + 1)
                if it2:
                    pe.wait_ge(sem("tg"), 3 * s)
                elif s >= 1:
                    pe.wait_ge(sem("tg"), 3 * s - 2)
                for part in parts:
                    if part == 1:
                        if s >= 1:
                            pe.wait_ge(sem("sp"), 3 * (s - 1) + 1)
                        bias_out(s, 0, part)
                    shared_out(s, part).then_inc(sem(done[part]), 1)
                if s >= 1:
                    pe.wait_ge(sem("sp"), 3 * (s - 1) + 2)
                if it2:
                    pe.wait_ge(sem("ta"), 3 * (s - NCH) + 1)
                if s == 0:
                    pe.wait_ge(sem("lg"), NCH)
                for part in parts:
                    bias_out(s, 1, part)
                for j in range(HT):
                    if s == 0 and j == 1:
                        pe.wait_ge(sem("hid"), HT)
                        expand(NCH - 1, 6, 7)
                    if s == 0 and j == 3:
                        expand_weights(NCH - 1, 6, 7)
                    pe.wait_ge(sem("hlo"), 8 * s + j + 1)
                    for part in parts:
                        last = routed_out(s, 1, part, j)
                        if j == HT - 1:
                            last.then_inc(sem(done[part]), 1)
                if 1 <= s < STEPS - 1:
                    refine_a(s - 1)
                if s + 1 < STEPS:
                    hidden(s + 1)
                pe.wait_ge(sem("hlo"), 8 * s + 8)
                for part in (1, 0, 2) if it2 else (1, 2):
                    if part == 1:
                        if s >= 1:
                            pe.wait_ge(sem("sp"), 3 * s)
                    elif it2:
                        pe.wait_ge(sem("tg"), 3 * s + 1)
                        pe.wait_ge(sem("ta"), 3 * (s - NCH) + 2)
                    bias_out(s, 2, part)
                    for j in range(HT):
                        last = routed_out(s, 2, part, j)
                    last.then_inc(sem(done[part]), 1)
                if s == STEPS - 1:
                    refine_a(s - 1)
                if s >= 1:
                    refine_b(s - 1)
            refine_a(STEPS - 1)
            refine_b(STEPS - 1)


def kernel(**inputs):
    import concourse.bacc as bacc
    from concourse.bass_utils import run_bass_kernel_spmd

    f32 = np.float32
    g = {k: np.asarray(v) for k, v in inputs.items()}

    def col(a, rows=128):
        return np.ascontiguousarray(a.reshape(-1, rows).T)

    def rep(a):
        return np.ascontiguousarray(np.broadcast_to(a.reshape(1, -1), (128, a.size)))

    f = np.arange(NF)[:, None]
    n = np.arange(S)[None, :]
    ang = 2 * np.pi * ((f * n) % S) / S
    twice = np.where((f == 0) | (f == S // 2), 1.0, 2.0)
    shape_only = {"cl": np.cos(ang).T, "sl": np.sin(ang).T, "cf": np.cos(ang), "sf": np.sin(ang),
                  "a1": twice / (S * B * DH), "a2": twice / S, "ident": np.eye(128),
                  "tile_expert": 2 * np.arange(HT)[None, :] + (np.arange(128)[:, None] >= H),
                  "bias_expert": np.arange(96)[:, None] % 32}
    shape_only = {k: v.astype(f32) for k, v in shape_only.items()}

    def thrice(a):
        out = np.zeros((96, a.shape[1]), f32)
        for q in range(3):
            out[32 * q:32 * q + a.shape[0]] = a
        return out

    x = lambda k: g["L1_ffn_" + k]
    parts = dict(shape_only)
    parts.update(
        wq8=g["L0_xattn_Wq"], bq8=rep(g["L0_xattn_bq"]), log1=rep(g["L0_ffn_fc1_logits"]),
        log2=rep(g["L0_ffn_fc2_logits"]), wout=g["L0_xattn_Wout"], bout=col(g["L0_xattn_bout"]),
        wq=g["L1_xattn_Wq"], wk=g["L1_xattn_Wk"], wv=g["L1_xattn_Wv"], wo=g["L1_xattn_Wo"],
        bq=col(g["L1_xattn_bq"]), bk=col(g["L1_xattn_bk"]), bv=col(g["L1_xattn_bv"]), bo=col(g["L1_xattn_bo"]),
        wr1=x("w_r1"), br1=col(x("b_r1"), 32), wr2=np.concatenate([x("w_r2"), x("b_r2")[None]], 0),
        wh1=x("w_h1"), bh1=col(x("b_h1"), 32), wh2=x("w_h2"), bh2=rep(x("b_h2")),
        ew1=x("expert_w1").reshape(E, 2, D, H).transpose(2, 1, 0, 3).reshape(D, -1),
        eb1=col(x("expert_b1")),
        eb2=thrice(x("expert_b2")),
        ws1=x("w_s1").reshape(2, D, H).transpose(1, 0, 2).reshape(D, -1), bs1=col(x("b_s1"), H),
        ws2=x("w_s2"), bs2=thrice(x("b_s2")[None]), wf1=x("w_f1"), bf1=col(x("b_f1")),
        wf2=x("w_f2").reshape(2, 128, D).transpose(1, 0, 2).reshape(128, -1), bf2=col(x("b_f2")),
        bs2c=col(x("b_s2")), iw=col(x("integration_weight")), mu=col(x("mu")), sw=rep(x("shared_weight")))

    def pack(layout):
        at, total = columns(layout)
        out = np.zeros((128, total), f32)
        for name, (rows, a, cols) in at.items():
            out[0:rows, a:a + cols] = parts[name]
        return out

    def rows(a):
        return np.ascontiguousarray(a.reshape(KC, 128, -1).transpose(1, 0, 2))

    arrays = {
        "xtok": np.ascontiguousarray(g["x"].transpose(1, 0, 2)),
        "xT": np.ascontiguousarray(g["x"].transpose(2, 0, 1).reshape(D, T)),
        "ctxT": np.ascontiguousarray(g["ctx_1024"].transpose(2, 0, 1).reshape(D, T)),
        "packA": pack(PACK_A), "packB": pack(PACK_B),
        "ew2": np.ascontiguousarray(x("expert_w2").reshape(HT, 128, 3 * D).transpose(1, 0, 2).reshape(128, -1)),
        "fc1a": rows(g["L0_ffn_fc1_A"].transpose(0, 2, 1).reshape(PRIM * RANK, D)),
        "fc1b": rows(g["L0_ffn_fc1_B"].reshape(PRIM * RANK, FF)),
        "fc2a": rows(g["L0_ffn_fc2_A"].transpose(0, 2, 1).reshape(PRIM * RANK, FF)),
        "fc2b": rows(g["L0_ffn_fc2_B"].reshape(PRIM * RANK, D)),
    }
    arrays = {"in_" + k: v for k, v in arrays.items()}
    nc = bacc.Bacc("TRN2", target_bir_lowering=False, num_devices=1)
    args = [nc.dram_tensor(k, a.shape, mybir.dt.from_np(a.dtype), kind="ExternalInput").ap()
            for k, a in arrays.items()]
    out = nc.dram_tensor("outT", (D, T), mybir.dt.float32, kind="ExternalOutput").ap()
    build(nc, *args, out)
    r = run_bass_kernel_spmd(nc, [arrays], core_ids=[0])
    got = np.asarray(r.results[0]["outT"])
    return np.ascontiguousarray(got.reshape(D, B, S).transpose(1, 2, 0))
```
